# Optimizing a Trainium2 kernel written in Bass

```python
import numpy as np
import jax
import jax.numpy as jnp

def _softmax(x, axis=-1):
    return jax.nn.softmax(x, axis=axis)

def _gelu(x):
    return jax.nn.gelu(x, approximate=True)

def _silu(x):
    return jax.nn.silu(x)

def _sigmoid(x):
    return jax.nn.sigmoid(x)

def _layernorm(x, axis=-1, eps=1e-05):
    m = jnp.mean(x, axis=axis, keepdims=True)
    v = jnp.var(x, axis=axis, keepdims=True)
    return (x - m) / jnp.sqrt(v + eps)

def _scatter_add(tgt, idx, src, axis=0):
    return tgt.at[idx].add(src)

def _segment_sum(src, seg, n):
    return jax.ops.segment_sum(src, seg, n)
kernel_name = 'mk_flamingo_gated_d2_seqx_r8_35eef1'

def setup_inputs(seed: int=0):
    np.random.seed(seed)
    _w = jnp.asarray

    def _rec_inputs():
        import jax
        import jax.numpy as jnp
        _rk = jax.random.key(seed)
        x = 7.22e-05 + 1 * jax.random.normal(jax.random.fold_in(_rk, 1), (128, 64, 128), jnp.float32)
        _lenS = 64 - jax.random.randint(jax.random.fold_in(_rk, 7), (128,), 0, max(1, 64 // 4) + 1, jnp.int32)
        _lenS2 = 64 - jax.random.randint(jax.random.fold_in(_rk, 8), (128,), 0, max(1, 64 // 4) + 1, jnp.int32)
        _ctx_1024P = jax.random.normal(jax.random.fold_in(_rk, 11), (128, 16, 128), jnp.float32)
        _ctx_1024c = jax.random.dirichlet(jax.random.fold_in(_rk, 511), 0.3 * jnp.ones((16,), jnp.float32), (128, 64))
        _ctx_1024t = jnp.einsum('bsk,bkd->bsd', _ctx_1024c, _ctx_1024P)
        _ctx_1024t = _ctx_1024t * jax.lax.rsqrt(jnp.mean(jnp.square(_ctx_1024t)) + 1e-12) * 0.953939
        ctx_1024 = 4.13588e-05 + 0.999923 * (_ctx_1024t + 0.3 * jax.random.normal(jax.random.fold_in(_rk, 611), (128, 64, 128), jnp.float32))
        _g = jax.random.normal(jax.random.fold_in(_rk, 9001), (2, 2), jnp.float32)
        _g = jnp.sign(_g) * jnp.maximum(jnp.abs(_g), 1.0) + (_g == 0) * 1.0
        g_xattn = _g[0]
        g_ffn = _g[1]
        return (x, ctx_1024, g_xattn, g_ffn)
    x, ctx_1024, g_xattn, g_ffn = _rec_inputs()

    def _L0_xattn_setup():
        import jax, jax.numpy as jnp
        import numpy as np
        DIM = 128
        NHEADS = 16
        HEAD_DIM = DIM // NHEADS

        def _split_heads(x):
            B, S, _ = x.shape
            return x.reshape(B, S, NHEADS, HEAD_DIM).transpose(0, 2, 1, 3)
        key = jax.random.key(seed)
        ks = jax.random.split(key, 11)
        B, S = (4, 256)
        scale = 1.0 / np.sqrt(DIM)
        inp = {'Q': jax.random.normal(ks[0], (B, S, DIM), jnp.float32), 'K': jax.random.normal(ks[1], (B, S, DIM), jnp.float32), 'V': jax.random.normal(ks[2], (B, S, DIM), jnp.float32), 'Wq': jax.random.normal(ks[3], (DIM, DIM), jnp.float32) * scale, 'bq': jnp.zeros((DIM,), jnp.float32), 'Wk': jax.random.normal(ks[4], (DIM, DIM), jnp.float32) * scale, 'bk': jnp.zeros((DIM,), jnp.float32), 'Wv': jax.random.normal(ks[5], (DIM, DIM), jnp.float32) * scale, 'bv': jnp.zeros((DIM,), jnp.float32), 'Wo': jax.random.normal(ks[6], (DIM, DIM), jnp.float32) * scale, 'bo': jnp.zeros((DIM,), jnp.float32)}
        return inp
    _L0_xattn_all = _L0_xattn_setup()
    _L0_xattn_in = {k: v for k, v in _L0_xattn_all.items() if k in ('Wq', 'bq', 'Wk', 'bk', 'Wv', 'bv', 'Wo', 'bo')}
    del _L0_xattn_all

    def _L0_ffn_setup():
        import math
        import jax, jax.numpy as jnp
        import numpy as np
        E = 8
        TOPK = 2
        CF = 1.25
        EPS = 1e-05
        NEG = -1e+30

        def _layer_norm(x, gamma, beta):
            mu = jnp.mean(x, axis=-1, keepdims=True)
            var = jnp.mean((x - mu) ** 2, axis=-1, keepdims=True)
            return (x - mu) * jax.lax.rsqrt(var + EPS) * gamma + beta
        key = jax.random.key(seed)
        ks = jax.random.split(key, 8)
        B, S, H, F = (4, 256, 128, 512)
        hidden_states = jax.random.normal(ks[0], (B, S, H), jnp.float32)
        token_mask = jnp.ones((B, S), jnp.int32)
        Wr = jax.random.normal(ks[1], (H, E), jnp.float32) * 0.001
        br = jnp.zeros((E,), jnp.float32)
        W1 = jax.random.normal(ks[2], (E, H, F), jnp.float32) * (1.0 / np.sqrt(H))
        b1 = jax.random.normal(ks[3], (E, F), jnp.float32) * 0.01
        W2 = jax.random.normal(ks[4], (E, F, H), jnp.float32) * (1.0 / np.sqrt(F))
        b2 = jax.random.normal(ks[5], (E, H), jnp.float32) * 0.01
        gamma = jnp.ones((H,), jnp.float32)
        beta = jnp.zeros((H,), jnp.float32)
        return {'hidden_states': hidden_states, 'Wr': Wr, 'br': br, 'W1': W1, 'b1': b1, 'W2': W2, 'b2': b2, 'gamma': gamma, 'beta': beta, 'token_mask': token_mask}
    _L0_ffn_all = _L0_ffn_setup()
    _L0_ffn_in = {k: v for k, v in _L0_ffn_all.items() if k in ('Wr', 'br', 'W1', 'b1', 'W2', 'b2', 'gamma', 'beta', 'token_mask')}
    del _L0_ffn_all

    def _L1_xattn_setup():
        import jax, jax.numpy as jnp
        import numpy as np
        D_MODEL = 128
        N_HEADS = 16
        SPARSITY_FACTOR = 4
        HEAD_DIM = D_MODEL // N_HEADS
        SCALE = HEAD_DIM ** (-0.5)

        def _band_mask(seq_len: int, stride: int) -> jnp.ndarray:
            i = jnp.arange(seq_len)[:, None]
            j = jnp.arange(seq_len)[None, :]
            return jnp.abs(i - j) <= stride
        key = jax.random.key(seed)
        kq, kk, kv = jax.random.split(key, 3)
        B, S = (32, 128)
        q = jax.random.normal(kq, (B, S, D_MODEL), dtype=jnp.float32)
        k = jax.random.normal(kk, (B, S, D_MODEL), dtype=jnp.float32)
        v = jax.random.normal(kv, (B, S, D_MODEL), dtype=jnp.float32)
        return {'q': q, 'k': k, 'v': v}
    _L1_xattn_all = _L1_xattn_setup()
    _L1_xattn_in = {k: v for k, v in _L1_xattn_all.items() if k in ()}
    del _L1_xattn_all

    def _L1_ffn_setup():
        import jax, jax.numpy as jnp
        import numpy as np
        import math
        HID, HD, E, MIN_E = (128, 128, 16, 2)
        B, T = (4, 256)
        IS_CAUSAL = True

        def _l2norm(x, axis):
            return x / jnp.sqrt(jnp.sum(x * x, axis=axis, keepdims=True) + 1e-12)

        def _gating(hidden_states, sim_matrix, gates):
            b, t, c = hidden_states.shape
            flat = hidden_states.reshape(b * t, c)
            logits = _l2norm(flat, -1) @ _l2norm(sim_matrix, 0) - jax.nn.sigmoid(gates)
            gated = jax.nn.relu(logits)
            mask = (gated > 0).astype(gated.dtype)
            inactive = jnp.sum(mask, axis=1) == 0
            _, top_idx = jax.lax.top_k(logits, MIN_E)
            fb = jnp.sum(jax.nn.one_hot(top_idx, E, dtype=mask.dtype), axis=1)
            mask = mask + inactive[:, None].astype(mask.dtype) * fb
            masked = jnp.where(mask > 0, gated, -jnp.inf)
            probs = jax.nn.softmax(masked, axis=-1)
            return probs
        key = jax.random.key(seed)
        ks = jax.random.split(key, 6)
        a_qkv = math.sqrt(6.0 / (HID + HD))
        a_o = math.sqrt(6.0 / (HD + HID))
        return {'hidden_states': jax.random.normal(ks[0], (B, T, HID), jnp.float32), 'sim_matrix': jax.random.normal(ks[1], (HID, E), jnp.float32), 'gates': jnp.zeros((E,), jnp.float32), 'q_proj': jax.random.uniform(ks[2], (E, HID, HD), jnp.float32, -a_qkv, a_qkv), 'k_proj': jax.random.uniform(ks[3], (E, HID, HD), jnp.float32, -a_qkv, a_qkv), 'v_proj': jax.random.uniform(ks[4], (E, HID, HD), jnp.float32, -a_qkv, a_qkv), 'o_proj': jax.random.uniform(ks[5], (E, HD, HID), jnp.float32, -a_o, a_o)}
    _L1_ffn_all = _L1_ffn_setup()
    _L1_ffn_in = {k: v for k, v in _L1_ffn_all.items() if k in ('sim_matrix', 'gates', 'q_proj', 'k_proj', 'v_proj', 'o_proj')}
    del _L1_ffn_all
    return {'x': x, 'ctx_1024': ctx_1024, 'g_xattn': g_xattn, 'g_ffn': g_ffn, 'L0_xattn_Wq': _L0_xattn_in['Wq'], 'L0_xattn_bq': _L0_xattn_in['bq'], 'L0_xattn_Wk': _L0_xattn_in['Wk'], 'L0_xattn_bk': _L0_xattn_in['bk'], 'L0_xattn_Wv': _L0_xattn_in['Wv'], 'L0_xattn_bv': _L0_xattn_in['bv'], 'L0_xattn_Wo': _L0_xattn_in['Wo'], 'L0_xattn_bo': _L0_xattn_in['bo'], 'L0_ffn_Wr': _L0_ffn_in['Wr'], 'L0_ffn_br': _L0_ffn_in['br'], 'L0_ffn_W1': _L0_ffn_in['W1'], 'L0_ffn_b1': _L0_ffn_in['b1'], 'L0_ffn_W2': _L0_ffn_in['W2'], 'L0_ffn_b2': _L0_ffn_in['b2'], 'L0_ffn_gamma': _L0_ffn_in['gamma'], 'L0_ffn_beta': _L0_ffn_in['beta'], 'L0_ffn_token_mask': _L0_ffn_in['token_mask'], 'L1_ffn_sim_matrix': _L1_ffn_in['sim_matrix'], 'L1_ffn_gates': _L1_ffn_in['gates'], 'L1_ffn_q_proj': _L1_ffn_in['q_proj'], 'L1_ffn_k_proj': _L1_ffn_in['k_proj'], 'L1_ffn_v_proj': _L1_ffn_in['v_proj'], 'L1_ffn_o_proj': _L1_ffn_in['o_proj']}

def reference(x, ctx_1024, g_xattn, g_ffn, L0_xattn_Wq, L0_xattn_bq, L0_xattn_Wk, L0_xattn_bk, L0_xattn_Wv, L0_xattn_bv, L0_xattn_Wo, L0_xattn_bo, L0_ffn_Wr, L0_ffn_br, L0_ffn_W1, L0_ffn_b1, L0_ffn_W2, L0_ffn_b2, L0_ffn_gamma, L0_ffn_beta, L0_ffn_token_mask, L1_ffn_sim_matrix, L1_ffn_gates, L1_ffn_q_proj, L1_ffn_k_proj, L1_ffn_v_proj, L1_ffn_o_proj):
    import jax
    import jax.numpy as jnp

    def _L0_xattn_ref(Q, K, V, Wq, bq, Wk, bk, Wv, bv, Wo, bo):
        import jax, jax.numpy as jnp
        import numpy as np
        DIM = 128
        NHEADS = 16
        HEAD_DIM = DIM // NHEADS

        def _split_heads(x):
            B, S, _ = x.shape
            return x.reshape(B, S, NHEADS, HEAD_DIM).transpose(0, 2, 1, 3)
        q = _split_heads(Q @ Wq + bq)
        k = _split_heads(K @ Wk + bk)
        v = _split_heads(V @ Wv + bv)
        scores = jnp.einsum('bhqd,bhkd->bhqk', q, k) / np.sqrt(HEAD_DIM)
        attn = jax.nn.softmax(scores, axis=-1)
        out = jnp.einsum('bhqk,bhkd->bhqd', attn, v)
        B, H, S, hd = out.shape
        out = out.transpose(0, 2, 1, 3).reshape(B, S, H * hd)
        return out @ Wo + bo

    def _L0_ffn_ref(hidden_states, Wr, br, W1, b1, W2, b2, gamma, beta, token_mask):
        import math
        import jax, jax.numpy as jnp
        import numpy as np
        E = 8
        TOPK = 2
        CF = 1.25
        EPS = 1e-05
        NEG = -1e+30

        def _layer_norm(x, gamma, beta):
            mu = jnp.mean(x, axis=-1, keepdims=True)
            var = jnp.mean((x - mu) ** 2, axis=-1, keepdims=True)
            return (x - mu) * jax.lax.rsqrt(var + EPS) * gamma + beta
        B, S, H = hidden_states.shape
        x = hidden_states.reshape(-1, H)
        N = x.shape[0]
        logits = x @ Wr + br
        top_vals, top_idx = jax.lax.top_k(logits, TOPK)
        w = jax.nn.softmax(top_vals, axis=-1)
        flat_idx = top_idx.reshape(-1)
        flat_tok = jnp.repeat(jnp.arange(N), TOPK)
        w_flat = w.reshape(-1)
        cap = max(int(math.ceil(N / E * CF)), 1)
        key_mat = jnp.where(flat_idx[None, :] == jnp.arange(E)[:, None], w_flat[None, :], NEG)
        kv, ki = jax.lax.top_k(key_mat, cap)
        valid = kv > NEG / 2
        tok = flat_tok[ki]
        gate = jnp.where(valid, w_flat[ki], 0.0)
        xe = x[tok]
        h1 = jnp.einsum('ech,ehf->ecf', xe, W1) + b1[:, None, :]
        h1 = jax.nn.gelu(h1, approximate=False)
        y = jnp.einsum('ecf,efh->ech', h1, W2) + b2[:, None, :]
        out = jnp.zeros_like(x).at[tok.reshape(-1)].add((y * gate[..., None]).reshape(-1, H))
        out = out.reshape(B, S, H) + hidden_states
        return _layer_norm(out, gamma, beta)

    def _L1_xattn_ref(q, k, v):
        import jax, jax.numpy as jnp
        import numpy as np
        D_MODEL = 128
        N_HEADS = 16
        SPARSITY_FACTOR = 4
        HEAD_DIM = D_MODEL // N_HEADS
        SCALE = HEAD_DIM ** (-0.5)

        def _band_mask(seq_len: int, stride: int) -> jnp.ndarray:
            i = jnp.arange(seq_len)[:, None]
            j = jnp.arange(seq_len)[None, :]
            return jnp.abs(i - j) <= stride
        B, S, _ = q.shape
        qh = q.reshape(B, S, N_HEADS, HEAD_DIM).transpose(0, 2, 1, 3)
        kh = k.reshape(B, S, N_HEADS, HEAD_DIM).transpose(0, 2, 1, 3)
        vh = v.reshape(B, S, N_HEADS, HEAD_DIM).transpose(0, 2, 1, 3)
        scores = jnp.einsum('bhqd,bhkd->bhqk', qh, kh) * SCALE
        mask = _band_mask(S, SPARSITY_FACTOR)
        scores = jnp.where(mask, scores, -jnp.inf)
        weights = jax.nn.softmax(scores, axis=-1)
        out = jnp.einsum('bhqk,bhkd->bhqd', weights, vh)
        return out.transpose(0, 2, 1, 3).reshape(B, S, D_MODEL)

    def _L1_ffn_ref(hidden_states, sim_matrix, gates, q_proj, k_proj, v_proj, o_proj):
        import jax, jax.numpy as jnp
        import numpy as np
        import math
        HID, HD, E, MIN_E = (128, 128, 16, 2)
        B, T = (4, 256)
        IS_CAUSAL = True

        def _l2norm(x, axis):
            return x / jnp.sqrt(jnp.sum(x * x, axis=axis, keepdims=True) + 1e-12)

        def _gating(hidden_states, sim_matrix, gates):
            b, t, c = hidden_states.shape
            flat = hidden_states.reshape(b * t, c)
            logits = _l2norm(flat, -1) @ _l2norm(sim_matrix, 0) - jax.nn.sigmoid(gates)
            gated = jax.nn.relu(logits)
            mask = (gated > 0).astype(gated.dtype)
            inactive = jnp.sum(mask, axis=1) == 0
            _, top_idx = jax.lax.top_k(logits, MIN_E)
            fb = jnp.sum(jax.nn.one_hot(top_idx, E, dtype=mask.dtype), axis=1)
            mask = mask + inactive[:, None].astype(mask.dtype) * fb
            masked = jnp.where(mask > 0, gated, -jnp.inf)
            probs = jax.nn.softmax(masked, axis=-1)
            return probs
        b, t, c = hidden_states.shape
        rw = _gating(hidden_states, sim_matrix, gates).reshape(b, t, E)
        q = jnp.einsum('btc,ech,bte->bth', hidden_states, q_proj, rw)
        k = jnp.einsum('btc,ech,bte->bth', hidden_states, k_proj, rw)
        v = jnp.einsum('btc,ech,bte->bth', hidden_states, v_proj, rw)
        scale = 1.0 / math.sqrt(HD)
        scores = jnp.einsum('bqh,bkh->bqk', q, k) * scale
        if IS_CAUSAL:
            causal = jnp.tril(jnp.ones((t, t), dtype=bool))
            scores = jnp.where(causal[None], scores, -jnp.inf)
        attn = jax.nn.softmax(scores, axis=-1)
        ao = jnp.einsum('bqk,bkh->bqh', attn, v)
        out = jnp.einsum('bth,ehc,bte->btc', ao, o_proj, rw)
        return out
    x = x + jnp.tanh(g_xattn[0]) * _L0_xattn_ref(_layernorm(x, axis=-1), ctx_1024, ctx_1024, L0_xattn_Wq, L0_xattn_bq, L0_xattn_Wk, L0_xattn_bk, L0_xattn_Wv, L0_xattn_bv, L0_xattn_Wo, L0_xattn_bo)
    x = x + jnp.tanh(g_ffn[0]) * _L0_ffn_ref(_layernorm(x, axis=-1), L0_ffn_Wr, L0_ffn_br, L0_ffn_W1, L0_ffn_b1, L0_ffn_W2, L0_ffn_b2, L0_ffn_gamma, L0_ffn_beta, L0_ffn_token_mask)
    x = x + jnp.tanh(g_xattn[1]) * _L1_xattn_ref(_layernorm(x, axis=-1), ctx_1024, ctx_1024)
    x = x + jnp.tanh(g_ffn[1]) * _L1_ffn_ref(_layernorm(x, axis=-1), L1_ffn_sim_matrix, L1_ffn_gates, L1_ffn_q_proj, L1_ffn_k_proj, L1_ffn_v_proj, L1_ffn_o_proj)
    return x

_drawn_inputs = setup_inputs


def setup_inputs(seed=0):
    import zlib

    import numpy as np

    out = dict(_drawn_inputs(seed))
    spreads = {'g_ffn': (-1.0, 0.2),
     'L0_xattn_bq': (0.0, 0.1),
     'L0_xattn_bk': (0.0, 0.8),
     'L0_xattn_bv': (0.0, 0.1),
     'L0_xattn_bo': (0.0, 0.1),
     'L0_ffn_br': (0.0, 0.1),
     'L0_ffn_gamma': (1.0, 0.2),
     'L0_ffn_beta': (0.0, 0.1),
     'L1_ffn_gates': (0.0, 0.1)}
    factors = {'L0_ffn_b1': 4.62, 'L0_ffn_b2': 3.679}
    for name, (base, spread) in spreads.items():
        noise = np.random.default_rng([zlib.crc32(name.encode()), seed]).standard_normal(out[name].shape)
        drawn = base * np.exp(spread * noise) if base else spread * noise
        out[name] = jnp.asarray(drawn.astype(out[name].dtype))
    for name, factor in factors.items():
        out[name] = (out[name] * factor).astype(out[name].dtype)
    return out
```

```python
from contextlib import ExitStack

import concourse.bass as bass
from concourse import mybir

ALU = mybir.AluOpType
ACT = mybir.ActivationFunctionType
F32 = mybir.dt.float32
BF16 = mybir.dt.bfloat16
I32 = mybir.dt.int32
U32 = mybir.dt.uint32
AX = mybir.AxisListType

P = 128
B, SEQ, DM = 128, 64, 128
N = B * SEQ
T = N // P
NH = 16
HD = DM // NH
SCALE = float(HD) ** -0.5
G = 4
E0, F0 = 8, 512
FB = F0 // P
CAP = 1280
ROWS = E0 * CAP
XT = CAP // 256
E1 = 16
EPS = 1e-5
BAND = 4
NEG = -1.0e30
LOWEST = -3.0e38
SATURATED = 16.635532
SKIP = 1 << 20
W1COL = HD + 1
C = 1
STOP = None


def build(nc, x, ctx_in, g_xattn, g_ffn, Wq, bq, Wk, bk, Wv, bv, Wo, bo, Wr, br, W1, b1, W2, b2,
          gamma, beta, token_mask, sim_matrix, gates, q_proj, k_proj, v_proj, o_proj, out):
    with ExitStack() as stack:
        def sb(name, shape, dt=F32):
            return stack.enter_context(nc.sbuf_tensor(name, shape, dt))

        def sem(name):
            return stack.enter_context(nc.semaphore(name))

        x_d = x.rearrange("b s d -> (b s) d").rearrange("(t p) d -> p t d", p=P)
        out_d = out.rearrange("b s d -> (b s) d").rearrange("(t p) d -> p t d", p=P)
        ctx_d = ctx_in.rearrange("b s d -> (b s) d").rearrange("(t p) d -> p t d", p=P)
        ctxdup_d = ctx_in.rearrange("(t b) s d -> s t b d", b=2)
        routed = nc.dram_tensor("routed_rows", [ROWS, DM], F32, kind="Internal").ap()
        expert_out = nc.dram_tensor("expert_rows", [ROWS, DM], F32, kind="Internal").ap()

        ident = sb("ident", [P, P])
        ones = sb("ones", [P, P])
        ones_bf = sb("ones_bf", [P, P], BF16)
        ident_bf = sb("ident_bf", [P, P], BF16)
        before = sb("before", [P, P], BF16)
        arena = sb("arena", [P, 3 * E1 * DM])
        zero1 = arena[:, 2 * E1 * DM:3 * E1 * DM]

        def part(n, *dims):
            names = "abcd"[:len(dims)]
            size = 1
            for d in dims:
                size *= d
            return arena[:, n * size:(n + 1) * size].rearrange(
                f"p ({' '.join(names)}) -> p {' '.join(names)}", **dict(zip(names, dims)))

        headmask4 = sb("headmask4", [P, 4])
        headmask = sb("headmask", [P, 2, 4, SEQ])
        band = sb("band", [P, SEQ], BF16)
        band4 = sb("band4", [P, 4, SEQ], BF16)
        causal = sb("causal", [P, P])
        powr = sb("powr", [P, T])
        iota8 = sb("iota8", [P, E0])
        iota16 = sb("iota16", [P, E1])
        caps = sb("caps", [P, E0])
        wq_sb = sb("wq_sb", [P, DM])
        wk_sb = sb("wk_sb", [P, DM])
        wv_sb = sb("wv_sb", [P, DM])
        wo_sb = sb("wo_sb", [P, DM])
        wr_sb = sb("wr_sb", [P, E0])
        bq_sb = sb("bq_sb", [P, 1])
        bk_sb = sb("bk_sb", [P, 1])
        bv_sb = sb("bv_sb", [P, 2, DM])
        bo_sb = sb("bo_sb", [P, DM])
        br_sb = sb("br_sb", [P, E0])
        gamma_sb = sb("gamma_sb", [P, DM])
        beta_sb = sb("beta_sb", [P, DM])
        g_sb = sb("g_sb", [P, 4])
        tg = sb("tg", [P, 4])
        tgbo = sb("tgbo", [P, DM])
        xres = sb("xres", [P, T, DM])
        hres = sb("hres", [P, T, DM])
        stats = sb("stats", [P, 6])
        mv = sb("mv", [P, 2])
        veps = sb("veps", [P, 1])
        rstd = sb("rstd", [P, 1])
        stats2 = sb("stats2", [P, 6])
        mv2 = sb("mv2", [P, 2])
        veps2 = sb("veps2", [P, 1])
        rstd2 = sb("rstd2", [P, 1])
        xn = sb("xn", [P, DM])
        ctok = sb("ctok", [P, 2, DM])
        xT = sb("xT", [P, P])
        cT = sb("cT", [P, 2, 2, SEQ])
        qx = sb("qx", [P, 2, 4, SEQ])
        kT = sb("kT", [P, P])
        vx = sb("vx", [P, 2, 2, G, 2, 2, W1COL])
        es = sb("es", [P, 2, G, 2, 2 * SEQ])
        mx = sb("mx", [P, NH])
        pT = sb("pT", [P, 2, G, P])
        rc = sb("rc", [P, NH])
        osb = sb("osb", [P, NH, HD])
        oT = sb("oT", [P, P])
        ytmp = sb("ytmp", [P, DM])
        hn = sb("hn", [P, DM])
        hT = sb("hT", [P, P])
        lg = sb("lg", [P, E0])
        mx8 = sb("mx8", [P, 8])
        ix8 = sb("ix8", [P, 8], U32)
        topv = sb("topv", [P, T, 2])
        topi = sb("topi", [P, T, 2])

        dist = sb("dist", [P, T])
        near = sb("near", [P, T])
        first = part(0, E0, T)
        second = part(1, E0, T)
        key = part(2, E0, T)
        scratch = part(3, E0, T)
        rank = part(4, E0, T)
        keep = part(5, E0, T)
        flags = sb("flags", [P, E0, T], BF16)
        restart = part(6, E0, T)
        counts = sb("counts", [P, E0], BF16)
        thr = sb("thr", [P, E0], I32)
        cand = sb("cand", [P, E0], I32)
        bit = sb("bit", [P, E0], I32)
        accept = sb("accept", [P, E0], I32)
        left = sb("left", [P, E0])
        kept = sb("kept", [P, 2, T])
        gate = sb("gate", [P, T, 2])
        gexp = sb("gexp", [P, 2, T])
        rowf = sb("rowf", [P, 2, T])
        put_row = sb("put_row", [P, T, 2], U32)
        get_row = sb("get_row", [P, T, 2], U32)
        staged = sb("staged", [P, 4, DM])
        staged_row = sb("staged_row", [P, 4, 2], U32)
        w1_sb = part(0, 2, F0)
        w2_sb = part(1, 2, FB, DM)
        b1_sb = sb("b1_sb", [P, 2, FB])
        b2_sb = sb("b2_sb", [P, 2, DM])
        rows_in = sb("rows_in", [P, 2, 2, DM])
        rowsT = sb("rowsT", [P, 2, 2 * P])
        hidT = part(1, 2, FB, 2 * P)
        rows_out = sb("rows_out", [P, 2, 2, DM])
        tggamma = sb("tggamma", [P, DM])
        tgbeta = sb("tgbeta", [P, DM])
        fetch_row = sb("fetch_row", [P, 2, 2], U32)
        fetched = sb("fetched", [P, 2, 2, DM])
        moe = sb("moe", [P, DM])
        moe2 = sb("moe2", [P, DM])
        stats3 = sb("stats3", [P, 6])
        mv3 = sb("mv3", [P, 2])
        veps3 = sb("veps3", [P, 1])
        rstd3 = sb("rstd3", [P, 1])
        vdup = sb("vdup", [P, 2, 2, DM])
        sim_sb = sb("sim_sb", [P, E1])
        simsq = sb("simsq", [P, E1])
        simn = sb("simn", [P, E1])
        sig = sb("sig", [P, E1])
        hsq = sb("hsq", [P, DM])
        ssum = sb("ssum", [P, 1])
        rnorm = sb("rnorm", [P, 1])
        lgr = sb("lgr", [P, E1])
        relu = sb("relu", [P, E1])
        active = sb("active", [P, E1])
        nomax = sb("nomax", [P, 1])
        idle = sb("idle", [P, 1])
        ixf = sb("ixf", [P, 2])
        oneh = sb("oneh", [P, E1])
        oneh2 = sb("oneh2", [P, E1])
        gex = sb("gex", [P, E1])
        gpr = sb("gpr", [P, E1])
        gsum = sb("gsum", [P, 1])
        grec = sb("grec", [P, 1])
        rw = sb("rw", [P, T, E1])
        wqkv = sb("wqkv", [P, E1, 3 * DM])
        wo1 = sb("wo1", [P, E1, DM])
        xs = part(0, E1, DM)
        xsT = part(1, E1, DM)
        qkv = sb("qkv", [P, 3 * DM])
        v2 = sb("v2", [P, 2, DM])
        qkT = sb("qkT", [P, 2 * P])
        sc = sb("sc", [P, P])
        scmax = sb("scmax", [P, 1])
        scsum = sb("scsum", [P, 1])
        screc = sb("screc", [P, 1])
        pr = sb("pr", [P, P])
        prT = sb("prT", [P, P])
        aoT = sb("aoT", [P, P])
        rwt = sb("rwt", [P, E1])
        z = part(2, E1, DM)
        zsum = sb("zsum", [P, DM])
        result = sb("result", [P, 2, DM])

        psS = stack.enter_context(nc.psum_tensor("psS", [P, G, 512], F32))
        psT = stack.enter_context(nc.psum_tensor("psT", [P, 512], F32))
        psP = stack.enter_context(nc.psum_tensor("psP", [P, 512], F32))
        psR = stack.enter_context(nc.psum_tensor("psR", [P, 512], F32))
        psO = stack.enter_context(nc.psum_tensor("psO", [P, 512], F32))
        o_ps = psO[:, 0:NH * W1COL].rearrange("p (h w) -> p h w", w=W1COL)
        oT_ps = psO[:, 144:272]
        y_ps = psO[:, 272:400]
        lg_ps = psO[:, 400:400 + E1]

        loads = sem("loads")
        made = sem("made")
        consts = sem("consts")
        prep = sem("prep")
        tanhs = sem("tanhs")
        ctx_in_s = sem("ctx_in_s")
        x_var = sem("x_var")
        x_rstd = sem("x_rstd")
        x_norm = sem("x_norm")
        ln_step = sem("ln_step")
        xc_ps = sem("xc_ps")
        xc_sb = sem("xc_sb")
        proj = sem("proj")
        qx_w = sem("qx_w")
        kT_w = sem("kT_w")
        vx_w = sem("vx_w")
        scores = sem("scores")
        smax = sem("smax")
        shifted = sem("shifted")
        probs = sem("probs")
        pT_ps = sem("pT_ps")
        pT_sb = sem("pT_sb")
        av = sem("av")
        recip = sem("recip")
        o_norm = sem("o_norm")
        oT_p = sem("oT_p")
        oT_s = sem("oT_s")
        y_p = sem("y_p")
        y_s = sem("y_s")
        x_res = sem("x_res")
        h_var = sem("h_var")
        h_rstd = sem("h_rstd")
        h_norm = sem("h_norm")
        h_kept = sem("h_kept")
        hT_p = sem("hT_p")
        hT_s = sem("hT_s")
        lg_p = sem("lg_p")
        lg_s = sem("lg_s")
        top = sem("top")
        top_kept = sem("top_kept")
        out_s = sem("out_s")
        searched = sem("searched")
        counted = sem("counted")
        simprep = sem("simprep")
        gexp_s = sem("gexp_s")
        routes_d = sem("routes_d")
        routes = sem("routes")
        zeroed = sem("zeroed")
        staged_s = sem("staged_s")
        put = sem("put")
        put_go = sem("put_go")
        w_in = [sem(f"w_in{j}") for j in range(2)]
        rows_in_s = [sem(f"rows_in_s{j}") for j in range(2)]
        rT_ps = sem("rT_ps")
        rT_sb = sem("rT_sb")
        hid_ps = sem("hid_ps")
        hid_sb = sem("hid_sb")
        yrow_ps = sem("yrow_ps")
        yrow_sb = sem("yrow_sb")
        rows_out_s = [sem(f"rows_out_s{j}") for j in range(2)]
        fetch_idx = sem("fetch_idx")
        fetch_go = sem("fetch_go")
        fetched_s = [sem(f"fetched_s{j}") for j in range(2)]
        merged = sem("merged")
        m_var = sem("m_var")
        m_rstd = sem("m_rstd")
        vdup_s = [sem(f"vdup_s{j}") for j in range(2)]
        ctx2_s = sem("ctx2_s")
        cT_p = sem("cT_p")
        xT_p = sem("xT_p")
        n_sum = sem("n_sum")
        n_root = sem("n_root")
        g_in = sem("g_in")
        g_ex = sem("g_ex")
        rw_s = sem("rw_s")
        ewts = sem("ewts")
        xs_s = sem("xs_s")
        xsT_p = sem("xsT_p")
        xsT_s = sem("xsT_s")
        qkv_p = sem("qkv_p")
        qkv_s = sem("qkv_s")
        qkT_p = sem("qkT_p")
        qkT_s = sem("qkT_s")
        sc_p = sem("sc_p")
        sc_m = sem("sc_m")
        pr_e = sem("pr_e")
        pr_s = sem("pr_s")
        prT_p = sem("prT_p")
        prT_s = sem("prT_s")
        ao_p = sem("ao_p")
        ao_s = sem("ao_s")
        z_p = sem("z_p")
        z_s = sem("z_s")
        res_s = sem("res_s")
        res_out = [sem(f"res_out{j}") for j in range(2)]
        LOOPED = [searched, counted, staged_s, put_go, *w_in, *rows_in_s, rT_ps, rT_sb, hid_ps, hid_sb, yrow_ps,
                  yrow_sb, *rows_out_s, fetch_idx, fetch_go, merged, m_var, m_rstd, *vdup_s, ctx2_s, cT_p, xT_p,
                  n_sum, n_root, g_in, g_ex, rw_s, xs_s, xsT_p, xsT_s, qkv_p, qkv_s, qkT_p, qkT_s, sc_p, sc_m, pr_e,
                  pr_s, prT_p, prT_s, ao_p, ao_s, z_p, z_s, res_s, *res_out,
                  ctx_in_s, x_var, x_rstd, x_norm, xc_ps, xc_sb, proj, qx_w, kT_w, vx_w, scores, smax, shifted, probs,
                  pT_ps, pT_sb, av, recip, o_norm, oT_p, oT_s, y_p, y_s, x_res, h_var, h_rstd, h_norm, h_kept, hT_p,
                  hT_s, lg_p, lg_s, top, top_kept]

        def tile(a, k, j):
            return a[:, :, :].rearrange("p (k j) d -> p k j d", j=2)[:, bass.ds(k, 1), j, :].rearrange("p o d -> p (o d)")

        def bcast(v, n):
            return v.rearrange("(o n) -> o n", o=1).broadcast_to([P, n])

        LOADS = [
            (wq_sb[:, :], Wq), (wk_sb[:, :], Wk), (wv_sb[:, :], Wv), (wo_sb[:, :], Wo), (wr_sb[:, :], Wr),
            (bq_sb[:, :], bq.rearrange("(n o) -> n o", o=1)), (bk_sb[:, :], bk.rearrange("(n o) -> n o", o=1)),
            (bv_sb[:, 0, :], bcast(bv, DM)), (bv_sb[:, 1, :], bcast(bv, DM)), (bo_sb[:, :], bcast(bo, DM)),
            (br_sb[:, :], bcast(br, E0)), (gamma_sb[:, :], bcast(gamma, DM)), (beta_sb[:, :], bcast(beta, DM)),
            (sim_sb[:, :], sim_matrix), (sig[:, :], bcast(gates, E1)),
            (g_sb[:, 0:2], bcast(g_xattn, 2)), (g_sb[:, 2:4], bcast(g_ffn, 2)),
        ]
        block = stack.enter_context(nc.Block())

        @block.sync
        def _(sp):
            for s in LOOPED:
                sp.sem_inc(s, C)
            for dst, src in LOADS:
                sp.dma_start(dst, src).then_inc(loads, 16)
            sp.dma_start(xres[:, :, :], x_d).then_inc(loads, 16)
            sp.wait_ge(made, 2)
            for c in range(ROWS // P // 16):
                sp.dma_start(routed.rearrange("(p r) d -> p (r d)", p=P)[:, c * 2048:(c + 1) * 2048], zero1[:, :]).then_inc(zeroed, 16)
            for e3, w in enumerate((q_proj, k_proj, v_proj)):
                sp.dma_start(wqkv[:, :, e3 * DM:(e3 + 1) * DM], w.rearrange("e c h -> c e h")).then_inc(ewts, 16)
            sp.dma_start(wo1[:, :, :], o_proj.rearrange("e h c -> h e c")).then_inc(ewts, 16)
            with sp.Fori(0, T, 1) as i:
                sp.wait_ge(xc_ps, i + C)
                sp.dma_start(ctok[:, 0, :], ctx_d[:, bass.ds(i, 1), :].rearrange("p o d -> p (o d)")).then_inc(ctx_in_s, 16)
            sp.wait_ge(put, 32 * T)
            w1_d = W1.rearrange("(k j) c f -> k j c f", j=2)
            w2_d = W2.rearrange("(k j) (f p) c -> k j p f c", j=2, p=P)
            b1_d = b1.rearrange("(k j) (f p) -> k j p f", j=2, p=P)
            b2_d = b2.rearrange("(k j) (o c) -> k j o c", j=2, o=1)
            in_d = routed.rearrange("(k j m r p) d -> k j m p r d", j=2, m=XT, r=2, p=P)
            out_rows_d = expert_out.rearrange("(k j m r p) d -> k j m p r d", j=2, m=XT, r=2, p=P)

            def store_rows(k, t):
                sp.wait_ge(yrow_sb, k * (2 * XT) + t + 1 + C)
                sp.dma_start(out_rows_d[bass.ds(k, 1), t // XT, t % XT].rearrange("o p r d -> (o p) r d"),
                             rows_out[:, t % 2, :, :]).then_inc(rows_out_s[t % 2], 16)

            with sp.Fori(0, E0 // 2) as k:
                for j in range(2):
                    sp.wait_ge(yrow_ps, k * (2 * XT) + C)
                    one = bass.ds(k, 1)
                    sp.dma_start(w1_sb[:, j, :], w1_d[one, j].rearrange("o c f -> (o c) f")).then_inc(w_in[j], 16)
                    sp.dma_start(w2_sb[:, j, :, :], w2_d[one, j].rearrange("o p f c -> (o p) f c")).then_inc(w_in[j], 16)
                    with nc.allow_non_contiguous_dma(reason="one bias per partition"):
                        sp.dma_start(b1_sb[:, j, :], b1_d[one, j].rearrange("o p f -> (o p) f")).then_inc(w_in[j], 16)
                    sp.dma_start(b2_sb[:, j, :], b2_d[one, j].rearrange("o q c -> (o q) c").broadcast_to([P, DM])).then_inc(w_in[j], 16)
                    for m in range(XT):
                        t = j * XT + m
                        if t >= 2:
                            sp.wait_ge(rT_ps, k * (2 * XT) + t - 1 + C)
                        else:
                            sp.wait_ge(rT_ps, k * (2 * XT) + C)
                        sp.dma_start(rows_in[:, t % 2, :, :], in_d[one, j, m].rearrange("o p r d -> (o p) r d")).then_inc(rows_in_s[t % 2], 16)
                        if t >= 2:
                            store_rows(k, t - 2)
                store_rows(k, 2 * XT - 2)
                store_rows(k, 2 * XT - 1)
            for s in rows_out_s:
                sp.wait_ge(s, 16 * XT * (E0 // 2) + C)
            if STOP != "C":
              with sp.Fori(0, T // 2) as k:
                i0 = k * 2
                for j in range(2):
                    i = i0 + j
                    sp.wait_ge(cT_p, i + C)
                    sp.dma_start(ctok[:, 1, :], tile(ctx_d, k, j)).then_inc(ctx2_s, 16)
                    sp.wait_ge(vx_w, i0 * 2 + 2 * T + C)
                    for h in range(2):
                        sp.dma_start(vdup[h * SEQ:(h + 1) * SEQ, j, :, :],
                                     ctxdup_d.rearrange("s (k j) b d -> s k j b d", j=2)[:, bass.ds(k, 1), j].rearrange("s o b d -> s (o b) d")).then_inc(vdup_s[j], 16)
            if STOP:
                sp.wait_ge(h_norm, (2 * T if STOP == "D" else T) + C)
                sp.wait_ge(rw_s, (T if STOP == "D" else 0) + C)
                sp.dma_start(out_d, xres[:, :, :]).then_inc(out_s, 16)
                sp.wait_ge(out_s, 16)
            else:
                with sp.Fori(0, T // 2) as k:
                    i0 = k * 2
                    for j in range(2):
                        sp.wait_ge(res_s, i0 + j + 1 + C)
                        sp.dma_start(tile(out_d, k, j), result[:, j, :]).then_inc(res_out[j], 16)
                for s in res_out:
                    sp.wait_ge(s, 16 * (T // 2) + C)

        @block.gpsimd
        def _(pool):
            steps = []

            def make(instruction):
                instruction.then_inc(made, 1)
                steps.append(1)
                pool.wait_ge(made, len(steps))
            make(pool.memset(ones[:, :], 1.0))
            make(pool.memset(zero1[:, :], 0.0))
            make(pool.memset(powr[:, :], -0.5))
            make(pool.affine_select(out=ident[:, :], in_=ones[:, :], pattern=[[-1, P]], compare_op=ALU.is_equal,
                                    fill=0.0, base=0, channel_multiplier=1))
            make(pool.affine_select(out=before[:, :], in_=ones[:, :], pattern=[[1, P]], compare_op=ALU.is_gt,
                                    fill=0.0, base=0, channel_multiplier=-1))
            make(pool.affine_select(out=causal[:, :], in_=zero1[:, 0:P], pattern=[[-1, P]], compare_op=ALU.is_ge,
                                    fill=NEG, base=0, channel_multiplier=1))
            make(pool.memset(causal[SEQ:P, 0:SEQ], NEG))
            for h in range(2):
                rows = slice(h * SEQ, (h + 1) * SEQ)
                make(pool.affine_select(out=band[rows, :], in_=zero1[rows, 0:SEQ], pattern=[[-1, SEQ]],
                                        compare_op=ALU.is_ge, fill=NEG, base=BAND, channel_multiplier=1))
                make(pool.affine_select(out=band[rows, :], in_=band[rows, :], pattern=[[1, SEQ]],
                                        compare_op=ALU.is_ge, fill=NEG, base=BAND, channel_multiplier=-1))
            make(pool.iota(iota8[:, :], pattern=[[1, E0]], base=0, channel_multiplier=0,
                           allow_small_or_imprecise_dtypes=True))
            make(pool.iota(iota16[:, :], pattern=[[1, E1]], base=0, channel_multiplier=0,
                           allow_small_or_imprecise_dtypes=True))
            make(pool.iota(caps[:, :], pattern=[[CAP, E0]], base=0, channel_multiplier=0,
                           allow_small_or_imprecise_dtypes=True))
            with pool.Fori(0, T // 2) as k:
                i0 = k * 2
                for j in range(2):
                    pool.wait_ge(x_var, i0 + j + 1 + C)
                    pool.tensor_tensor(rstd[:, :], veps[:, :], powr[:, 0:1], ALU.pow).then_inc(x_rstd, 1)
                for j in range(2):
                    pool.wait_ge(h_var, i0 + j + 1 + C)
                    pool.tensor_tensor(rstd2[:, :], veps2[:, :], powr[:, 0:1], ALU.pow).then_inc(h_rstd, 1)
                    pool.wait_ge(h_norm, i0 + j + 1 + C)
                    pool.tensor_copy(tile(hres, k, j), hn[:, :]).then_inc(h_kept, 1)
                    pool.wait_ge(top, i0 * 2 + 2 * j + 2 + C)
                    pool.tensor_copy(tile(topv, k, j), mx8[:, 0:2]).then_inc(top_kept, 1)
                    pool.tensor_copy(tile(topi, k, j), ix8[:, 0:2]).then_inc(top_kept, 1)

            pool.wait_ge(simprep, 2)
            pool.tensor_tensor(simsq[:, :], simsq[:, :], powr[:, 0:E1], ALU.pow).then_inc(simprep, 1)
            pool.wait_ge(routes, 1)
            pool.wait_ge(zeroed, 16 * (ROWS // P // 16))

            def scatter(k):
                for j in range(2):
                    if not isinstance(k, int):
                        pool.wait_ge(put, k * 64)
                    pool.tensor_copy(staged[:, j, :], tile(hres, k, j)).then_inc(staged_s, 1)
                    pool.tensor_copy(staged_row[:, j, :], tile(put_row, k, j)).then_inc(staged_s, 1)
                for j in range(2):
                    pool.wait_ge(staged_s, k * 4 + 2 * j + 2 + C)
                    pool.sem_inc(put_go, 1)
                    for s in range(2):
                        pool.indirect_dma_start(
                            out=routed, out_offset=bass.IndirectOffsetOnAxis(ap=staged_row[:, j, s:s + 1], axis=0),
                            in_=staged[:, j, :], in_offset=None, bounds_check=ROWS - 1, oob_is_err=False).then_inc(put, 16)

            scatter(0)
            with pool.Fori(1, T // 2) as k:
                scatter(k)
            for s in rows_out_s:
                pool.wait_ge(s, 16 * XT * (E0 // 2) + C)
            with pool.Fori(0, T // 2) as k:
                i0 = k * 2
                for j in range(2):
                    i = i0 + j
                    pool.wait_ge(merged, i0 + C)
                    pool.tensor_copy(fetch_row[:, j, :], tile(get_row, k, j)).then_inc(fetch_idx, 1)
                    pool.wait_ge(fetch_idx, i + 1 + C)
                    pool.sem_inc(fetch_go, 1)
                    for s in range(2):
                        pool.indirect_dma_start(
                            out=fetched[:, j, s, :], out_offset=None, in_=expert_out,
                            in_offset=bass.IndirectOffsetOnAxis(ap=fetch_row[:, j, s:s + 1], axis=0)).then_inc(fetched_s[j], 16)
                for j in range(2):
                    i = i0 + j
                    pool.wait_ge(m_var, i + 1 + C)
                    pool.tensor_tensor(rstd3[:, :], veps3[:, :], powr[:, 0:1], ALU.pow).then_inc(m_rstd, 1)
                    pool.wait_ge(x_var, T + i + 1 + C)
                    pool.tensor_tensor(rstd[:, :], veps[:, :], powr[:, 0:1], ALU.pow).then_inc(x_rstd, 1)
                for j in range(2):
                    i = i0 + j
                    pool.wait_ge(h_var, T + i + 1 + C)
                    pool.tensor_tensor(rstd2[:, :], veps2[:, :], powr[:, 0:1], ALU.pow).then_inc(h_rstd, 1)
                    pool.wait_ge(n_sum, i + 1 + C)
                    pool.tensor_tensor(rnorm[:, :], ssum[:, :], powr[:, 0:1], ALU.pow).then_inc(n_root, 1)
                    pool.tensor_copy(tile(hres, k, j), hn[:, :]).then_inc(h_kept, 1)

        MADE = 14

        @block.vector
        def _(dve):
            dve.wait_ge(made, MADE)
            dve.wait_ge(loads, 16 * (len(LOADS) + 1))
            dve.tensor_reduce(headmask4[:, :], ident[:, :].rearrange("p (g h d) -> p h g d", g=G, h=4),
                              AX.XY, ALU.add).then_inc(prep, 1)
            dve.wait_ge(prep, 1)
            for b in range(2):
                dve.tensor_copy(headmask[:, b, :, :], headmask4[:, :].unsqueeze(2).broadcast_to([P, 4, SEQ])).then_inc(prep, 1)
            dve.tensor_copy(ident_bf[:, :], ident[:, :]).then_inc(prep, 1)
            dve.tensor_copy(ones_bf[:, :], ones[:, :]).then_inc(prep, 1)
            dve.memset(vx[:, :, :, :, :, :, :], 0.0).then_inc(prep, 1)
            dve.wait_ge(prep, 6)
            for h in range(2):
                dve.memset(vx[h * SEQ:(h + 1) * SEQ, :, :, :, :, h, HD].rearrange("p u b g h -> p (u b g h)"), 1.0).then_inc(prep, 1)
            dve.wait_ge(tanhs, 1)
            dve.tensor_scalar(tgbo[:, :], bo_sb[:, :], tg[:, 0:1], None, ALU.mult).then_inc(prep, 1)
            dve.wait_ge(prep, 9)
            dve.tensor_copy(mx[:, 0:1], tg[:, 0:1]).then_inc(consts, 1)

            with dve.Fori(0, T // 2) as k:
                i0 = k * 2
                for j in range(2):
                    i = i0 + j
                    xt = tile(xres, k, j)
                    dve.bn_stats(stats[:, :], xt).then_inc(ln_step, 1)
                    dve.drain()
                    dve.bn_aggr(mv[:, :], stats[:, :]).then_inc(ln_step, 1)
                    dve.drain()
                    dve.tensor_scalar(veps[:, :], mv[:, 1:2], EPS, None, ALU.add).then_inc(x_var, 1)
                    dve.wait_ge(x_rstd, i + 1 + C)
                    dve.wait_ge(xc_ps, i + C)
                    dve.tensor_scalar(xn[:, :], xt, mv[:, 0:1], rstd[:, 0:1], ALU.subtract, ALU.mult).then_inc(x_norm, 1)
                    dve.wait_ge(proj, i + 1 + C)
                    dve.wait_ge(scores, i + C)
                    for b in range(2):
                        q = psP[:, b * SEQ:(b + 1) * SEQ].unsqueeze(1).broadcast_to([P, 4, SEQ])
                        dve.scalar_tensor_tensor(qx[:, b, :, :], q, bq_sb[:, 0:1], headmask[:, b, :, :],
                                                 ALU.add, ALU.mult).then_inc(qx_w, 1)
                    dve.wait_ge(av, i0 + C)
                    for h in range(2):
                        rows = slice(h * SEQ, (h + 1) * SEQ)
                        v = psP[rows, 2 * P:4 * P].rearrange("p (b g j h d) -> p (b g) j h d", b=2, g=G, j=2, h=2)[:, :, h, :, :]
                        bvv = bv_sb[rows, :, :].rearrange("p b (g j h d) -> p (b g) j h d", g=G, j=2, h=2)[:, :, h, :, :]
                        dst = vx[rows, j, :, :, :, h, 0:HD].rearrange("p b g h d -> p (b g) h d")
                        dve.tensor_tensor(dst, v, bvv, ALU.add).then_inc(vx_w, 1)
                for j in range(2):
                    i = i0 + j
                    s4 = psS[:, :, 0:2 * P].rearrange("p g (a k) -> p g a k", k=SEQ)
                    dve.wait_ge(scores, i + 1 + C)
                    dve.tensor_reduce(mx[:, :].rearrange("p (g a) -> p g a", g=G), s4, AX.X, ALU.max).then_inc(smax, 1)
                    dve.wait_ge(smax, i + 1 + C)
                    dve.wait_ge(pT_ps, i0 * 2 + C)
                    dve.tensor_tensor(es[:, j].rearrange("p g b (a k) -> p g (b a) k", k=SEQ), s4,
                                      mx[:, :].rearrange("p (g a) -> p g a", g=G).unsqueeze(3).broadcast_to([P, G, 4, SEQ]),
                                      ALU.subtract).then_inc(shifted, 1)
                for j in range(2):
                    i = i0 + j
                    dve.wait_ge(av, i + 1 + C)
                    dve.reciprocal(rc[:, :], o_ps[:, :, HD]).then_inc(recip, 1)
                    dve.wait_ge(recip, i + 1 + C)
                    dve.wait_ge(oT_p, i + C)
                    dve.tensor_tensor(osb[:, :, :], o_ps[:, :, 0:HD], rc[:, :].unsqueeze(2).broadcast_to([P, NH, HD]),
                                      ALU.mult).then_inc(o_norm, 1)
                    dve.wait_ge(y_p, i + 1 + C)
                    dve.scalar_tensor_tensor(ytmp[:, :], y_ps, tg[:, 0:1], tgbo[:, :], ALU.mult, ALU.add).then_inc(y_s, 1)
                    dve.wait_ge(y_s, i + 1 + C)
                    xt = tile(xres, k, j)
                    dve.tensor_tensor(xt, xt, ytmp[:, :], ALU.add).then_inc(x_res, 1)
                    dve.drain()
                    dve.bn_stats(stats2[:, :], xt).then_inc(ln_step, 1)
                    dve.drain()
                    dve.bn_aggr(mv2[:, :], stats2[:, :]).then_inc(ln_step, 1)
                    dve.drain()
                    dve.tensor_scalar(veps2[:, :], mv2[:, 1:2], EPS, None, ALU.add).then_inc(h_var, 1)
                    dve.wait_ge(h_rstd, i + 1 + C)
                    dve.wait_ge(h_kept, i + C)
                    dve.tensor_scalar(hn[:, :], xt, mv2[:, 0:1], rstd2[:, 0:1], ALU.subtract, ALU.mult).then_inc(h_norm, 1)
                    dve.wait_ge(lg_p, i + 1 + C)
                    dve.wait_ge(top_kept, i0 * 2 + 2 * j + C)
                    dve.tensor_tensor(lg[:, :], psO[:, 400:400 + E0], br_sb[:, :], ALU.add).then_inc(lg_s, 1)
                    dve.drain()
                    dve.max(mx8[:, :], lg[:, :]).then_inc(top, 1)
                    dve.drain()
                    dve.max_index(ix8[:, :], mx8[:, :], lg[:, :]).then_inc(top, 1)

            dve.tensor_tensor(simsq[:, :], sim_sb[:, :], sim_sb[:, :], ALU.mult).then_inc(simprep, 1)
            dve.wait_ge(counted, 1 + C)
            dve.tensor_scalar(simsq[:, :], psT[:, 0:E1], 1e-12, None, ALU.add).then_inc(simprep, 1)
            dve.wait_ge(simprep, 3)
            dve.tensor_tensor(simn[:, :], sim_sb[:, :], simsq[:, :], ALU.mult)
            dve.wait_ge(tanhs, 2)
            dve.tensor_scalar(sig[:, :], sig[:, :], 1.0, None, ALU.add)
            dve.drain()
            dve.reciprocal(sig[:, :], sig[:, :])
            dve.tensor_scalar(tggamma[:, :], gamma_sb[:, :], tg[:, 2:3], None, ALU.mult)
            dve.tensor_scalar(tgbeta[:, :], beta_sb[:, :], tg[:, 2:3], None, ALU.mult)
            dve.tensor_copy(band4[:, :, :], band[:, :].unsqueeze(1).broadcast_to([P, 4, SEQ]))
            dve.wait_ge(top_kept, 2 * T + C)
            dve.tensor_tensor(dist[:, :], topv[:, :, 0], topv[:, :, 1], ALU.subtract).then_inc(routes_d, 1)
            dve.memset(restart[:, :, :], 1.0)
            dve.memset(bit[:, :], 0)
            for slot, hot in enumerate((first, second)):
                dve.tensor_tensor(hot[:, :, :], topi[:, :, slot].unsqueeze(1).broadcast_to([P, E0, T]),
                                  iota8[:, :].unsqueeze(2).broadcast_to([P, E0, T]), ALU.is_equal)
            dve.drain()
            dve.memset(restart[:, :, 0], 0.0)
            dve.tensor_scalar(near[:, :], dist[:, :], SATURATED, None, ALU.min)
            dve.tensor_tensor(scratch[:, :, :], first[:, :, :], second[:, :, :], ALU.add)
            dve.drain()
            dve.tensor_tensor(key[:, :, :], first[:, :, :], near[:, :].unsqueeze(1).broadcast_to([P, E0, T]), ALU.mult)
            dve.tensor_tensor(rank[:, :, :], second[:, :, :], dist[:, :].unsqueeze(1).broadcast_to([P, E0, T]), ALU.mult)
            dve.tensor_scalar(scratch[:, :, :], scratch[:, :, :], -LOWEST, LOWEST, ALU.mult, ALU.add)
            dve.drain()
            dve.tensor_tensor(key[:, :, :], key[:, :, :], rank[:, :, :], ALU.subtract)
            dve.drain()
            dve.tensor_tensor(key[:, :, :], key[:, :, :], scratch[:, :, :], ALU.add)
            dve.memset(cand[:, :], 0)
            dve.drain()

            def count(op, against):
                dve.tensor_tensor(flags[:, :, :], key[:, :, :],
                                  against[:, :].bitcast(F32).unsqueeze(2).broadcast_to([P, E0, T]), op)
                dve.drain()
                with nc.allow_low_precision(reason="counts up to 64 are exact in bfloat16"):
                    dve.tensor_reduce(counts[:, :], flags[:, :, :], AX.X, ALU.add).then_inc(searched, 1)

            count(ALU.is_ge, cand)
            dve.wait_ge(counted, 2 + C)
            dve.tensor_scalar(accept[:, :], psP[:, 0:E0], float(CAP), -1.0, ALU.is_ge, ALU.mult)
            dve.memset(bit[:, :], 0x40000000)
            dve.drain()
            dve.tensor_scalar(thr[:, :], accept[:, :], -1, None, ALU.bitwise_xor)
            dve.drain()
            with dve.Fori(0, 31) as n:
                dve.tensor_tensor(cand[:, :], thr[:, :], bit[:, :], ALU.bitwise_xor)
                dve.drain()
                count(ALU.is_ge, cand)
                dve.wait_ge(counted, n + 3 + C)
                dve.tensor_scalar(accept[:, :], psP[:, 0:E0], float(CAP), -1.0, ALU.is_ge, ALU.mult)
                dve.drain()
                dve.tensor_tensor(accept[:, :], accept[:, :], bit[:, :], ALU.bitwise_and)
                dve.drain()
                dve.tensor_tensor(thr[:, :], thr[:, :], accept[:, :], ALU.bitwise_xor)
                dve.tensor_scalar(bit[:, :], bit[:, :], 1, None, ALU.logical_shift_right)
                dve.drain()
            count(ALU.is_gt, thr)
            dve.wait_ge(counted, 34 + C)
            dve.tensor_scalar(left[:, :], psP[:, 0:E0], -1.0, float(CAP), ALU.mult, ALU.add)
            dve.tensor_copy(keep[:, :, :], flags[:, :, :])
            dve.drain()
            dve.tensor_tensor(scratch[:, :, :], key[:, :, :], thr[:, :].bitcast(F32).unsqueeze(2).broadcast_to([P, E0, T]), ALU.is_equal)
            dve.tensor_scalar(rank[:, :, :], key[:, :, :], LOWEST, None, ALU.is_gt)
            dve.drain()
            dve.tensor_tensor(scratch[:, :, :], scratch[:, :, :], rank[:, :, :], ALU.mult)
            dve.drain()
            dve.tensor_copy(flags[:, :, :], scratch[:, :, :]).then_inc(searched, 1)

            def ranks(n):
                dve.wait_ge(counted, 35 + n + C)
                flat = rank[:, :, :].rearrange("p e t -> p (e t)")
                dve.tensor_tensor_scan(flat, restart[:, :, :].rearrange("p e t -> p (e t)"), psR[:, :], 0.0, ALU.mult, ALU.add)
                dve.drain()
                dve.tensor_tensor(flat, flat, psR[:, :], ALU.subtract)
                dve.drain()
                dve.tensor_tensor(flat, flat, psT[:, :], ALU.add)
                dve.drain()

            ranks(0)
            dve.tensor_tensor(rank[:, :, :], rank[:, :, :], left[:, :].unsqueeze(2).broadcast_to([P, E0, T]), ALU.is_lt)
            dve.drain()
            dve.tensor_tensor(rank[:, :, :], rank[:, :, :], scratch[:, :, :], ALU.mult)
            dve.drain()
            dve.tensor_tensor(keep[:, :, :], keep[:, :, :], rank[:, :, :], ALU.add)
            dve.drain()
            dve.tensor_copy(flags[:, :, :], keep[:, :, :]).then_inc(searched, 1)
            ranks(1)
            dve.tensor_tensor(rank[:, :, :], rank[:, :, :], caps[:, :].unsqueeze(2).broadcast_to([P, E0, T]), ALU.add)
            dve.wait_ge(gexp_s, 1)
            dve.tensor_scalar(gexp[:, 0, :], gexp[:, 1, :], 1.0, None, ALU.add)
            dve.drain()
            dve.reciprocal(gexp[:, 0, :], gexp[:, 0, :])
            dve.drain()
            dve.tensor_tensor(gexp[:, 1, :], gexp[:, 1, :], gexp[:, 0, :], ALU.mult)
            for slot, hot in enumerate((first, second)):
                dve.tensor_tensor(scratch[:, :, :], hot[:, :, :], keep[:, :, :], ALU.mult)
                dve.drain()
                dve.tensor_reduce(kept[:, slot, :], scratch[:, :, :].rearrange("p e t -> p t e"), AX.X, ALU.add)
                dve.drain()
                dve.tensor_tensor(scratch[:, :, :], scratch[:, :, :], rank[:, :, :], ALU.mult)
                dve.drain()
                dve.tensor_reduce(rowf[:, slot, :], scratch[:, :, :].rearrange("p e t -> p t e"), AX.X, ALU.add)
                dve.drain()
                dve.tensor_tensor(gate[:, :, slot], gexp[:, slot, :], kept[:, slot, :], ALU.mult)
                dve.tensor_copy(get_row[:, :, slot], rowf[:, slot, :])
                dve.tensor_scalar(near[:, :], kept[:, slot, :], -float(SKIP), float(SKIP), ALU.mult, ALU.add)
                dve.drain()
                dve.tensor_tensor(put_row[:, :, slot], rowf[:, slot, :], near[:, :], ALU.add)
                dve.drain()
            dve.tensor_copy(near[:, 0:1], near[:, 0:1]).then_inc(routes, 1)
            yb = (psR, psO)
            tb = (psT, psP)

            def add_bias(k, t):
                n = k * (2 * XT) + t
                dve.wait_ge(yrow_ps, n + 1 + C)
                dve.wait_ge(rows_out_s[t % 2], k * (16 * XT) + 16 * (t // 2) + C)
                dve.tensor_tensor(rows_out[:, t % 2, :, :], yb[t % 2][:, 0:2 * P].rearrange("p (r d) -> p r d", r=2),
                                  b2_sb[:, t // XT, :].unsqueeze(1).broadcast_to([P, 2, DM]), ALU.add).then_inc(yrow_sb, 1)

            with dve.Fori(0, E0 // 2) as k:
                for t in range(2 * XT):
                    n = k * (2 * XT) + t
                    dve.wait_ge(rT_ps, n + 1 + C)
                    if t >= 2:
                        dve.wait_ge(hid_ps, n - 1 + C)
                    else:
                        dve.wait_ge(hid_ps, k * (2 * XT) + C)
                    dve.tensor_copy(rowsT[:, t % 2, :], tb[t % 2][:, 0:2 * P]).then_inc(rT_sb, 1)
                    if t % XT == 0:
                        dve.wait_ge(w_in[t // XT], k * 64 + 64 + C)
                    if t >= 1:
                        add_bias(k, t - 1)
                add_bias(k, 2 * XT - 1)
            if STOP != "C":
              with dve.Fori(0, T // 2) as k:
                i0 = k * 2
                for j in range(2):
                    i = i0 + j
                    xt = tile(xres, k, j)
                    gt = tile(gate, k, j)
                    dve.wait_ge(fetched_s[j], k * 32 + 32)
                    dve.scalar_tensor_tensor(moe[:, :], fetched[:, j, 0, :], gt[:, 0:1], tile(hres, k, j), ALU.mult, ALU.add)
                    dve.drain()
                    dve.scalar_tensor_tensor(moe2[:, :], fetched[:, j, 1, :], gt[:, 1:2], moe[:, :], ALU.mult, ALU.add).then_inc(merged, 1)
                    dve.drain()
                    dve.bn_stats(stats3[:, :], moe2[:, :])
                    dve.drain()
                    dve.bn_aggr(mv3[:, :], stats3[:, :])
                    dve.drain()
                    dve.tensor_scalar(veps3[:, :], mv3[:, 1:2], EPS, None, ALU.add).then_inc(m_var, 1)
                    dve.wait_ge(m_rstd, i + 1 + C)
                    dve.tensor_scalar(moe[:, :], moe2[:, :], mv3[:, 0:1], rstd3[:, 0:1], ALU.subtract, ALU.mult)
                    dve.drain()
                    dve.tensor_tensor(moe[:, :], moe[:, :], tggamma[:, :], ALU.mult)
                    dve.tensor_tensor(xt, xt, tgbeta[:, :], ALU.add)
                    dve.drain()
                    dve.tensor_tensor(xt, xt, moe[:, :], ALU.add)
                    dve.drain()
                    dve.bn_stats(stats[:, :], xt)
                    dve.drain()
                    dve.bn_aggr(mv[:, :], stats[:, :])
                    dve.drain()
                    dve.tensor_scalar(veps[:, :], mv[:, 1:2], EPS, None, ALU.add).then_inc(x_var, 1)
                    dve.wait_ge(x_rstd, T + i + 1 + C)
                    dve.wait_ge(xT_p, i + C)
                    dve.tensor_scalar(xn[:, :], xt, mv[:, 0:1], rstd[:, 0:1], ALU.subtract, ALU.mult).then_inc(x_norm, 1)
                    dve.wait_ge(vdup_s[j], k * 32 + 32 + C)
                    dve.wait_ge(av, T + i0 + C)
                    for h in range(2):
                        rows = slice(h * SEQ, (h + 1) * SEQ)
                        v = vdup[rows, j, :, :].rearrange("p b (g j h d) -> p (b g) j h d", g=G, j=2, h=2)[:, :, h, :, :]
                        dst = vx[rows, j, :, :, :, h, 0:HD].rearrange("p b g h d -> p (b g) h d")
                        dve.tensor_copy(dst, v).then_inc(vx_w, 1)
                    dve.wait_ge(xT_p, i + 1 + C)
                    dve.wait_ge(scores, T + i + C)
                    for b in range(2):
                        q = psP[:, b * SEQ:(b + 1) * SEQ].unsqueeze(1).broadcast_to([P, 4, SEQ])
                        dve.tensor_tensor(qx[:, b, :, :], q, headmask[:, b, :, :], ALU.mult).then_inc(qx_w, 1)
                for j in range(2):
                    i = i0 + j
                    s4 = psS[:, :, 0:2 * P].rearrange("p g (a k) -> p g a k", k=SEQ)
                    dve.wait_ge(scores, T + i + 1 + C)
                    dve.tensor_reduce(mx[:, :].rearrange("p (g a) -> p g a", g=G), s4, AX.X, ALU.max).then_inc(smax, 1)
                    dve.wait_ge(smax, T + i + 1 + C)
                    dve.wait_ge(pT_ps, 2 * T + i0 * 2 + C)
                    dve.tensor_tensor(es[:, j].rearrange("p g b (a k) -> p g (b a) k", k=SEQ), s4,
                                      mx[:, :].rearrange("p (g a) -> p g a", g=G).unsqueeze(3).broadcast_to([P, G, 4, SEQ]),
                                      ALU.subtract).then_inc(shifted, 1)
                for j in range(2):
                    i = i0 + j
                    xt = tile(xres, k, j)
                    dve.wait_ge(av, T + i + 1 + C)
                    dve.reciprocal(rc[:, :], o_ps[:, :, HD]).then_inc(recip, 1)
                    dve.wait_ge(recip, T + i + 1 + C)
                    dve.tensor_tensor(osb[:, :, :], o_ps[:, :, 0:HD], rc[:, :].unsqueeze(2).broadcast_to([P, NH, HD]),
                                      ALU.mult).then_inc(o_norm, 1)
                    dve.drain()
                    dve.scalar_tensor_tensor(xt, osb[:, :, :].rearrange("p h d -> p (h d)"), tg[:, 1:2], xt, ALU.mult, ALU.add).then_inc(x_res, 1)
                    dve.drain()
                    dve.bn_stats(stats2[:, :], xt)
                    dve.drain()
                    dve.bn_aggr(mv2[:, :], stats2[:, :])
                    dve.drain()
                    dve.tensor_scalar(veps2[:, :], mv2[:, 1:2], EPS, None, ALU.add).then_inc(h_var, 1)
                    dve.wait_ge(h_rstd, T + i + 1 + C)
                    dve.wait_ge(h_kept, T + i + C)
                    dve.tensor_scalar(hn[:, :], xt, mv2[:, 0:1], rstd2[:, 0:1], ALU.subtract, ALU.mult).then_inc(h_norm, 1)
                    dve.drain()
                    dve.tensor_tensor_reduce(hsq[:, :], hn[:, :], hn[:, :], 1.0, 1e-12, ALU.mult, ALU.add, ssum[:, :]).then_inc(n_sum, 1)
                    dve.wait_ge(n_root, i + 1 + C)
                    dve.wait_ge(lg_p, T + i + 1 + C)
                    dve.scalar_tensor_tensor(lgr[:, :], lg_ps, rnorm[:, 0:1], sig[:, :], ALU.mult, ALU.subtract).then_inc(lg_s, 1)
                    dve.drain()
                    dve.max(mx8[:, :], lgr[:, :])
                    dve.tensor_scalar(relu[:, :], lgr[:, :], 0.0, None, ALU.max)
                    dve.tensor_scalar(active[:, :], lgr[:, :], 0.0, None, ALU.is_gt)
                    dve.drain()
                    dve.tensor_scalar(nomax[:, :], mx8[:, 0:1], 0.0, -1.0, ALU.max, ALU.mult).then_inc(g_in, 1)
                    dve.max_index(ix8[:, :], mx8[:, :], lgr[:, :])
                    dve.tensor_scalar(idle[:, :], mx8[:, 0:1], 0.0, None, ALU.is_le)
                    dve.drain()
                    dve.tensor_copy(ixf[:, :], ix8[:, 0:2])
                    dve.drain()
                    dve.tensor_scalar(oneh[:, :], iota16[:, :], ixf[:, 0:1], None, ALU.is_equal)
                    dve.drain()
                    dve.scalar_tensor_tensor(oneh2[:, :], iota16[:, :], ixf[:, 1:2], oneh[:, :], ALU.is_equal, ALU.add)
                    dve.drain()
                    dve.scalar_tensor_tensor(oneh[:, :], oneh2[:, :], idle[:, 0:1], active[:, :], ALU.mult, ALU.add)
                    dve.drain()
                    dve.wait_ge(g_ex, i + 1 + C)
                    dve.tensor_tensor_reduce(gpr[:, :], gex[:, :], oneh[:, :], 1.0, 0.0, ALU.mult, ALU.add, gsum[:, :])
                    dve.drain()
                    dve.reciprocal(grec[:, :], gsum[:, :])
                    dve.drain()
                    dve.tensor_scalar(tile(rw, k, j), gpr[:, :], grec[:, 0:1], None, ALU.mult).then_inc(rw_s, 1)
            if not STOP:
                def weigh(k, j, i):
                    dve.wait_ge(xsT_p, i * 4 + C)
                    dve.wait_ge(h_kept, T + i + 1 + C)
                    dve.tensor_tensor(xs[:, :, :], tile(hres, k, j).unsqueeze(1).broadcast_to([P, E1, DM]),
                                      tile(rw, k, j).unsqueeze(2).broadcast_to([P, E1, DM]), ALU.mult).then_inc(xs_s, 1)

                def projected(i, j):
                    dve.wait_ge(qkv_p, i + 1 + C)
                    dve.wait_ge(qkT_p, i + C)
                    dve.tensor_copy(qkv[:, 0:2 * DM], psP[:, 0:2 * DM])
                    dve.tensor_copy(v2[:, j, :], psP[:, 2 * DM:3 * DM]).then_inc(qkv_s, 1)

                def softmax(i):
                    dve.wait_ge(sc_p, i + 1 + C)
                    dve.wait_ge(pr_e, i + C)
                    dve.scalar_tensor_tensor(sc[:, :], psT[:, 2 * P:3 * P], float(DM) ** -0.5, causal[:, :], ALU.mult, ALU.add)
                    dve.drain()
                    dve.tensor_reduce(scmax[:, :], sc[:, :], AX.X, ALU.max, negate=True).then_inc(sc_m, 1)
                    dve.wait_ge(pr_e, i + 1 + C)
                    dve.reciprocal(screc[:, :], scsum[:, :])
                    dve.drain()
                    dve.tensor_scalar(pr[:, :], pr[:, :], screc[:, 0:1], None, ALU.mult).then_inc(pr_s, 1)

                def combine(k, j, i):
                    rwi = tile(rw, k, j)
                    xt = tile(xres, k, j)
                    for c in range(4):
                        dve.wait_ge(z_p, i * 4 + c + 1 + C)
                        dve.tensor_tensor(z[:, 4 * c:4 * c + 4, :], (psR, psO)[c % 2][:, :].rearrange("p (e d) -> p e d", e=4),
                                          rwi[:, 4 * c:4 * c + 4].unsqueeze(2).broadcast_to([P, 4, DM]), ALU.mult).then_inc(z_s, 1)
                    dve.drain()
                    dve.tensor_reduce(zsum[:, :], z[:, :, :].rearrange("p e d -> p d e"), AX.X, ALU.add)
                    dve.drain()
                    dve.wait_ge(res_out[j], k * 16 + C)
                    dve.scalar_tensor_tensor(result[:, j, :], zsum[:, :], tg[:, 3:4], xt, ALU.mult, ALU.add).then_inc(res_s, 1)

                weigh(0, 0, 0)
                projected(0, 0)
                last = T // 2 - 1
                with dve.Fori(0, last) as k:
                    for j in range(2):
                        i = k * 2 + j
                        weigh(k + j, 1 - j, i + 1)
                        softmax(i)
                        projected(i + 1, 1 - j)
                        combine(k, j, i)
                weigh(last, 1, T - 1)
                softmax(T - 2)
                projected(T - 1, 1)
                combine(last, 0, T - 2)
                softmax(T - 1)
                combine(last, 1, T - 1)

        @block.scalar
        def _(act):
            act.wait_ge(loads, 16 * (len(LOADS) + 1))
            act.activation(tg[:, :], g_sb[:, :], ACT.Tanh).then_inc(tanhs, 1)
            act.activation(sig[:, :], sig[:, :], ACT.Exp, scale=-1.0).then_inc(tanhs, 1)
            act.wait_ge(consts, 1)
            with act.Fori(0, T // 2) as k:
                i0 = k * 2
                for j in range(2):
                    i = i0 + j
                    act.wait_ge(xc_ps, i + 1 + C)
                    act.wait_ge(proj, i + C)
                    act.copy(xT[:, :], psT[:, 0:P]).then_inc(xc_sb, 1)
                    act.copy(cT[:, :, :, :], psT[:, P:2 * P].rearrange("p (b k) -> p b k", b=2).unsqueeze(2)
                             .broadcast_to([P, 2, 2, SEQ])).then_inc(xc_sb, 1)
                    act.wait_ge(proj, i + 1 + C)
                    act.wait_ge(scores, i + C)
                    act.activation(kT[:, :], psT[:, 2 * P:3 * P], ACT.Identity, bias=bk_sb[:, 0:1]).then_inc(kT_w, 1)
                for j in range(2):
                    i = i0 + j
                    act.wait_ge(shifted, i + 1 + C)
                    e = es[:, j].rearrange("p g b k -> p (g b k)")
                    act.activation(e, e, ACT.Exp, scale=SCALE).then_inc(probs, 1)
                for j in range(2):
                    i = i0 + j
                    for b in range(2):
                        act.wait_ge(pT_ps, i * 2 + b + 1 + C)
                        act.wait_ge(av, i + C)
                        act.copy(pT[:, b].rearrange("p g k -> p (g k)"), psR[:, :]).then_inc(pT_sb, 1)
                    act.wait_ge(oT_p, i + 1 + C)
                    act.copy(oT[:, :], oT_ps).then_inc(oT_s, 1)
                    act.wait_ge(hT_p, i + 1 + C)
                    act.copy(hT[:, :], oT_ps).then_inc(hT_s, 1)

            act.wait_ge(routes_d, 1)
            act.activation(gexp[:, 1, :], dist[:, :], ACT.Exp, scale=-1.0).then_inc(gexp_s, 1)
            with act.Fori(0, E0 // 2) as k:
                for t in range(2 * XT):
                    j = t // XT
                    n = k * (2 * XT) + t
                    if t % XT == 0:
                        act.wait_ge(w_in[j], k * 64 + 64 + C)
                    act.wait_ge(hid_ps, n + 1 + C)
                    if t >= 2:
                        act.wait_ge(yrow_ps, n - 1 + C)
                    else:
                        act.wait_ge(yrow_ps, k * (2 * XT) + C)
                    for f in range(FB):
                        m = act.activation(hidT[:, t % 2, f, :], psS[:, 2 * (t % 2) + f // 2, (f % 2) * 256:(f % 2) * 256 + 256],
                                           ACT.Gelu, bias=b1_sb[:, j, f:f + 1])
                    m.then_inc(hid_sb, 1)
            if STOP != "C":
              with act.Fori(0, T // 2) as k:
                i0 = k * 2
                for j in range(2):
                    i = i0 + j
                    act.wait_ge(cT_p, i + 1 + C)
                    act.wait_ge(scores, T + i + C)
                    act.copy(kT[:, :], psT[:, 0:P]).then_inc(kT_w, 1)
                for j in range(2):
                    i = i0 + j
                    act.wait_ge(shifted, T + i + 1 + C)
                    e = es[:, j].rearrange("p g b k -> p (g b k)")
                    act.activation(e, e, ACT.Exp, scale=SCALE).then_inc(probs, 1)
                for j in range(2):
                    i = i0 + j
                    for b in range(2):
                        act.wait_ge(pT_ps, 2 * T + i * 2 + b + 1 + C)
                        act.wait_ge(av, T + i + C)
                        act.copy(pT[:, b].rearrange("p g k -> p (g k)"), psR[:, :]).then_inc(pT_sb, 1)
                    act.wait_ge(hT_p, T + i + 1 + C)
                    act.copy(hT[:, :], oT_ps).then_inc(hT_s, 1)
                    act.wait_ge(g_in, i + 1 + C)
                    act.activation(gex[:, :], relu[:, :], ACT.Exp, bias=nomax[:, 0:1]).then_inc(g_ex, 1)
            if not STOP:
                def evac(i):
                    for c in range(4):
                        act.wait_ge(xsT_p, i * 4 + c + 1 + C)
                        act.wait_ge(qkv_p, i + C)
                        act.copy(xsT[:, 4 * c:4 * c + 4, :].rearrange("p e t -> p (e t)"), psS[:, c, :]).then_inc(xsT_s, 1)

                def attend(i, j):
                    act.wait_ge(qkT_p, i + 1 + C)
                    act.copy(qkT[:, :], psT[:, 0:2 * P]).then_inc(qkT_s, 1)
                    act.wait_ge(sc_m, i + 1 + C)
                    act.wait_ge(prT_p, i + C)
                    act.activation(pr[:, :], sc[:, :], ACT.Exp, bias=scmax[:, 0:1], accum_out=scsum[:, :]).then_inc(pr_e, 1)
                    act.wait_ge(prT_p, i + 1 + C)
                    act.copy(prT[:, :], psT[:, 3 * P:4 * P]).then_inc(prT_s, 1)
                    act.wait_ge(ao_p, i + 1 + C)
                    act.copy(aoT[:, :], psT[:, 0:P]).then_inc(ao_s, 1)

                evac(0)
                with act.Fori(0, T // 2 - 1) as k:
                    for j in range(2):
                        evac(k * 2 + j + 1)
                        attend(k * 2 + j, j)
                evac(T - 1)
                attend(T - 2, 0)
                attend(T - 1, 1)

        @block.tensor
        def _(pe):
            pe.wait_ge(consts, 1)
            with pe.Fori(0, T // 2) as k:
                i0 = k * 2
                for j in range(2):
                    i = i0 + j
                    pe.wait_ge(xc_sb, i * 2 + C)
                    pe.wait_ge(kT_w, i + C)
                    pe.wait_ge(x_norm, i + 1 + C)
                    pe.transpose(psT[:, 0:P], xn[:, :], ident[:, :])
                    pe.wait_ge(ctx_in_s, i * 16 + 16 + C)
                    pe.transpose(psT[:, P:2 * P], ctok[:, 0, :], ident[:, :]).then_inc(xc_ps, 1)
                    pe.wait_ge(xc_sb, i * 2 + 2 + C)
                    pe.wait_ge(qx_w, i * 2 + C)
                    pe.wait_ge(kT_w, i + C)
                    pe.wait_ge(vx_w, i * 2 + C)
                    pe.matmul(psP[:, 0:P], wq_sb[:, :], xT[:, :], start=True, stop=True)
                    pe.matmul(psT[:, 2 * P:3 * P], wk_sb[:, :], cT[:, :, 0, :], start=True, stop=True)
                    for b in range(2):
                        m = pe.matmul(psP[:, (2 + b) * P:(3 + b) * P],
                                      cT[:, b, :, :], wv_sb[:, :], start=True, stop=True)
                    m.then_inc(proj, 1)
                    pe.wait_ge(qx_w, i * 2 + 2 + C)
                    pe.wait_ge(kT_w, i + 1 + C)
                    pe.wait_ge(shifted, i + C)
                    for b in range(2):
                        for hj in range(2):
                            for g in range(G):
                                rows = slice(32 * g, 32 * g + 32)
                                m = pe.matmul(psS[:, g, (2 * b + hj) * SEQ:(2 * b + hj + 1) * SEQ],
                                              qx[rows, b, 2 * hj:2 * hj + 2, :], kT[rows, b * SEQ:(b + 1) * SEQ],
                                              start=True, stop=True)
                    m.then_inc(scores, 1)
                for j in range(2):
                    i = i0 + j
                    pe.wait_ge(probs, i + 1 + C)
                    for b in range(2):
                        pe.wait_ge(pT_sb, i * 2 + b + C)
                        for g in range(G):
                            m = pe.transpose(psR[:, g * P:(g + 1) * P], es[:, j, g, b, :], ident[:, :])
                        m.then_inc(pT_ps, 1)
                    pe.wait_ge(vx_w, i * 2 + 2 + C)
                    pe.wait_ge(lg_s, i + C)
                    for b in range(2):
                        pe.wait_ge(pT_sb, i * 2 + b + 1 + C)
                        for g in range(G):
                            for h in range(2):
                                head = 4 * g + h
                                m = pe.matmul(o_ps[b * SEQ:(b + 1) * SEQ, head:head + 3:2, :],
                                              pT[:, b, g, h * SEQ:(h + 1) * SEQ], vx[:, j, b, g, h, :, :],
                                              start=True, stop=True)
                    m.then_inc(av, 1)
                    pe.wait_ge(o_norm, i + 1 + C)
                    pe.transpose(oT_ps, osb[:, :, :].rearrange("p h d -> p (h d)"), ident[:, :]).then_inc(oT_p, 1)
                    pe.wait_ge(oT_s, i + 1 + C)
                    pe.matmul(y_ps, oT[:, :], wo_sb[:, :], start=True, stop=True).then_inc(y_p, 1)
                    pe.wait_ge(h_norm, i + 1 + C)
                    pe.transpose(oT_ps, hn[:, :], ident[:, :]).then_inc(hT_p, 1)
                    pe.wait_ge(hT_s, i + 1 + C)
                    pe.matmul(psO[:, 400:400 + E0], hT[:, :], wr_sb[:, :], start=True, stop=True).then_inc(lg_p, 1)
            pe.wait_ge(simprep, 1)
            pe.matmul(psT[:, 0:E1], ones[:, :], simsq[:, :], start=True, stop=True).then_inc(counted, 1)
            with pe.Fori(0, 32) as n:
                pe.wait_ge(searched, n + 1 + C)
                pe.matmul(psP[:, 0:E0], ones_bf[:, :], counts[:, :], start=True, stop=True).then_inc(counted, 1)
            pe.wait_ge(searched, 33 + C)
            pe.matmul(psP[:, 0:E0], ones_bf[:, :], counts[:, :], start=True, stop=True).then_inc(counted, 1)
            for r in range(2):
                pe.wait_ge(searched, 34 + r + C)
                f = flags[:, :, :].rearrange("p e t -> p (e t)")
                pe.matmul(psT[:, :], before[:, :], f, start=True, stop=True)
                pe.matmul(psR[:, :], ones_bf[:, :], f, start=True, stop=True).then_inc(counted, 1)
            yb = (psR, psO)
            tb = (psT, psP)

            def expert_out_rows(k, t):
                n = k * (2 * XT) + t
                pe.wait_ge(hid_sb, n + 1 + C)
                if t >= 2:
                    pe.wait_ge(yrow_sb, n - 1 + C)
                else:
                    pe.wait_ge(yrow_sb, k * (2 * XT) + C)
                for r in range(2):
                    for f in range(FB):
                        m = pe.matmul(yb[t % 2][:, r * P:(r + 1) * P], hidT[:, t % 2, f, r * P:(r + 1) * P],
                                      w2_sb[:, t // XT, f, :], start=(f == 0), stop=(f == FB - 1))
                m.then_inc(yrow_ps, 1)

            with pe.Fori(0, E0 // 2) as k:
                for t in range(2 * XT):
                    n = k * (2 * XT) + t
                    if t >= 2:
                        pe.wait_ge(rT_sb, n - 1 + C)
                    else:
                        pe.wait_ge(rT_sb, k * (2 * XT) + C)
                    pe.wait_ge(rows_in_s[t % 2], k * (16 * XT) + 16 * (t // 2) + 16 + C)
                    for r in range(2):
                        m = pe.transpose(tb[t % 2][:, r * P:(r + 1) * P], rows_in[:, t % 2, r, :], ident[:, :])
                    m.then_inc(rT_ps, 1)
                    if t % XT == 0:
                        pe.wait_ge(w_in[t // XT], k * 64 + 64 + C)
                    pe.wait_ge(rT_sb, n + 1 + C)
                    if t >= 2:
                        pe.wait_ge(hid_sb, n - 1 + C)
                    else:
                        pe.wait_ge(hid_sb, k * (2 * XT) + C)
                    for f in range(FB):
                        m = pe.matmul(psS[:, 2 * (t % 2) + f // 2, (f % 2) * 256:(f % 2) * 256 + 256],
                                      w1_sb[:, t // XT, f * P:(f + 1) * P], rowsT[:, t % 2, :], start=True, stop=True)
                    m.then_inc(hid_ps, 1)
                    if t >= 1:
                        expert_out_rows(k, t - 1)
                expert_out_rows(k, 2 * XT - 1)
            if STOP != "C":
              with pe.Fori(0, T // 2) as k:
                i0 = k * 2
                for j in range(2):
                    i = i0 + j
                    pe.wait_ge(ctx2_s, i * 16 + 16 + C)
                    pe.wait_ge(kT_w, T + i + C)
                    pe.transpose(psT[:, 0:P], ctok[:, 1, :], ident[:, :]).then_inc(cT_p, 1)
                    pe.wait_ge(x_norm, T + i + 1 + C)
                    pe.wait_ge(qx_w, 2 * T + i * 2 + C)
                    pe.transpose(psP[:, 0:P], xn[:, :], ident[:, :]).then_inc(xT_p, 1)
                    pe.wait_ge(qx_w, 2 * T + i * 2 + 2 + C)
                    pe.wait_ge(kT_w, T + i + 1 + C)
                    pe.wait_ge(shifted, T + i + C)
                    for g in range(G):
                        pe.matmul(psS[:, g, 0:2 * P], ident_bf[:, :], band4[:, :, :], start=True, stop=True, skip_group_check=True)
                    for b in range(2):
                        for hj in range(2):
                            for g in range(G):
                                rows = slice(32 * g, 32 * g + 32)
                                m = pe.matmul(psS[:, g, (2 * b + hj) * SEQ:(2 * b + hj + 1) * SEQ],
                                              qx[rows, b, 2 * hj:2 * hj + 2, :], kT[rows, b * SEQ:(b + 1) * SEQ],
                                              start=False, stop=True, skip_group_check=True)
                    m.then_inc(scores, 1)
                for j in range(2):
                    i = i0 + j
                    pe.wait_ge(probs, T + i + 1 + C)
                    for b in range(2):
                        pe.wait_ge(pT_sb, 2 * T + i * 2 + b + C)
                        for g in range(G):
                            m = pe.transpose(psR[:, g * P:(g + 1) * P], es[:, j, g, b, :], ident[:, :])
                        m.then_inc(pT_ps, 1)
                    pe.wait_ge(vx_w, 2 * T + i * 2 + 2 + C)
                    pe.wait_ge(lg_s, T + i + C)
                    for b in range(2):
                        pe.wait_ge(pT_sb, 2 * T + i * 2 + b + 1 + C)
                        for g in range(G):
                            for h in range(2):
                                head = 4 * g + h
                                m = pe.matmul(o_ps[b * SEQ:(b + 1) * SEQ, head:head + 3:2, :],
                                              pT[:, b, g, h * SEQ:(h + 1) * SEQ], vx[:, j, b, g, h, :, :],
                                              start=True, stop=True)
                    m.then_inc(av, 1)
                    pe.wait_ge(h_norm, T + i + 1 + C)
                    pe.transpose(oT_ps, hn[:, :], ident[:, :]).then_inc(hT_p, 1)
                    pe.wait_ge(hT_s, T + i + 1 + C)
                    pe.matmul(lg_ps, hT[:, :], simn[:, :], start=True, stop=True).then_inc(lg_p, 1)
            if not STOP:
                zb = (psR, psO)

                def turn(i):
                    pe.wait_ge(xs_s, i + 1 + C)
                    for c in range(4):
                        pe.wait_ge(xsT_s, i * 4 + c + C)
                        for e in range(4 * c, 4 * c + 4):
                            m = pe.transpose(psS[:, c, (e % 4) * P:(e % 4 + 1) * P], xs[:, e, :], ident[:, :])
                        m.then_inc(xsT_p, 1)

                def project(i, lo, hi):
                    if lo == 0:
                        pe.wait_ge(qkv_s, i + C)
                    for e in range(lo, hi):
                        pe.wait_ge(xsT_s, i * 4 + e // 4 + 1 + C)
                        m = pe.matmul(psP[:, 0:3 * DM], xsT[:, e, :], wqkv[:, e, :], start=(e == 0), stop=(e == E1 - 1))
                    if hi == E1:
                        m.then_inc(qkv_p, 1)

                def qk_turn(i):
                    pe.wait_ge(qkv_s, i + 1 + C)
                    pe.wait_ge(ao_s, i + C)
                    pe.transpose(psT[:, 0:P], qkv[:, 0:P], ident[:, :])
                    pe.transpose(psT[:, P:2 * P], qkv[:, P:2 * P], ident[:, :]).then_inc(qkT_p, 1)

                def attention(i):
                    pe.wait_ge(qkT_s, i + 1 + C)
                    pe.matmul(psT[:, 2 * P:3 * P], qkT[:, 0:P], qkT[:, P:2 * P], start=True, stop=True).then_inc(sc_p, 1)

                def out_rows(i, j):
                    pe.wait_ge(pr_s, i + 1 + C)
                    pe.transpose(psT[:, 3 * P:4 * P], pr[:, :], ident[:, :]).then_inc(prT_p, 1)
                    pe.wait_ge(prT_s, i + 1 + C)
                    pe.matmul(psT[:, 0:P], v2[:, j, :], prT[:, :], start=True, stop=True).then_inc(ao_p, 1)
                    pe.wait_ge(ao_s, i + 1 + C)
                    for c in range(4):
                        if c >= 2:
                            pe.wait_ge(z_s, i * 4 + c - 1 + C)
                        else:
                            pe.wait_ge(z_s, i * 4 + C)
                        pe.matmul(zb[c % 2][:, :], aoT[:, :], wo1[:, 4 * c:4 * c + 4, :], start=True, stop=True).then_inc(z_p, 1)

                pe.wait_ge(ewts, 64)
                turn(0)
                project(0, 0, E1)
                with pe.Fori(0, T // 2 - 1) as k:
                    for j in range(2):
                        i = k * 2 + j
                        turn(i + 1)
                        qk_turn(i)
                        project(i + 1, 0, 4)
                        attention(i)
                        project(i + 1, 4, E1)
                        out_rows(i, j)
                turn(T - 1)
                qk_turn(T - 2)
                project(T - 1, 0, 4)
                attention(T - 2)
                project(T - 1, 4, E1)
                out_rows(T - 2, 0)
                qk_turn(T - 1)
                attention(T - 1)
                out_rows(T - 1, 1)


_INS = ['x', 'ctx_1024', 'g_xattn', 'g_ffn', 'L0_xattn_Wq', 'L0_xattn_bq', 'L0_xattn_Wk', 'L0_xattn_bk', 'L0_xattn_Wv',
        'L0_xattn_bv', 'L0_xattn_Wo', 'L0_xattn_bo', 'L0_ffn_Wr', 'L0_ffn_br', 'L0_ffn_W1', 'L0_ffn_b1', 'L0_ffn_W2',
        'L0_ffn_b2', 'L0_ffn_gamma', 'L0_ffn_beta', 'L0_ffn_token_mask', 'L1_ffn_sim_matrix', 'L1_ffn_gates',
        'L1_ffn_q_proj', 'L1_ffn_k_proj', 'L1_ffn_v_proj', 'L1_ffn_o_proj']
_OUTS = [((128, 64, 128), 'float32')]


def kernel(**inputs):
    import numpy as _np
    import concourse.bacc as _bacc
    from concourse import mybir as _mybir
    from concourse.bass_utils import run_bass_kernel_spmd as _run

    nc = _bacc.Bacc("TRN2", target_bir_lowering=False, num_devices=1)
    arrays, args = {}, []
    for name in _INS:
        a = _np.ascontiguousarray(inputs[name])
        arrays[f"in_{name}_dram"] = a
        args.append(nc.dram_tensor(f"in_{name}_dram", a.shape, _mybir.dt.from_np(a.dtype), kind="ExternalInput").ap())
    for i, (shape, dtype) in enumerate(_OUTS):
        dt = _mybir.dt.from_np(_np.dtype(dtype))
        args.append(nc.dram_tensor(f"out_{i}_dram", shape, dt, kind="ExternalOutput").ap())
    build(nc, *args)
    r = _run(nc, [arrays], core_ids=[0])
    got = tuple(r.results[0][f"out_{i}_dram"] for i in range(len(_OUTS)))
    return got[0]
```

```python
from contextlib import ExitStack

import concourse.bass as bass
from concourse import mybir

ALU = mybir.AluOpType
ACT = mybir.ActivationFunctionType
F32 = mybir.dt.float32
BF16 = mybir.dt.bfloat16
I32 = mybir.dt.int32
U32 = mybir.dt.uint32
AX = mybir.AxisListType

P = 128
B, SEQ, DM = 128, 64, 128
N = B * SEQ
T = N // P
NH = 16
HD = DM // NH
SCALE = float(HD) ** -0.5
G = 4
E0, F0 = 8, 512
FB = F0 // P
CAP = 1280
ROWS = E0 * CAP
XT = CAP // 256
E1 = 16
EPS = 1e-5
BAND = 4
NEG = -1.0e30
LOWEST = -3.0e38
SATURATED = 16.635532
RING = 8
SKIP = 1 << 20
W1COL = HD + 1
C = 2


def build(nc, x, ctx_in, g_xattn, g_ffn, Wq, bq, Wk, bk, Wv, bv, Wo, bo, Wr, br, W1, b1, W2, b2,
          gamma, beta, token_mask, sim_matrix, gates, q_proj, k_proj, v_proj, o_proj, out):
    with ExitStack() as stack:
        def sb(name, shape, dt=F32):
            return stack.enter_context(nc.sbuf_tensor(name, shape, dt))

        def sem(name):
            return stack.enter_context(nc.semaphore(name))

        x_d = x.rearrange("b s d -> (b s) d").rearrange("(t p) d -> p t d", p=P)
        out_d = out.rearrange("b s d -> (b s) d").rearrange("(t p) d -> p t d", p=P)
        ctx_d = ctx_in.rearrange("b s d -> (b s) d").rearrange("(t p) d -> p t d", p=P)
        ctxdup_d = ctx_in.rearrange("(t b) s d -> s t b d", b=2)
        routed = nc.dram_tensor("routed_rows", [ROWS, DM], F32, kind="Internal").ap()
        expert_out = nc.dram_tensor("expert_rows", [ROWS, DM], F32, kind="Internal").ap()

        ident = sb("ident", [P, P])
        ones = sb("ones", [P, P])
        ones_bf = sb("ones_bf", [P, P], BF16)
        ident_bf = sb("ident_bf", [P, P], BF16)
        before = sb("before", [P, P], BF16)
        arena = sb("arena", [P, 3 * E1 * DM])
        zero1 = arena[:, 2 * E1 * DM:3 * E1 * DM]

        def part(n, *dims):
            names = "abcd"[:len(dims)]
            size = 1
            for d in dims:
                size *= d
            return arena[:, n * size:(n + 1) * size].rearrange(
                f"p ({' '.join(names)}) -> p {' '.join(names)}", **dict(zip(names, dims)))

        headmask4 = sb("headmask4", [P, 4])
        headmask = sb("headmask", [P, 2, 4, SEQ])
        band = sb("band", [P, SEQ], BF16)
        band4 = sb("band4", [P, 4, SEQ], BF16)
        causal = sb("causal", [P, P])
        powr = sb("powr", [P, T])
        iota8 = sb("iota8", [P, E0])
        iota16 = sb("iota16", [P, E1])
        caps = sb("caps", [P, E0])
        wq_sb = sb("wq_sb", [P, DM])
        wk_sb = sb("wk_sb", [P, DM])
        wv_sb = sb("wv_sb", [P, DM])
        wo_sb = sb("wo_sb", [P, DM])
        wr_sb = sb("wr_sb", [P, E0])
        bq_sb = sb("bq_sb", [P, 1])
        bk_sb = sb("bk_sb", [P, 1])
        bv_sb = sb("bv_sb", [P, 2, DM])
        bo_sb = sb("bo_sb", [P, DM])
        br_sb = sb("br_sb", [P, E0])
        gamma_sb = sb("gamma_sb", [P, DM])
        beta_sb = sb("beta_sb", [P, DM])
        g_sb = sb("g_sb", [P, 4])
        tg = sb("tg", [P, 4])
        tgbo = sb("tgbo", [P, DM])
        xres = sb("xres", [P, T, DM])
        hres = sb("hres", [P, T, DM])
        stats = sb("stats", [P, 3, 6])
        mv = sb("mv", [P, 3, 2])
        veps = sb("veps", [P, 3])
        root = sb("root", [P, 3])
        squares = sb("squares", [P, 1])
        norm = sb("norm", [P, 1])
        xn = sb("xn", [P, DM])
        ctok = sb("ctok", [P, 2, DM])
        xT = sb("xT", [P, P])
        cT = sb("cT", [P, 2, 2, SEQ])
        qx = sb("qx", [P, 2, 4, SEQ])
        kT = sb("kT", [P, P])
        vx = sb("vx", [P, 2, 2, G, 2, 2, W1COL])
        es = sb("es", [P, 2, G, 2, 2 * SEQ])
        mx = sb("mx", [P, NH])
        pT = sb("pT", [P, 2, G, P])
        rc = sb("rc", [P, NH])
        osb = sb("osb", [P, NH, HD])
        oT = sb("oT", [P, P])
        ytmp = sb("ytmp", [P, DM])
        hn = sb("hn", [P, DM])
        hT = sb("hT", [P, P])
        lg = sb("lg", [P, E0])
        mx8 = sb("mx8", [P, 8])
        ix8 = sb("ix8", [P, 8], U32)
        topv = sb("topv", [P, T, 2])
        topi = sb("topi", [P, T, 2])

        dist = sb("dist", [P, T])
        near = sb("near", [P, T])
        first = part(0, E0, T)
        second = part(1, E0, T)
        key = part(2, E0, T)
        scratch = part(3, E0, T)
        rank = part(4, E0, T)
        keep = part(5, E0, T)
        flags = sb("flags", [P, E0, T], BF16)
        restart = part(6, E0, T)
        counts = sb("counts", [P, E0], BF16)
        thr = sb("thr", [P, E0], I32)
        cand = sb("cand", [P, E0], I32)
        bit = sb("bit", [P, E0], I32)
        accept = sb("accept", [P, E0], I32)
        left = sb("left", [P, E0])
        kept = sb("kept", [P, 2, T])
        gate = sb("gate", [P, T, 2])
        gexp = sb("gexp", [P, 2, T])
        rowf = sb("rowf", [P, 2, T])
        put_row = sb("put_row", [P, T, 2], U32)
        get_row = sb("get_row", [P, T, 2], U32)
        staged = sb("staged", [P, RING, DM])
        staged_row = sb("staged_row", [P, RING, 2], U32)
        w1_sb = part(0, 2, F0)
        w2_sb = part(1, 2, FB, DM)
        b1_sb = sb("b1_sb", [P, 2, FB])
        b2_sb = sb("b2_sb", [P, 2, DM])
        rows_in = sb("rows_in", [P, 2, 2, DM])
        rowsT = sb("rowsT", [P, 2, 2 * P])
        hidT = part(1, 2, FB, 2 * P)
        rows_out = sb("rows_out", [P, 2, 2, DM])
        tggamma = sb("tggamma", [P, DM])
        tgbeta = sb("tgbeta", [P, DM])
        fetch_row = sb("fetch_row", [P, 2, 2], U32)
        fetched = sb("fetched", [P, 2, 2, DM])
        moe = sb("moe", [P, DM])
        moe2 = sb("moe2", [P, DM])
        moen = sb("moen", [P, DM])
        vdup = sb("vdup", [P, 2, 2, DM])
        sim_sb = sb("sim_sb", [P, E1])
        simsq = sb("simsq", [P, E1])
        simn = sb("simn", [P, E1])
        sig = sb("sig", [P, E1])
        hsq = sb("hsq", [P, DM])
        lgr = sb("lgr", [P, E1])
        relu = sb("relu", [P, E1])
        active = sb("active", [P, E1])
        nomax = sb("nomax", [P, 1])
        idle = sb("idle", [P, 1])
        ixf = sb("ixf", [P, 2])
        oneh = sb("oneh", [P, E1])
        oneh2 = sb("oneh2", [P, E1])
        gex = sb("gex", [P, E1])
        gpr = sb("gpr", [P, E1])
        gsum = sb("gsum", [P, 1])
        grec = sb("grec", [P, 1])
        rw = sb("rw", [P, T, E1])
        wqkv = sb("wqkv", [P, E1, 3 * DM])
        wo1 = sb("wo1", [P, E1, DM])
        xs = part(0, E1, DM)
        xsT = sb("xsT", [P, 2, E1, DM])
        qkv = sb("qkv", [P, 2, 3 * DM])
        qkT = sb("qkT", [P, 2 * P])
        sc = sb("sc", [P, P])
        scmax = sb("scmax", [P, 1])
        scsum = sb("scsum", [P, 1])
        screc = sb("screc", [P, 1])
        pr = sb("pr", [P, P])
        prn = sb("prn", [P, P])
        prT = sb("prT", [P, P])
        aoT = sb("aoT", [P, P])
        rwt = sb("rwt", [P, E1])
        z = part(1, E1, DM)
        zsum = sb("zsum", [P, DM])
        result = sb("result", [P, 2, DM])

        psS = stack.enter_context(nc.psum_tensor("psS", [P, G, 512], F32))
        psT = stack.enter_context(nc.psum_tensor("psT", [P, 512], F32))
        psP = stack.enter_context(nc.psum_tensor("psP", [P, 512], F32))
        psR = stack.enter_context(nc.psum_tensor("psR", [P, 512], F32))
        psO = stack.enter_context(nc.psum_tensor("psO", [P, 512], F32))
        o_ps = psO[:, 0:NH * W1COL].rearrange("p (h w) -> p h w", w=W1COL)
        y_ps = psO[:, 272:400]
        zb = (psP, psR, psO)
        pq = (psS[:, 2, :], psS[:, 3, :])
        lg_ps = psO[:, 400:400 + E1]

        loads = sem("loads")
        made = sem("made")
        consts = sem("consts")
        prep = sem("prep")
        tanhs = sem("tanhs")
        x_in = sem("x_in")
        ctx_s = [sem(f"ctx_s{j}") for j in range(2)]
        variances = sem("variances")
        roots = sem("roots")
        x_norm = sem("x_norm")
        xc_ps = sem("xc_ps")
        xc_sb = sem("xc_sb")
        proj = sem("proj")
        qx_w = sem("qx_w")
        kT_w = sem("kT_w")
        vx_w = sem("vx_w")
        scores = sem("scores")
        shifted = sem("shifted")
        probs = sem("probs")
        pT_ps = sem("pT_ps")
        pT_sb = sem("pT_sb")
        av = sem("av")
        o_norm = sem("o_norm")
        oT_p = sem("oT_p")
        oT_s = sem("oT_s")
        y_p = sem("y_p")
        y_s = sem("y_s")
        h_norm = sem("h_norm")
        h_kept = sem("h_kept")
        hT_p = sem("hT_p")
        hT_s = sem("hT_s")
        lg_p = sem("lg_p")
        lg_s = sem("lg_s")
        top = sem("top")
        top_kept = sem("top_kept")
        out_s = sem("out_s")
        searched = sem("searched")
        counted = sem("counted")
        simprep = sem("simprep")
        gexp_s = sem("gexp_s")
        routes_d = sem("routes_d")
        zeroed = sem("zeroed")
        staged_s = sem("staged_s")
        put = [sem(f"put{j}") for j in range(RING)]
        taken = sem("taken")
        w_in = [sem(f"w_in{j}") for j in range(2)]
        rows_in_s = [sem(f"rows_in_s{j}") for j in range(2)]
        rT_ps = sem("rT_ps")
        rT_sb = sem("rT_sb")
        hid_ps = sem("hid_ps")
        hid_sb = sem("hid_sb")
        yrow_ps = sem("yrow_ps")
        yrow_sb = sem("yrow_sb")
        rows_out_s = [sem(f"rows_out_s{j}") for j in range(2)]
        fetch_idx = sem("fetch_idx")
        fetched_s = [sem(f"fetched_s{j}") for j in range(2)]
        merged = sem("merged")
        moe_n = sem("moe_n")
        squares_s = sem("squares_s")
        norm_s = sem("norm_s")
        x2_s = sem("x2_s")
        vdup_s = [sem(f"vdup_s{j}") for j in range(2)]
        g_in = sem("g_in")
        g_ex = sem("g_ex")
        rw_s = sem("rw_s")
        ewts = sem("ewts")
        xs_s = sem("xs_s")
        xsT_p = sem("xsT_p")
        xsT_s = sem("xsT_s")
        qkv_p = sem("qkv_p")
        qkv_s = sem("qkv_s")
        qkT_p = sem("qkT_p")
        qkT_s = sem("qkT_s")
        sc_p = sem("sc_p")
        sc_m = sem("sc_m")
        pr_e = sem("pr_e")
        pr_s = sem("pr_s")
        prT_p = sem("prT_p")
        prT_s = sem("prT_s")
        ao_p = sem("ao_p")
        ao_s = sem("ao_s")
        z_p = sem("z_p")
        z_s = sem("z_s")
        res_s = sem("res_s")
        res_out = [sem(f"res_out{j}") for j in range(2)]
        LOOPED = [*ctx_s, variances, roots, x_norm, xc_ps, xc_sb, proj, qx_w, kT_w, vx_w, scores, shifted, probs, pT_ps,
                  pT_sb, av, o_norm, oT_p, oT_s, y_p, y_s, h_norm, h_kept, hT_p, hT_s, lg_p, lg_s, top, top_kept,
                  searched, counted, staged_s, taken, *w_in, *rows_in_s, rT_ps, rT_sb, hid_ps, hid_sb, yrow_ps,
                  yrow_sb, *rows_out_s, fetch_idx, merged, moe_n, x2_s, squares_s, norm_s, *vdup_s, g_in, g_ex, rw_s, xs_s, xsT_p, xsT_s,
                  qkv_p, qkv_s, qkT_p, qkT_s, sc_p, sc_m, pr_e, pr_s, prT_p, prT_s, ao_p, ao_s, z_p, z_s, res_s,
                  *res_out]

        def number(k, off):
            return off if k is None else k * 2 + off

        def tile(a, k, off):
            if k is None:
                return a[:, off]
            half = a[:, :, :].rearrange("p (k j) d -> p k j d", j=2)
            return half[:, bass.ds(k + off // 2, 1), off % 2, :].rearrange("p o d -> p (o d)")

        def after(engine, semaphore, count):
            if not isinstance(count, int) or count > 0:
                engine.wait_ge(semaphore, count + C)

        def run_steps(engine, first, last, before, behind, step):
            lo = -before
            hi = T - 1 - behind
            hi -= (hi - lo + 1) % 2
            for s in range(first, lo):
                step(None, s)
            with engine.Fori(0, (hi - lo + 1) // 2) as k:
                for j in range(2):
                    step(k, lo + j)
            for s in range(hi + 1, last + 1):
                step(None, s)

        def bcast(v, n):
            return v.rearrange("(o n) -> o n", o=1).broadcast_to([P, n])

        LOADS = [
            (wq_sb[:, :], Wq), (wk_sb[:, :], Wk), (wv_sb[:, :], Wv), (wo_sb[:, :], Wo), (wr_sb[:, :], Wr),
            (bq_sb[:, :], bq.rearrange("(n o) -> n o", o=1)), (bk_sb[:, :], bk.rearrange("(n o) -> n o", o=1)),
            (bv_sb[:, 0, :], bcast(bv, DM)), (bv_sb[:, 1, :], bcast(bv, DM)), (bo_sb[:, :], bcast(bo, DM)),
            (br_sb[:, :], bcast(br, E0)), (gamma_sb[:, :], bcast(gamma, DM)), (beta_sb[:, :], bcast(beta, DM)),
            (sim_sb[:, :], sim_matrix), (sig[:, :], bcast(gates, E1)),
            (g_sb[:, 0:2], bcast(g_xattn, 2)), (g_sb[:, 2:4], bcast(g_ffn, 2)),
        ]
        block = stack.enter_context(nc.Block())

        @block.sync
        def _(sp):
            for s in LOOPED:
                sp.sem_inc(s, C)
            for dst, src in LOADS:
                sp.dma_start(dst, src).then_inc(loads, 16)
            sp.dma_start(xres[:, 0:4, :], x_d[:, 0:4, :]).then_inc(x_in, 16)

            def load_ctx(k, off):
                i = number(k, off)
                after(sp, xc_ps, i - 1)
                sp.dma_start(ctok[:, off % 2, :], tile(ctx_d, k, off)).then_inc(ctx_s[off % 2], 16)

            for i in range(2):
                load_ctx(None, i)
            sp.wait_ge(x_in, 16)
            sp.dma_start(xres[:, 4:T, :], x_d[:, 4:T, :]).then_inc(x_in, 16)
            with sp.Fori(0, T // 2 - 1) as k:
                for j in range(2):
                    load_ctx(k, 2 + j)
            sp.wait_ge(made, 2)
            for c in range(ROWS // P // 16):
                sp.dma_start(routed.rearrange("(p r) d -> p (r d)", p=P)[:, c * 2048:(c + 1) * 2048], zero1[:, :]).then_inc(zeroed, 16)
            for e3, w in enumerate((q_proj, k_proj, v_proj)):
                sp.dma_start(wqkv[:, :, e3 * DM:(e3 + 1) * DM], w.rearrange("e c h -> c e h")).then_inc(ewts, 16)
            sp.dma_start(wo1[:, :, :], o_proj.rearrange("e h c -> h e c")).then_inc(ewts, 16)
            for s in put:
                sp.wait_ge(s, 32 * T // RING)
            w1_d = W1.rearrange("(k j) c f -> k j c f", j=2)
            w2_d = W2.rearrange("(k j) (f p) c -> k j p f c", j=2, p=P)
            b1_d = b1.rearrange("(k j) (f p) -> k j p f", j=2, p=P)
            b2_d = b2.rearrange("(k j) (o c) -> k j o c", j=2, o=1)
            in_d = routed.rearrange("(k j m r p) d -> k j m p r d", j=2, m=XT, r=2, p=P)
            out_rows_d = expert_out.rearrange("(k j m r p) d -> k j m p r d", j=2, m=XT, r=2, p=P)

            def store_rows(k, t):
                sp.wait_ge(yrow_sb, k * (2 * XT) + t + 1 + C)
                sp.dma_start(out_rows_d[bass.ds(k, 1), t // XT, t % XT].rearrange("o p r d -> (o p) r d"),
                             rows_out[:, t % 2, :, :]).then_inc(rows_out_s[t % 2], 16)

            with sp.Fori(0, E0 // 2) as k:
                for j in range(2):
                    sp.wait_ge(yrow_ps, k * (2 * XT) + C)
                    one = bass.ds(k, 1)
                    sp.dma_start(w1_sb[:, j, :], w1_d[one, j].rearrange("o c f -> (o c) f")).then_inc(w_in[j], 16)
                    sp.dma_start(w2_sb[:, j, :, :], w2_d[one, j].rearrange("o p f c -> (o p) f c")).then_inc(w_in[j], 16)
                    with nc.allow_non_contiguous_dma(reason="one bias per partition"):
                        sp.dma_start(b1_sb[:, j, :], b1_d[one, j].rearrange("o p f -> (o p) f")).then_inc(w_in[j], 16)
                    sp.dma_start(b2_sb[:, j, :], b2_d[one, j].rearrange("o q c -> (o q) c").broadcast_to([P, DM])).then_inc(w_in[j], 16)
                    for m in range(XT):
                        t = j * XT + m
                        if t >= 2:
                            sp.wait_ge(rT_ps, k * (2 * XT) + t - 1 + C)
                        else:
                            sp.wait_ge(rT_ps, k * (2 * XT) + C)
                        sp.dma_start(rows_in[:, t % 2, :, :], in_d[one, j, m].rearrange("o p r d -> (o p) r d")).then_inc(rows_in_s[t % 2], 16)
                        if t >= 2:
                            store_rows(k, t - 2)
                store_rows(k, 2 * XT - 2)
                store_rows(k, 2 * XT - 1)
            for s in rows_out_s:
                sp.wait_ge(s, 16 * XT * (E0 // 2) + C)

            def load_ctx2(k, off):
                i = number(k, off)
                after(sp, xc_ps, T + i - 1)
                sp.dma_start(ctok[:, off % 2, :], tile(ctx_d, k, off)).then_inc(ctx_s[off % 2], 16)
                after(sp, vx_w, 2 * T + i * 2 - 2)
                half = ctxdup_d.rearrange("s (k j) b d -> s k j b d", j=2)[:, :, off % 2]
                src = half[:, off // 2] if k is None else half[:, bass.ds(k + off // 2, 1)].rearrange("s o b d -> s (o b) d")
                for h in range(2):
                    sp.dma_start(vdup[h * SEQ:(h + 1) * SEQ, off % 2, :, :], src).then_inc(vdup_s[off % 2], 16)

            with sp.Fori(0, T // 2) as k:
                for j in range(2):
                    load_ctx2(k, j)
            with sp.Fori(0, T // 2) as k:
                for j in range(2):
                    after(sp, res_s, number(k, j) + 1)
                    sp.dma_start(tile(out_d, k, j), result[:, j, :]).then_inc(res_out[j], 16)
            for s in res_out:
                sp.wait_ge(s, 16 * (T // 2) + C)

        @block.gpsimd
        def _(pool):
            steps = []

            def make(instruction):
                instruction.then_inc(made, 1)
                steps.append(1)
                pool.wait_ge(made, len(steps))
            make(pool.memset(ones[:, :], 1.0))
            make(pool.memset(zero1[:, :], 0.0))
            make(pool.memset(powr[:, :], -0.5))
            make(pool.affine_select(out=ident[:, :], in_=ones[:, :], pattern=[[-1, P]], compare_op=ALU.is_equal,
                                    fill=0.0, base=0, channel_multiplier=1))
            make(pool.affine_select(out=before[:, :], in_=ones[:, :], pattern=[[1, P]], compare_op=ALU.is_gt,
                                    fill=0.0, base=0, channel_multiplier=-1))
            make(pool.affine_select(out=causal[:, :], in_=zero1[:, 0:P], pattern=[[-1, P]], compare_op=ALU.is_ge,
                                    fill=NEG, base=0, channel_multiplier=1))
            make(pool.memset(causal[SEQ:P, 0:SEQ], NEG))
            for h in range(2):
                rows = slice(h * SEQ, (h + 1) * SEQ)
                make(pool.affine_select(out=band[rows, :], in_=zero1[rows, 0:SEQ], pattern=[[-1, SEQ]],
                                        compare_op=ALU.is_ge, fill=NEG, base=BAND, channel_multiplier=1))
                make(pool.affine_select(out=band[rows, :], in_=band[rows, :], pattern=[[1, SEQ]],
                                        compare_op=ALU.is_ge, fill=NEG, base=BAND, channel_multiplier=-1))
            make(pool.iota(iota8[:, :], pattern=[[1, E0]], base=0, channel_multiplier=0,
                           allow_small_or_imprecise_dtypes=True))
            make(pool.iota(iota16[:, :], pattern=[[1, E1]], base=0, channel_multiplier=0,
                           allow_small_or_imprecise_dtypes=True))
            make(pool.iota(caps[:, :], pattern=[[CAP, E0]], base=0, channel_multiplier=0,
                           allow_small_or_imprecise_dtypes=True))

            def step(k, off):
                n = number(k, off)
                after(pool, variances, n + 4)
                pool.tensor_tensor(root[:, 0:2], veps[:, 0:2], powr[:, 0:2], ALU.pow).then_inc(roots, 1)
                if k is not None or 0 <= off - 1 < T:
                    after(pool, h_norm, n)
                    pool.sem_inc(taken, 1)
                    pool.tensor_copy(tile(hres, k, off - 1), hn[:, :]).then_inc(h_kept, 1)
                if k is not None or 0 <= off - 2 < T:
                    after(pool, top, 2 * n - 2)
                    pool.sem_inc(taken, 1)
                    pool.tensor_copy(tile(topv, k, off - 2), mx8[:, 0:2]).then_inc(top_kept, 1)
                    pool.tensor_copy(tile(topi, k, off - 2), ix8[:, 0:2]).then_inc(top_kept, 1)

            run_steps(pool, -3, T + 1, -2, 3, step)
            pool.wait_ge(simprep, 2)
            pool.tensor_tensor(simsq[:, :], simsq[:, :], powr[:, 0:E1], ALU.pow).then_inc(simprep, 1)
            pool.wait_ge(zeroed, 16 * (ROWS // P // 16))
            with pool.Fori(0, T // RING) as k:
                for j in range(RING):
                    pool.wait_ge(staged_s, k * (2 * RING) + 2 * j + 2 + C)
                    pool.sem_inc(taken, 1)
                    for slot in range(2):
                        pool.indirect_dma_start(
                            out=routed, out_offset=bass.IndirectOffsetOnAxis(ap=staged_row[:, j, slot:slot + 1], axis=0),
                            in_=staged[:, j, :], in_offset=None, bounds_check=ROWS - 1, oob_is_err=False).then_inc(put[j], 16)
            for s in rows_out_s:
                pool.wait_ge(s, 16 * XT * (E0 // 2) + C)

            def fetch(k, off):
                i = number(k, off)
                after(pool, merged, i - 1)
                pool.sem_inc(taken, 1)
                pool.tensor_copy(fetch_row[:, off % 2, :], tile(get_row, k, off)).then_inc(fetch_idx, 1)
                after(pool, fetch_idx, i + 1)
                pool.sem_inc(taken, 1)
                for slot in range(2):
                    pool.indirect_dma_start(
                        out=fetched[:, off % 2, slot, :], out_offset=None, in_=expert_out,
                        in_offset=bass.IndirectOffsetOnAxis(ap=fetch_row[:, off % 2, slot:slot + 1], axis=0)).then_inc(fetched_s[off % 2], 16)

            def step(k, off):
                n = number(k, off)
                after(pool, variances, T + 5 + n + 5)
                pool.tensor_tensor(root[:, :], veps[:, :], powr[:, 0:3], ALU.pow).then_inc(roots, 1)
                if k is not None or 0 <= off + 4 < T:
                    xt = tile(xres, k, off + 4)
                    after(pool, moe_n, n + 5)
                    pool.sem_inc(taken, 1)
                    pool.tensor_tensor(moen[:, :], moen[:, :], tggamma[:, :], ALU.mult)
                    pool.tensor_tensor(xt, xt, tgbeta[:, :], ALU.add).then_inc(x2_s, 1)
                    after(pool, x2_s, 2 * n + 9)
                    pool.sem_inc(taken, 1)
                    pool.tensor_tensor(xt, xt, moen[:, :], ALU.add).then_inc(x2_s, 1)
                if k is not None or 0 <= off < T:
                    after(pool, squares_s, n + 1)
                    after(pool, lg_s, T + n)
                    pool.tensor_tensor(norm[:, :], squares[:, :], powr[:, 0:1], ALU.pow).then_inc(norm_s, 1)
                    after(pool, h_norm, T + n + 1)
                    pool.sem_inc(taken, 1)
                    pool.tensor_copy(tile(hres, k, off), hn[:, :]).then_inc(h_kept, 1)
                if k is not None or 0 <= off + 6 < T:
                    fetch(k, off + 6)

            for i in range(2):
                fetch(None, i)
            run_steps(pool, -4, T + 1, -2, 6, step)

        MADE = 14

        @block.vector
        def _(dve):
            dve.wait_ge(made, MADE)
            dve.wait_ge(loads, 16 * len(LOADS))
            dve.tensor_reduce(headmask4[:, :], ident[:, :].rearrange("p (g h d) -> p h g d", g=G, h=4),
                              AX.XY, ALU.add).then_inc(prep, 1)
            dve.wait_ge(prep, 1)
            for b in range(2):
                dve.tensor_copy(headmask[:, b, :, :], headmask4[:, :].unsqueeze(2).broadcast_to([P, 4, SEQ])).then_inc(prep, 1)
            dve.tensor_copy(ident_bf[:, :], ident[:, :]).then_inc(prep, 1)
            dve.tensor_copy(ones_bf[:, :], ones[:, :]).then_inc(prep, 1)
            dve.memset(vx[:, :, :, :, :, :, :], 0.0).then_inc(prep, 1)
            dve.wait_ge(prep, 6)
            for h in range(2):
                dve.memset(vx[h * SEQ:(h + 1) * SEQ, :, :, :, :, h, HD].rearrange("p u b g h -> p (u b g h)"), 1.0).then_inc(prep, 1)
            dve.wait_ge(tanhs, 1)
            dve.tensor_scalar(tgbo[:, :], bo_sb[:, :], tg[:, 0:1], None, ALU.mult).then_inc(prep, 1)
            dve.wait_ge(prep, 9)
            dve.tensor_copy(mx[:, 0:1], tg[:, 0:1]).then_inc(consts, 1)

            dve.memset(mv[:, :, :], 1.0)
            dve.memset(veps[:, :], 1.0)
            dve.drain()

            s4 = psS[:, :, 0:2 * P].rearrange("p g (a k) -> p g a k", k=SEQ)

            def shift_scores(done, i, buffer):
                after(dve, scores, done + i + 1)
                dve.tensor_reduce(mx[:, :].rearrange("p (g a) -> p g a", g=G), s4, AX.X, ALU.max)
                dve.drain()
                after(dve, pT_ps, 2 * (done + i) - 2)
                dve.tensor_tensor(es[:, buffer].rearrange("p g b (a k) -> p g (b a) k", k=SEQ), s4,
                                  mx[:, :].rearrange("p (g a) -> p g a", g=G).unsqueeze(3).broadcast_to([P, G, 4, SEQ]),
                                  ALU.subtract).then_inc(shifted, 1)

            def norm_heads():
                dve.reciprocal(rc[:, :], o_ps[:, :, HD])
                dve.drain()
                dve.tensor_tensor(osb[:, :, :], o_ps[:, :, 0:HD], rc[:, :].unsqueeze(2).broadcast_to([P, NH, HD]),
                                  ALU.mult).then_inc(o_norm, 1)

            def step(k, off):
                n = number(k, off)

                def has(lag):
                    return k is not None or 0 <= off + lag < T

                if has(1):
                    shift_scores(0, n + 1, (off + 1) % 2)
                if has(2):
                    after(dve, proj, n + 3)
                    after(dve, scores, n + 2)
                    for b in range(2):
                        q = psP[:, b * SEQ:(b + 1) * SEQ].unsqueeze(1).broadcast_to([P, 4, SEQ])
                        dve.scalar_tensor_tensor(qx[:, b, :, :], q, bq_sb[:, 0:1], headmask[:, b, :, :],
                                                 ALU.add, ALU.mult).then_inc(qx_w, 1)
                    dve.tensor_scalar(kT[:, :], psP[:, P:2 * P], bk_sb[:, 0:1], None, ALU.add).then_inc(kT_w, 1)
                if has(0):
                    after(dve, av, n + 1)
                if has(-1):
                    after(dve, y_p, n)
                if has(-2):
                    after(dve, lg_p, n - 1)
                if has(0):
                    after(dve, oT_p, n)
                    norm_heads()
                if has(-1):
                    dve.scalar_tensor_tensor(ytmp[:, :], y_ps, tg[:, 0:1], tgbo[:, :], ALU.mult, ALU.add).then_inc(y_s, 1)
                if has(-2):
                    after(dve, top_kept, 2 * n - 4)
                    dve.tensor_tensor(lg[:, :], psO[:, 400:400 + E0], br_sb[:, :], ALU.add).then_inc(lg_s, 1)
                if has(2):
                    for h in range(2):
                        rows = slice(h * SEQ, (h + 1) * SEQ)
                        v = psP[rows, 2 * P:4 * P].rearrange("p (b g j h d) -> p (b g) j h d", b=2, g=G, j=2, h=2)[:, :, h, :, :]
                        bvv = bv_sb[rows, :, :].rearrange("p b (g j h d) -> p (b g) j h d", g=G, j=2, h=2)[:, :, h, :, :]
                        dst = vx[rows, off % 2, :, :, :, h, 0:HD].rearrange("p b g h d -> p (b g) h d")
                        dve.tensor_tensor(dst, v, bvv, ALU.add).then_inc(vx_w, 1)
                dve.drain()
                if has(-1):
                    x1 = tile(xres, k, off - 1)
                    dve.tensor_tensor(x1, x1, ytmp[:, :], ALU.add)
                if has(3):
                    dve.bn_stats(stats[:, 0, :], tile(xres, k, off + 3))
                if has(-2):
                    dve.max(mx8[:, :], lg[:, :]).then_inc(top, 1)
                dve.drain()
                if has(-1):
                    dve.bn_stats(stats[:, 1, :], x1)
                if has(3):
                    dve.bn_aggr(mv[:, 0, :], stats[:, 0, :])
                if has(-2):
                    dve.max_index(ix8[:, :], mx8[:, :], lg[:, :]).then_inc(top, 1)
                dve.drain()
                if has(-1):
                    dve.bn_aggr(mv[:, 1, :], stats[:, 1, :])
                    dve.drain()
                dve.tensor_scalar(veps[:, 0:2], mv[:, 0:2, 1], EPS, None, ALU.add).then_inc(variances, 1)
                after(dve, roots, n + 4)
                if has(3):
                    after(dve, xc_ps, n + 3)
                    dve.tensor_scalar(xn[:, :], tile(xres, k, off + 3), mv[:, 0, 0:1], root[:, 0:1],
                                      ALU.subtract, ALU.mult).then_inc(x_norm, 1)
                if has(-1):
                    after(dve, hT_p, n - 1)
                    after(dve, h_kept, n - 1)
                    dve.tensor_scalar(hn[:, :], x1, mv[:, 1, 0:1], root[:, 1:2], ALU.subtract, ALU.mult).then_inc(h_norm, 1)
                if k is None and off == 0:
                    dve.wait_ge(x_in, 32)

            dve.wait_ge(x_in, 16)
            run_steps(dve, -3, T + 1, -2, 3, step)
            dve.tensor_tensor(simsq[:, :], sim_sb[:, :], sim_sb[:, :], ALU.mult).then_inc(simprep, 1)
            dve.wait_ge(counted, 1 + C)
            dve.tensor_scalar(simsq[:, :], psT[:, 0:E1], 1e-12, None, ALU.add).then_inc(simprep, 1)
            dve.wait_ge(simprep, 3)
            dve.tensor_tensor(simn[:, :], sim_sb[:, :], simsq[:, :], ALU.mult)
            dve.wait_ge(tanhs, 2)
            dve.tensor_scalar(sig[:, :], sig[:, :], 1.0, None, ALU.add)
            dve.drain()
            dve.reciprocal(sig[:, :], sig[:, :])
            dve.tensor_scalar(tggamma[:, :], gamma_sb[:, :], tg[:, 2:3], None, ALU.mult)
            dve.tensor_scalar(tgbeta[:, :], beta_sb[:, :], tg[:, 2:3], None, ALU.mult)
            dve.tensor_copy(band4[:, :, :], band[:, :].unsqueeze(1).broadcast_to([P, 4, SEQ]))
            dve.wait_ge(top_kept, 2 * T + C)
            dve.tensor_tensor(dist[:, :], topv[:, :, 0], topv[:, :, 1], ALU.subtract).then_inc(routes_d, 1)
            dve.memset(restart[:, :, :], 1.0)
            dve.memset(bit[:, :], 0)
            for slot, hot in enumerate((first, second)):
                dve.tensor_tensor(hot[:, :, :], topi[:, :, slot].unsqueeze(1).broadcast_to([P, E0, T]),
                                  iota8[:, :].unsqueeze(2).broadcast_to([P, E0, T]), ALU.is_equal)
            dve.drain()
            dve.memset(restart[:, :, 0], 0.0)
            dve.tensor_scalar(near[:, :], dist[:, :], SATURATED, None, ALU.min)
            dve.tensor_tensor(scratch[:, :, :], first[:, :, :], second[:, :, :], ALU.add)
            dve.drain()
            dve.tensor_tensor(key[:, :, :], first[:, :, :], near[:, :].unsqueeze(1).broadcast_to([P, E0, T]), ALU.mult)
            dve.tensor_tensor(rank[:, :, :], second[:, :, :], dist[:, :].unsqueeze(1).broadcast_to([P, E0, T]), ALU.mult)
            dve.tensor_scalar(scratch[:, :, :], scratch[:, :, :], -LOWEST, LOWEST, ALU.mult, ALU.add)
            dve.drain()
            dve.tensor_tensor(key[:, :, :], key[:, :, :], rank[:, :, :], ALU.subtract)
            dve.drain()
            dve.tensor_tensor(key[:, :, :], key[:, :, :], scratch[:, :, :], ALU.add)
            dve.memset(cand[:, :], 0)
            dve.drain()

            def count(op, against):
                dve.tensor_tensor(flags[:, :, :], key[:, :, :],
                                  against[:, :].bitcast(F32).unsqueeze(2).broadcast_to([P, E0, T]), op)
                dve.drain()
                with nc.allow_low_precision(reason="counts up to 64 are exact in bfloat16"):
                    dve.tensor_reduce(counts[:, :], flags[:, :, :], AX.X, ALU.add).then_inc(searched, 1)

            count(ALU.is_ge, cand)
            dve.wait_ge(counted, 2 + C)
            dve.tensor_scalar(accept[:, :], psP[:, 0:E0], float(CAP), -1.0, ALU.is_ge, ALU.mult)
            dve.memset(bit[:, :], 0x40000000)
            dve.drain()
            dve.tensor_scalar(thr[:, :], accept[:, :], -1, None, ALU.bitwise_xor)
            dve.drain()
            with dve.Fori(0, 31) as n:
                dve.tensor_tensor(cand[:, :], thr[:, :], bit[:, :], ALU.bitwise_xor)
                dve.drain()
                count(ALU.is_ge, cand)
                dve.wait_ge(counted, n + 3 + C)
                dve.tensor_scalar(accept[:, :], psP[:, 0:E0], float(CAP), -1.0, ALU.is_ge, ALU.mult)
                dve.drain()
                dve.tensor_tensor(accept[:, :], accept[:, :], bit[:, :], ALU.bitwise_and)
                dve.drain()
                dve.tensor_tensor(thr[:, :], thr[:, :], accept[:, :], ALU.bitwise_xor)
                dve.tensor_scalar(bit[:, :], bit[:, :], 1, None, ALU.logical_shift_right)
                dve.drain()
            count(ALU.is_gt, thr)
            dve.wait_ge(counted, 34 + C)
            dve.tensor_scalar(left[:, :], psP[:, 0:E0], -1.0, float(CAP), ALU.mult, ALU.add)
            dve.tensor_copy(keep[:, :, :], flags[:, :, :])
            dve.drain()
            dve.tensor_tensor(scratch[:, :, :], key[:, :, :], thr[:, :].bitcast(F32).unsqueeze(2).broadcast_to([P, E0, T]), ALU.is_equal)
            dve.tensor_scalar(rank[:, :, :], key[:, :, :], LOWEST, None, ALU.is_gt)
            dve.drain()
            dve.tensor_tensor(scratch[:, :, :], scratch[:, :, :], rank[:, :, :], ALU.mult)
            dve.drain()
            dve.tensor_copy(flags[:, :, :], scratch[:, :, :]).then_inc(searched, 1)

            def ranks(n):
                dve.wait_ge(counted, 35 + n + C)
                flat = rank[:, :, :].rearrange("p e t -> p (e t)")
                dve.tensor_tensor_scan(flat, restart[:, :, :].rearrange("p e t -> p (e t)"), psR[:, :], 0.0, ALU.mult, ALU.add)
                dve.drain()
                dve.tensor_tensor(flat, flat, psR[:, :], ALU.subtract)
                dve.drain()
                dve.tensor_tensor(flat, flat, psT[:, :], ALU.add)
                dve.drain()

            ranks(0)
            dve.tensor_tensor(rank[:, :, :], rank[:, :, :], left[:, :].unsqueeze(2).broadcast_to([P, E0, T]), ALU.is_lt)
            dve.drain()
            dve.tensor_tensor(rank[:, :, :], rank[:, :, :], scratch[:, :, :], ALU.mult)
            dve.drain()
            dve.tensor_tensor(keep[:, :, :], keep[:, :, :], rank[:, :, :], ALU.add)
            dve.drain()
            dve.tensor_copy(flags[:, :, :], keep[:, :, :]).then_inc(searched, 1)
            ranks(1)
            dve.tensor_tensor(rank[:, :, :], rank[:, :, :], caps[:, :].unsqueeze(2).broadcast_to([P, E0, T]), ALU.add)
            dve.wait_ge(gexp_s, 1)
            dve.tensor_scalar(gexp[:, 0, :], gexp[:, 1, :], 1.0, None, ALU.add)
            dve.drain()
            dve.reciprocal(gexp[:, 0, :], gexp[:, 0, :])
            dve.drain()
            dve.tensor_tensor(gexp[:, 1, :], gexp[:, 1, :], gexp[:, 0, :], ALU.mult)
            for slot, hot in enumerate((first, second)):
                dve.tensor_tensor(scratch[:, :, :], hot[:, :, :], keep[:, :, :], ALU.mult)
                dve.drain()
                dve.tensor_reduce(kept[:, slot, :], scratch[:, :, :].rearrange("p e t -> p t e"), AX.X, ALU.add)
                dve.drain()
                dve.tensor_tensor(scratch[:, :, :], scratch[:, :, :], rank[:, :, :], ALU.mult)
                dve.drain()
                dve.tensor_reduce(rowf[:, slot, :], scratch[:, :, :].rearrange("p e t -> p t e"), AX.X, ALU.add)
                dve.drain()
                dve.tensor_tensor(gate[:, :, slot], gexp[:, slot, :], kept[:, slot, :], ALU.mult)
                dve.tensor_copy(get_row[:, :, slot], rowf[:, slot, :])
                dve.tensor_scalar(near[:, :], kept[:, slot, :], -float(SKIP), float(SKIP), ALU.mult, ALU.add)
                dve.drain()
                dve.tensor_tensor(put_row[:, :, slot], rowf[:, slot, :], near[:, :], ALU.add)
                dve.drain()
            def stage(k, j):
                if k is None:
                    h, r = hres[:, j, :], put_row[:, j, :]
                else:
                    dve.wait_ge(put[j], k * 32)
                    h = hres[:, :, :].rearrange("p (k j) d -> p k j d", j=RING)[:, bass.ds(k, 1), j, :].rearrange("p o d -> p (o d)")
                    r = put_row[:, :, :].rearrange("p (k j) d -> p k j d", j=RING)[:, bass.ds(k, 1), j, :].rearrange("p o d -> p (o d)")
                dve.tensor_copy(staged[:, j, :], h).then_inc(staged_s, 1)
                dve.tensor_copy(staged_row[:, j, :], r).then_inc(staged_s, 1)

            for j in range(RING):
                stage(None, j)
            with dve.Fori(1, T // RING) as k:
                for j in range(RING):
                    stage(k, j)
            yb = (psR, psO)
            tb = (psT, psP)

            def add_bias(k, t):
                n = k * (2 * XT) + t
                dve.wait_ge(yrow_ps, n + 1 + C)
                dve.wait_ge(rows_out_s[t % 2], k * (16 * XT) + 16 * (t // 2) + C)
                dve.tensor_tensor(rows_out[:, t % 2, :, :], yb[t % 2][:, 0:2 * P].rearrange("p (r d) -> p r d", r=2),
                                  b2_sb[:, t // XT, :].unsqueeze(1).broadcast_to([P, 2, DM]), ALU.add).then_inc(yrow_sb, 1)

            with dve.Fori(0, E0 // 2) as k:
                for t in range(2 * XT):
                    n = k * (2 * XT) + t
                    dve.wait_ge(rT_ps, n + 1 + C)
                    if t >= 2:
                        dve.wait_ge(hid_ps, n - 1 + C)
                    else:
                        dve.wait_ge(hid_ps, k * (2 * XT) + C)
                    dve.tensor_copy(rowsT[:, t % 2, :], tb[t % 2][:, 0:2 * P]).then_inc(rT_sb, 1)
                    if t % XT == 0:
                        dve.wait_ge(w_in[t // XT], k * 64 + 64 + C)
                    if t >= 1:
                        add_bias(k, t - 1)
                add_bias(k, 2 * XT - 1)
            def step(k, off):
                n = number(k, off)

                def has(lag):
                    return k is not None or 0 <= off + lag < T

                if has(4):
                    gt = tile(gate, k, off + 4)
                    dve.wait_ge(fetched_s[off % 2], (n + 4 - off % 2) * 16 + 32)
                    dve.scalar_tensor_tensor(moe[:, :], fetched[:, off % 2, 0, :], gt[:, 0:1], tile(hres, k, off + 4), ALU.mult, ALU.add)
                if has(1):
                    shift_scores(T, n + 1, (off + 1) % 2)
                else:
                    dve.drain()
                if has(4):
                    dve.scalar_tensor_tensor(moe2[:, :], fetched[:, off % 2, 1, :], gt[:, 1:2], moe[:, :], ALU.mult, ALU.add).then_inc(merged, 1)
                if has(2):
                    after(dve, xc_ps, T + n + 3)
                    after(dve, scores, T + n + 2)
                    if has(3):
                        after(dve, x2_s, 2 * n + 8)
                    for b in range(2):
                        q = psP[:, b * SEQ:(b + 1) * SEQ].unsqueeze(1).broadcast_to([P, 4, SEQ])
                        dve.tensor_tensor(qx[:, b, :, :], q, headmask[:, b, :, :], ALU.mult).then_inc(qx_w, 1)
                if has(3) and not has(2):
                    after(dve, x2_s, 2 * n + 8)
                dve.drain()
                if has(3):
                    dve.bn_stats(stats[:, 1, :], tile(xres, k, off + 3))
                if has(4):
                    dve.bn_stats(stats[:, 0, :], moe2[:, :])
                if has(0):
                    after(dve, av, T + n + 1)
                if has(-1):
                    after(dve, lg_p, T + n)
                    after(dve, norm_s, n)
                if has(0):
                    norm_heads()
                    x3 = tile(xres, k, off)
                if has(-1):
                    dve.scalar_tensor_tensor(lgr[:, :], lg_ps, norm[:, 0:1], sig[:, :], ALU.mult, ALU.subtract).then_inc(lg_s, 1)
                dve.drain()
                if has(0):
                    dve.scalar_tensor_tensor(x3, osb[:, :, :].rearrange("p h d -> p (h d)"), tg[:, 1:2], x3, ALU.mult, ALU.add)
                if has(-1):
                    dve.max(mx8[:, :], lgr[:, :])
                    dve.tensor_scalar(relu[:, :], lgr[:, :], 0.0, None, ALU.max)
                    dve.tensor_scalar(active[:, :], lgr[:, :], 0.0, None, ALU.is_gt)
                dve.drain()
                if has(0):
                    dve.bn_stats(stats[:, 2, :], x3)
                if has(-1):
                    dve.max_index(ix8[:, :], mx8[:, :], lgr[:, :])
                    dve.tensor_scalar(nomax[:, :], mx8[:, 0:1], 0.0, -1.0, ALU.max, ALU.mult).then_inc(g_in, 1)
                    dve.tensor_scalar(idle[:, :], mx8[:, 0:1], 0.0, None, ALU.is_le)
                dve.drain()
                if has(0):
                    dve.bn_aggr(mv[:, 2, :], stats[:, 2, :])
                if has(3):
                    dve.bn_aggr(mv[:, 1, :], stats[:, 1, :])
                if has(4):
                    dve.bn_aggr(mv[:, 0, :], stats[:, 0, :])
                if has(-1):
                    dve.tensor_copy(ixf[:, :], ix8[:, 0:2])
                dve.drain()
                dve.tensor_scalar(veps[:, 0:3], mv[:, :, 1], EPS, None, ALU.add).then_inc(variances, 1)
                if has(-1):
                    dve.tensor_scalar(oneh[:, :], iota16[:, :], ixf[:, 0:1], None, ALU.is_equal)
                    dve.drain()
                    dve.scalar_tensor_tensor(oneh2[:, :], iota16[:, :], ixf[:, 1:2], oneh[:, :], ALU.is_equal, ALU.add)
                    dve.drain()
                    dve.scalar_tensor_tensor(oneh[:, :], oneh2[:, :], idle[:, 0:1], active[:, :], ALU.mult, ALU.add)
                    dve.drain()
                    after(dve, g_ex, n)
                    dve.tensor_tensor_reduce(gpr[:, :], gex[:, :], oneh[:, :], 1.0, 0.0, ALU.mult, ALU.add, gsum[:, :])
                after(dve, roots, T + 5 + n + 5)
                if has(4):
                    after(dve, x2_s, 2 * n + 8)
                    dve.tensor_scalar(moen[:, :], moe2[:, :], mv[:, 0, 0:1], root[:, 0:1], ALU.subtract, ALU.mult).then_inc(moe_n, 1)
                if has(0):
                    after(dve, hT_p, T + n)
                    after(dve, h_kept, T + n)
                    dve.tensor_scalar(hn[:, :], x3, mv[:, 2, 0:1], root[:, 2:3], ALU.subtract, ALU.mult).then_inc(h_norm, 1)
                if has(3):
                    after(dve, xc_ps, T + n + 3)
                    dve.tensor_scalar(xn[:, :], tile(xres, k, off + 3), mv[:, 1, 0:1], root[:, 1:2],
                                      ALU.subtract, ALU.mult).then_inc(x_norm, 1)
                dve.drain()
                if has(-1):
                    dve.reciprocal(grec[:, :], gsum[:, :])
                if has(0):
                    dve.tensor_tensor_reduce(hsq[:, :], hn[:, :], hn[:, :], 1.0, 1e-12, ALU.mult, ALU.add, squares[:, 0:1]).then_inc(squares_s, 1)
                dve.drain()
                if has(-1):
                    dve.tensor_scalar(tile(rw, k, off - 1), gpr[:, :], grec[:, 0:1], None, ALU.mult).then_inc(rw_s, 1)

            run_steps(dve, -4, T + 1, -2, 6, step)

            def weigh(k, off):
                i = number(k, off)
                after(dve, xsT_p, i * 4)
                dve.tensor_tensor(xs[:, :, :], tile(hres, k, off).unsqueeze(1).broadcast_to([P, E1, DM]),
                                  tile(rw, k, off).unsqueeze(2).broadcast_to([P, E1, DM]), ALU.mult).then_inc(xs_s, 1)

            def combine(k, off):
                i = number(k, off)
                rwi = tile(rw, k, off)
                for c in range(4):
                    after(dve, z_p, i * 4 + c + 1)
                    dve.tensor_tensor(z[:, 4 * c:4 * c + 4, :], zb[c % 3][:, :].rearrange("p (e d) -> p e d", e=4),
                                      rwi[:, 4 * c:4 * c + 4].unsqueeze(2).broadcast_to([P, 4, DM]), ALU.mult).then_inc(z_s, 1)
                dve.drain()
                dve.tensor_reduce(zsum[:, :], z[:, :, :].rearrange("p e d -> p d e"), AX.X, ALU.add)
                dve.drain()
                dve.wait_ge(res_out[off % 2], (i - off % 2) * 8 + C)
                dve.scalar_tensor_tensor(result[:, off % 2, :], zsum[:, :], tg[:, 3:4], tile(xres, k, off),
                                         ALU.mult, ALU.add).then_inc(res_s, 1)

            def step(k, off):
                n = number(k, off)

                def has(lag):
                    return k is not None or 0 <= off + lag < T

                if has(-1):
                    after(dve, sc_p, n)
                    after(dve, pr_e, n - 1)
                    dve.scalar_tensor_tensor(sc[:, :], psT[:, 2 * P:3 * P], float(DM) ** -0.5, causal[:, :], ALU.mult, ALU.add)
                    dve.drain()
                    dve.tensor_reduce(scmax[:, :], sc[:, :], AX.X, ALU.max, negate=True).then_inc(sc_m, 1)
                if has(1):
                    weigh(k, off + 1)
                if has(-1):
                    after(dve, pr_e, n)
                    dve.reciprocal(screc[:, :], scsum[:, :])
                    dve.drain()
                    after(dve, prT_p, n - 1)
                    dve.tensor_scalar(prn[:, :], pr[:, :], screc[:, 0:1], None, ALU.mult).then_inc(pr_s, 1)
                if has(0):
                    after(dve, qkv_p, n + 1)
                    after(dve, ao_p, n - 1)
                    after(dve, qkT_p, n)
                    dve.tensor_copy(qkv[:, off % 2, :], pq[off % 2][:, 0:3 * DM]).then_inc(qkv_s, 1)
                if has(-1):
                    combine(k, off - 1)

            run_steps(dve, -1, T + 1, -2, 1, step)

        @block.scalar
        def _(act):
            act.wait_ge(loads, 16 * len(LOADS))
            act.activation(tg[:, :], g_sb[:, :], ACT.Tanh).then_inc(tanhs, 1)
            act.activation(sig[:, :], sig[:, :], ACT.Exp, scale=-1.0).then_inc(tanhs, 1)
            act.wait_ge(consts, 1)

            def evacuate_probs(done, i):
                for b in range(2):
                    after(act, pT_ps, 2 * (done + i) + b + 1)
                    after(act, av, done + i)
                    act.copy(pT[:, b].rearrange("p g k -> p (g k)"), psR[:, :]).then_inc(pT_sb, 1)

            def exponentials(done, i, buffer):
                after(act, shifted, done + i + 1)
                e = es[:, buffer].rearrange("p g b k -> p (g b k)")
                act.activation(e, e, ACT.Exp, scale=SCALE).then_inc(probs, 1)

            def step(k, off):
                n = number(k, off)

                def has(lag):
                    return k is not None or 0 <= off + lag < T

                if has(2):
                    after(act, xc_ps, n + 3)
                if has(-1):
                    after(act, oT_p, n)
                if has(-2):
                    after(act, hT_p, n - 1)
                if has(2):
                    after(act, proj, n + 2)
                    act.copy(xT[:, :], psT[:, 0:P]).then_inc(xc_sb, 1)
                    act.copy(cT[:, :, :, :], psT[:, P:2 * P].rearrange("p (b k) -> p b k", b=2).unsqueeze(2)
                             .broadcast_to([P, 2, 2, SEQ])).then_inc(xc_sb, 1)
                if has(0):
                    evacuate_probs(0, n)
                if has(-1):
                    after(act, y_p, n - 1)
                    act.copy(oT[:, :], psT[:, 2 * P:3 * P]).then_inc(oT_s, 1)
                if has(-2):
                    after(act, lg_p, n - 2)
                    act.copy(hT[:, :], psT[:, 3 * P:4 * P]).then_inc(hT_s, 1)
                if has(1):
                    exponentials(0, n + 1, (off + 1) % 2)

            run_steps(act, -3, T + 1, -2, 3, step)
            act.wait_ge(routes_d, 1)
            act.activation(gexp[:, 1, :], dist[:, :], ACT.Exp, scale=-1.0).then_inc(gexp_s, 1)
            with act.Fori(0, E0 // 2) as k:
                for t in range(2 * XT):
                    j = t // XT
                    n = k * (2 * XT) + t
                    if t % XT == 0:
                        act.wait_ge(w_in[j], k * 64 + 64 + C)
                    act.wait_ge(hid_ps, n + 1 + C)
                    if t >= 2:
                        act.wait_ge(yrow_ps, n - 1 + C)
                    else:
                        act.wait_ge(yrow_ps, k * (2 * XT) + C)
                    for f in range(FB):
                        m = act.activation(hidT[:, t % 2, f, :], psS[:, 2 * (t % 2) + f // 2, (f % 2) * 256:(f % 2) * 256 + 256],
                                           ACT.Gelu, bias=b1_sb[:, j, f:f + 1])
                    m.then_inc(hid_sb, 1)
            def step(k, off):
                n = number(k, off)

                def has(lag):
                    return k is not None or 0 <= off + lag < T

                if has(2):
                    after(act, xc_ps, T + n + 3)
                if has(-1):
                    after(act, hT_p, T + n)
                if has(2):
                    after(act, scores, T + n + 2)
                    act.copy(kT[:, :], psT[:, 0:P]).then_inc(kT_w, 1)
                if has(0):
                    evacuate_probs(T, n)
                if has(-1):
                    after(act, lg_p, T + n - 1)
                    act.copy(hT[:, :], psT[:, 3 * P:4 * P]).then_inc(hT_s, 1)
                if has(1):
                    exponentials(T, n + 1, (off + 1) % 2)
                if has(-1):
                    after(act, g_in, n)
                    act.activation(gex[:, :], relu[:, :], ACT.Exp, bias=nomax[:, 0:1]).then_inc(g_ex, 1)
                if has(2):
                    act.wait_ge(vdup_s[off % 2], (n + 2 - off % 2) * 16 + 32 + C)
                    after(act, av, T + n + 1)
                    for h in range(2):
                        rows = slice(h * SEQ, (h + 1) * SEQ)
                        v = vdup[rows, off % 2, :, :].rearrange("p b (g j h d) -> p (b g) j h d", g=G, j=2, h=2)[:, :, h, :, :]
                        dst = vx[rows, off % 2, :, :, :, h, 0:HD].rearrange("p b g h d -> p (b g) h d")
                        act.copy(dst, v).then_inc(vx_w, 1)

            run_steps(act, -4, T + 1, -2, 6, step)

            def evacuate_shares(n, buffer, c):
                after(act, xsT_p, n * 4 + c + 1)
                after(act, qkv_p, n - 1)
                act.copy(xsT[:, buffer, 4 * c:4 * c + 4, :].rearrange("p e t -> p (e t)"), psS[:, c % 2, :]).then_inc(xsT_s, 1)

            def step(k, off):
                n = number(k, off)

                def has(lag):
                    return k is not None or 0 <= off + lag < T

                if has(-1):
                    after(act, qkT_p, n)
                    act.copy(qkT[:, :], psT[:, 0:2 * P]).then_inc(qkT_s, 1)
                    after(act, sc_m, n)
                    after(act, pr_s, n - 1)
                    act.activation(pr[:, :], sc[:, :], ACT.Exp, bias=scmax[:, 0:1], accum_out=scsum[:, :]).then_inc(pr_e, 1)
                if has(1):
                    for c in range(2):
                        evacuate_shares(n + 1, (off + 1) % 2, c)
                if has(-1):
                    after(act, prT_p, n)
                    after(act, ao_p, n - 1)
                    act.copy(prT[:, :], psT[:, 3 * P:4 * P]).then_inc(prT_s, 1)
                if has(1):
                    evacuate_shares(n + 1, (off + 1) % 2, 2)
                if has(-1):
                    after(act, ao_p, n)
                    after(act, z_p, 4 * n - 4)
                    act.copy(aoT[:, :], psT[:, 0:P]).then_inc(ao_s, 1)
                if has(1):
                    evacuate_shares(n + 1, (off + 1) % 2, 3)

            run_steps(act, -1, T + 1, -2, 1, step)

        @block.tensor
        def _(pe):
            pe.wait_ge(consts, 1)

            def score_products(start):
                for b in range(2):
                    for hj in range(2):
                        for g in range(G):
                            rows = slice(32 * g, 32 * g + 32)
                            m = pe.matmul(psS[:, g, (2 * b + hj) * SEQ:(2 * b + hj + 1) * SEQ],
                                          qx[rows, b, 2 * hj:2 * hj + 2, :], kT[rows, b * SEQ:(b + 1) * SEQ],
                                          start=start, stop=True, skip_group_check=not start)
                m.then_inc(scores, 1)

            def turn_probs(done, i, buffer, b):
                after(pe, probs, done + i + 1)
                after(pe, pT_sb, 2 * (done + i) + b)
                for g in range(G):
                    m = pe.transpose(psR[:, g * P:(g + 1) * P], es[:, buffer, g, b, :], ident[:, :])
                m.then_inc(pT_ps, 1)

            def value_products(buffer):
                for b in range(2):
                    for g in range(G):
                        for h in range(2):
                            head = 4 * g + h
                            m = pe.matmul(o_ps[b * SEQ:(b + 1) * SEQ, head:head + 3:2, :],
                                          pT[:, b, g, h * SEQ:(h + 1) * SEQ], vx[:, buffer, b, g, h, :, :],
                                          start=True, stop=True)
                m.then_inc(av, 1)

            def step(k, off):
                n = number(k, off)

                def has(lag):
                    return k is not None or 0 <= off + lag < T

                if has(1):
                    after(pe, qx_w, 2 * n + 4)
                    after(pe, kT_w, n + 2)
                    after(pe, shifted, n + 1)
                    score_products(True)
                after(pe, xc_sb, min(2 * T, 2 * n + 4) if k is None else 2 * n + 4)
                after(pe, oT_s, n - 1)
                after(pe, hT_s, n - 2)
                if has(2):
                    after(pe, x_norm, n + 3)
                    pe.transpose(psT[:, 0:P], xn[:, :], ident[:, :])
                    pe.wait_ge(ctx_s[off % 2], (n + 2 - off % 2) * 8 + 16 + C)
                    pe.transpose(psT[:, P:2 * P], ctok[:, off % 2, :], ident[:, :]).then_inc(xc_ps, 1)
                if has(-1):
                    after(pe, o_norm, n)
                    pe.transpose(psT[:, 2 * P:3 * P], osb[:, :, :].rearrange("p h d -> p (h d)"), ident[:, :]).then_inc(oT_p, 1)
                if has(-2):
                    after(pe, h_norm, n - 1)
                    pe.transpose(psT[:, 3 * P:4 * P], hn[:, :], ident[:, :]).then_inc(hT_p, 1)
                if has(0):
                    turn_probs(0, n, off % 2, 0)
                if has(2):
                    after(pe, xc_sb, 2 * n + 6)
                    after(pe, qx_w, 2 * n + 4)
                    after(pe, kT_w, n + 2)
                    after(pe, vx_w, 2 * n + 4)
                    pe.matmul(psP[:, 0:P], wq_sb[:, :], xT[:, :], start=True, stop=True)
                    pe.matmul(psP[:, P:2 * P], wk_sb[:, :], cT[:, :, 0, :], start=True, stop=True)
                    for b in range(2):
                        m = pe.matmul(psP[:, (2 + b) * P:(3 + b) * P], cT[:, b, :, :], wv_sb[:, :], start=True, stop=True)
                    m.then_inc(proj, 1)
                if has(0):
                    turn_probs(0, n, off % 2, 1)
                after(pe, o_norm, min(T, n) if k is None else n)
                after(pe, y_s, n - 1)
                after(pe, lg_s, n - 2)
                if has(-1):
                    after(pe, oT_s, n)
                    pe.matmul(y_ps, oT[:, :], wo_sb[:, :], start=True, stop=True).then_inc(y_p, 1)
                if has(-2):
                    after(pe, hT_s, n - 1)
                    pe.matmul(psO[:, 400:400 + E0], hT[:, :], wr_sb[:, :], start=True, stop=True).then_inc(lg_p, 1)
                if has(0):
                    after(pe, pT_sb, 2 * n + 2)
                    after(pe, vx_w, 2 * n + 2)
                    value_products(off % 2)

            run_steps(pe, -3, T + 1, -2, 3, step)
            pe.wait_ge(simprep, 1)
            pe.matmul(psT[:, 0:E1], ones[:, :], simsq[:, :], start=True, stop=True).then_inc(counted, 1)
            with pe.Fori(0, 32) as n:
                pe.wait_ge(searched, n + 1 + C)
                pe.matmul(psP[:, 0:E0], ones_bf[:, :], counts[:, :], start=True, stop=True).then_inc(counted, 1)
            pe.wait_ge(searched, 33 + C)
            pe.matmul(psP[:, 0:E0], ones_bf[:, :], counts[:, :], start=True, stop=True).then_inc(counted, 1)
            for r in range(2):
                pe.wait_ge(searched, 34 + r + C)
                f = flags[:, :, :].rearrange("p e t -> p (e t)")
                pe.matmul(psT[:, :], before[:, :], f, start=True, stop=True)
                pe.matmul(psR[:, :], ones_bf[:, :], f, start=True, stop=True).then_inc(counted, 1)
            yb = (psR, psO)
            tb = (psT, psP)

            def expert_out_rows(k, t):
                n = k * (2 * XT) + t
                pe.wait_ge(hid_sb, n + 1 + C)
                if t >= 2:
                    pe.wait_ge(yrow_sb, n - 1 + C)
                else:
                    pe.wait_ge(yrow_sb, k * (2 * XT) + C)
                for r in range(2):
                    for f in range(FB):
                        m = pe.matmul(yb[t % 2][:, r * P:(r + 1) * P], hidT[:, t % 2, f, r * P:(r + 1) * P],
                                      w2_sb[:, t // XT, f, :], start=(f == 0), stop=(f == FB - 1))
                m.then_inc(yrow_ps, 1)

            with pe.Fori(0, E0 // 2) as k:
                for t in range(2 * XT):
                    n = k * (2 * XT) + t
                    if t >= 2:
                        pe.wait_ge(rT_sb, n - 1 + C)
                    else:
                        pe.wait_ge(rT_sb, k * (2 * XT) + C)
                    pe.wait_ge(rows_in_s[t % 2], k * (16 * XT) + 16 * (t // 2) + 16 + C)
                    for r in range(2):
                        m = pe.transpose(tb[t % 2][:, r * P:(r + 1) * P], rows_in[:, t % 2, r, :], ident[:, :])
                    m.then_inc(rT_ps, 1)
                    if t % XT == 0:
                        pe.wait_ge(w_in[t // XT], k * 64 + 64 + C)
                    pe.wait_ge(rT_sb, n + 1 + C)
                    if t >= 2:
                        pe.wait_ge(hid_sb, n - 1 + C)
                    else:
                        pe.wait_ge(hid_sb, k * (2 * XT) + C)
                    for f in range(FB):
                        m = pe.matmul(psS[:, 2 * (t % 2) + f // 2, (f % 2) * 256:(f % 2) * 256 + 256],
                                      w1_sb[:, t // XT, f * P:(f + 1) * P], rowsT[:, t % 2, :], start=True, stop=True)
                    m.then_inc(hid_ps, 1)
                    if t >= 1:
                        expert_out_rows(k, t - 1)
                expert_out_rows(k, 2 * XT - 1)
            def step(k, off):
                n = number(k, off)

                def has(lag):
                    return k is not None or 0 <= off + lag < T

                if has(1):
                    after(pe, qx_w, 2 * T + 2 * n + 4)
                    after(pe, kT_w, T + n + 2)
                    after(pe, shifted, T + n + 1)
                    for g in range(G):
                        pe.matmul(psS[:, g, 0:2 * P], ident_bf[:, :], band4[:, :, :], start=True, stop=True, skip_group_check=True)
                    score_products(False)
                after(pe, kT_w, min(2 * T, T + n + 2) if k is None else T + n + 2)
                after(pe, hT_s, T + n - 1)
                if has(2):
                    pe.wait_ge(ctx_s[off % 2], 8 * T + (n + 2 - off % 2) * 8 + 16 + C)
                    pe.transpose(psT[:, 0:P], ctok[:, off % 2, :], ident[:, :])
                    after(pe, x_norm, T + n + 3)
                    after(pe, qx_w, 2 * T + 2 * n + 4)
                    pe.transpose(psP[:, 0:P], xn[:, :], ident[:, :]).then_inc(xc_ps, 1)
                if has(-1):
                    after(pe, h_norm, T + n)
                    pe.transpose(psT[:, 3 * P:4 * P], hn[:, :], ident[:, :]).then_inc(hT_p, 1)
                if has(0):
                    turn_probs(T, n, off % 2, 0)
                    turn_probs(T, n, off % 2, 1)
                after(pe, o_norm, min(2 * T, T + n) if k is None else T + n)
                after(pe, lg_s, T + n - 1)
                if has(-1):
                    after(pe, hT_s, T + n)
                    pe.matmul(lg_ps, hT[:, :], simn[:, :], start=True, stop=True).then_inc(lg_p, 1)
                if has(0):
                    after(pe, pT_sb, 2 * T + 2 * n + 2)
                    after(pe, vx_w, 2 * T + 2 * n + 2)
                    value_products(off % 2)

            run_steps(pe, -4, T + 1, -2, 6, step)

            def turn_shares(n, c):
                after(pe, xs_s, n + 1)
                after(pe, xsT_s, n * 4 + c - 1)
                for e in range(4 * c, 4 * c + 4):
                    m = pe.transpose(psS[:, c % 2, (e % 4) * P:(e % 4 + 1) * P], xs[:, e, :], ident[:, :])
                m.then_inc(xsT_p, 1)

            def project(n, buffer, c):
                if c == 0:
                    after(pe, qkv_s, n - 1)
                after(pe, xsT_s, n * 4 + c + 1)
                for e in range(4 * c, 4 * c + 4):
                    m = pe.matmul(pq[buffer][:, 0:3 * DM], xsT[:, buffer, e, :], wqkv[:, e, :], start=(e == 0), stop=(e == E1 - 1))
                if c == 3:
                    m.then_inc(qkv_p, 1)

            def out_products(n, c):
                after(pe, ao_s, n + 1)
                if c % 3 == 0:
                    after(pe, z_s, n * 4 + c // 3)
                pe.matmul(zb[c % 3][:, :], aoT[:, :], wo1[:, 4 * c:4 * c + 4, :], start=True, stop=True).then_inc(z_p, 1)

            def step(k, off):
                n = number(k, off)
                b = off % 2
                o = 1 - b

                def has(lag):
                    return k is not None or 0 <= off + lag < T

                if has(-1):
                    after(pe, qkv_s, n)
                    after(pe, ao_s, n - 1)
                    after(pe, prT_s, n - 1)
                    pe.transpose(psT[:, 0:P], qkv[:, o, 0:P], ident[:, :])
                    pe.transpose(psT[:, P:2 * P], qkv[:, o, P:2 * P], ident[:, :]).then_inc(qkT_p, 1)
                if has(0):
                    project(n, b, 0)
                if has(-1):
                    after(pe, qkT_s, n)
                    pe.matmul(psT[:, 2 * P:3 * P], qkT[:, 0:P], qkT[:, P:2 * P], start=True, stop=True).then_inc(sc_p, 1)
                if has(0):
                    project(n, b, 1)
                if has(1):
                    turn_shares(n + 1, 0)
                    turn_shares(n + 1, 1)
                if has(-1):
                    after(pe, pr_s, n)
                    pe.transpose(psT[:, 3 * P:4 * P], prn[:, :], ident[:, :]).then_inc(prT_p, 1)
                if has(0):
                    project(n, b, 2)
                if has(1):
                    turn_shares(n + 1, 2)
                if has(-1):
                    after(pe, prT_s, n)
                    pe.matmul(psT[:, 0:P], qkv[:, o, 2 * P:3 * P], prT[:, :], start=True, stop=True).then_inc(ao_p, 1)
                if has(0):
                    project(n, b, 3)
                if has(1):
                    turn_shares(n + 1, 3)
                if has(-1):
                    for c in range(4):
                        out_products(n - 1, c)

            pe.wait_ge(ewts, 64)
            run_steps(pe, -1, T + 1, -2, 1, step)


_INS = ['x', 'ctx_1024', 'g_xattn', 'g_ffn', 'L0_xattn_Wq', 'L0_xattn_bq', 'L0_xattn_Wk', 'L0_xattn_bk', 'L0_xattn_Wv',
        'L0_xattn_bv', 'L0_xattn_Wo', 'L0_xattn_bo', 'L0_ffn_Wr', 'L0_ffn_br', 'L0_ffn_W1', 'L0_ffn_b1', 'L0_ffn_W2',
        'L0_ffn_b2', 'L0_ffn_gamma', 'L0_ffn_beta', 'L0_ffn_token_mask', 'L1_ffn_sim_matrix', 'L1_ffn_gates',
        'L1_ffn_q_proj', 'L1_ffn_k_proj', 'L1_ffn_v_proj', 'L1_ffn_o_proj']
_OUTS = [((128, 64, 128), 'float32')]


def kernel(**inputs):
    import numpy as _np
    import concourse.bacc as _bacc
    from concourse import mybir as _mybir
    from concourse.bass_utils import run_bass_kernel_spmd as _run

    nc = _bacc.Bacc("TRN2", target_bir_lowering=False, num_devices=1)
    arrays, args = {}, []
    for name in _INS:
        a = _np.ascontiguousarray(inputs[name])
        arrays[f"in_{name}_dram"] = a
        args.append(nc.dram_tensor(f"in_{name}_dram", a.shape, _mybir.dt.from_np(a.dtype), kind="ExternalInput").ap())
    for i, (shape, dtype) in enumerate(_OUTS):
        dt = _mybir.dt.from_np(_np.dtype(dtype))
        args.append(nc.dram_tensor(f"out_{i}_dram", shape, dt, kind="ExternalOutput").ap())
    build(nc, *args)
    r = _run(nc, [arrays], core_ids=[0])
    got = tuple(r.results[0][f"out_{i}_dram"] for i in range(len(_OUTS)))
    return got[0]
```

```python
from contextlib import ExitStack

import concourse.bass as bass
from concourse import mybir

ALU = mybir.AluOpType
ACT = mybir.ActivationFunctionType
F32 = mybir.dt.float32
BF16 = mybir.dt.bfloat16
F16 = mybir.dt.float16
I32 = mybir.dt.int32
U32 = mybir.dt.uint32
AX = mybir.AxisListType

P = 128
B, SEQ, DM = 128, 64, 128
N = B * SEQ
T = N // P
NH = 16
HD = DM // NH
SCALE = float(HD) ** -0.5
G = 4
E0, F0 = 8, 512
FB = F0 // P
CAP = 1280
ROWS = E0 * CAP
XT = CAP // 256
BLOCKS = 2 * XT
E1 = 16
EPS = 1e-5
BAND = 4
NEG = -1.0e30
LOWEST = -3.0e38
SATURATED = 16.635532
E_LAG = 3
SUM_LAG = 5
SPLIT_AT = 16
RING = 8
SHARE = 256.0
SKIP = 1 << 20
W1COL = HD + 1
C = 2


def build(nc, x, ctx_in, g_xattn, g_ffn, Wq, bq, Wk, bk, Wv, bv, Wo, bo, Wr, br, W1, b1, W2, b2,
          gamma, beta, token_mask, sim_matrix, gates, q_proj, k_proj, v_proj, o_proj, out):
    with ExitStack() as stack:
        def sb(name, shape, dt=F32):
            return stack.enter_context(nc.sbuf_tensor(name, shape, dt))

        def sem(name):
            return stack.enter_context(nc.semaphore(name))

        x_d = x.rearrange("b s d -> (b s) d").rearrange("(t p) d -> p t d", p=P)
        out_d = out.rearrange("b s d -> (b s) d").rearrange("(t p) d -> p t d", p=P)
        ctx_d = ctx_in.rearrange("b s d -> (b s) d").rearrange("(t p) d -> p t d", p=P)
        ctxdup_d = ctx_in.rearrange("(t b) s d -> s t b d", b=2)
        routed = nc.dram_tensor("routed_rows", [ROWS, DM], F32, kind="Internal").ap()
        expert_out = nc.dram_tensor("expert_rows", [ROWS, DM], F32, kind="Internal").ap()

        ident = sb("ident", [P, P])
        ones = sb("ones", [P, P])
        ones_bf = sb("ones_bf", [P, P], BF16)
        ident_bf = sb("ident_bf", [P, P], BF16)
        before = sb("before", [P, P], BF16)
        arena = sb("arena", [P, 3 * E1 * DM])
        zero1 = arena[:, 2 * E1 * DM:3 * E1 * DM]

        def part(n, *dims):
            names = "abcd"[:len(dims)]
            size = 1
            for d in dims:
                size *= d
            return arena[:, n * size:(n + 1) * size].rearrange(
                f"p ({' '.join(names)}) -> p {' '.join(names)}", **dict(zip(names, dims)))

        headmask4 = sb("headmask4", [P, 4])
        headmask = sb("headmask", [P, 2, 4, SEQ])
        band = sb("band", [P, SEQ], BF16)
        band4 = sb("band4", [P, 4, SEQ], BF16)
        causal = sb("causal", [P, P])
        powr = sb("powr", [P, T])
        iota8 = sb("iota8", [P, E0])
        iota16 = sb("iota16", [P, E1])
        caps = sb("caps", [P, E0])
        wq_sb = sb("wq_sb", [P, DM])
        wk_sb = sb("wk_sb", [P, DM])
        wv_sb = sb("wv_sb", [P, DM])
        wo_sb = sb("wo_sb", [P, DM])
        wr_sb = sb("wr_sb", [P, E0])
        bq_sb = sb("bq_sb", [P, 1])
        bk_sb = sb("bk_sb", [P, 1])
        bv_sb = sb("bv_sb", [P, 2, DM])
        bo_sb = sb("bo_sb", [P, DM])
        br_sb = sb("br_sb", [P, E0])
        gamma_sb = sb("gamma_sb", [P, DM])
        beta_sb = sb("beta_sb", [P, DM])
        g_sb = sb("g_sb", [P, 4])
        tg = sb("tg", [P, 4])
        tgbo = sb("tgbo", [P, DM])
        xres = sb("xres", [P, T, DM])
        hres = sb("hres", [P, T, DM])
        stats = sb("stats", [P, 3, 6])
        mv = sb("mv", [P, 3, 2])
        veps = sb("veps", [P, 3])
        root = sb("root", [P, 3])
        squares = sb("squares", [P, 1])
        norm = sb("norm", [P, 1])
        xn = sb("xn", [P, DM])
        ctok = sb("ctok", [P, 2, DM])
        xT = sb("xT", [P, P])
        cT = sb("cT", [P, 2, 2, SEQ])
        qx = sb("qx", [P, 2, 4, SEQ])
        kT = sb("kT", [P, P])
        vx = sb("vx", [P, 2, 2, G, 2, 2, W1COL])
        es = sb("es", [P, 2, G, 2, 2 * SEQ])
        mx = sb("mx", [P, NH])
        pT = sb("pT", [P, 2, G, P])
        rc = sb("rc", [P, NH])
        osb = sb("osb", [P, NH, HD])
        oT = sb("oT", [P, P])
        ytmp = sb("ytmp", [P, DM])
        hn = sb("hn", [P, DM])
        hT = sb("hT", [P, P])
        lg = sb("lg", [P, E0])
        mx8 = sb("mx8", [P, 8])
        ix8 = sb("ix8", [P, 8], U32)
        topv = sb("topv", [P, T, 2])
        topi = sb("topi", [P, T, 2])

        dist = sb("dist", [P, T])
        near = sb("near", [P, T])
        first = part(0, E0, T)
        second = part(1, E0, T)
        key = part(2, E0, T)
        scratch = part(3, E0, T)
        rank = part(4, E0, T)
        keep = part(5, E0, T)
        flags = sb("flags", [P, E0, T], BF16)
        restart = part(6, E0, T)
        counts = sb("counts", [P, E0], BF16)
        thr = sb("thr", [P, E0], I32)
        cand = sb("cand", [P, E0], I32)
        bit = sb("bit", [P, E0], I32)
        accept = sb("accept", [P, E0], I32)
        left = sb("left", [P, E0])
        kept = sb("kept", [P, 2, T])
        gate = sb("gate", [P, T, 2])
        gexp = sb("gexp", [P, 2, T])
        rowf = sb("rowf", [P, 2, T])
        put_row = sb("put_row", [P, T, 2], U32)
        get_row = sb("get_row", [P, T, 2], U32)
        staged = sb("staged", [P, RING, DM])
        staged_row = sb("staged_row", [P, RING, 2], U32)
        w1_sb = part(0, 2, F0)
        w2_sb = part(1, 2, FB, DM)
        b1_sb = sb("b1_sb", [P, 2, FB])
        b2_sb = sb("b2_sb", [P, 2, DM])
        rows_in = sb("rows_in", [P, 2, 2, DM])
        rowsT = sb("rowsT", [P, 2, 2 * P])
        hidT = part(1, 2, FB, 2 * P)
        rows_out = sb("rows_out", [P, 2, 2, DM])
        tggamma = sb("tggamma", [P, DM])
        tgbeta = sb("tgbeta", [P, DM])
        fetch_row = sb("fetch_row", [P, 2, 2], U32)
        fetched = sb("fetched", [P, 2, 2, DM])
        moe = sb("moe", [P, DM])
        moe2 = sb("moe2", [P, DM])
        moen = sb("moen", [P, DM])
        vdup = sb("vdup", [P, 2, 2, DM])
        sim_sb = sb("sim_sb", [P, E1])
        simsq = sb("simsq", [P, E1])
        simn = sb("simn", [P, E1])
        sig = sb("sig", [P, E1])
        hsq = sb("hsq", [P, DM])
        lgr = sb("lgr", [P, E1])
        relu = sb("relu", [P, E1])
        active = sb("active", [P, E1])
        nomax = sb("nomax", [P, 1])
        idle = sb("idle", [P, 1])
        ixf = sb("ixf", [P, 2])
        oneh = sb("oneh", [P, E1])
        oneh2 = sb("oneh2", [P, E1])
        gex = sb("gex", [P, E1])
        gpr = sb("gpr", [P, E1])
        gsum = sb("gsum", [P, 1])
        grec = sb("grec", [P, 1])
        rw = sb("rw", [P, T, E1])
        w16 = sb("w16", [P, 2, E1, 3 * DM], F16)
        widest = sb("widest", [P, 1])
        exponent = sb("exponent", [P, 1], I32)
        upscale = sb("upscale", [P, 1], I32)
        upscale_f = sb("upscale_f", [P, 1])
        downscale = sb("downscale", [P, 1])
        wqkv = hres[:, T - 3 * E1:T, :].rearrange("p (e t) d -> p e t d", t=3)
        wo1 = sb("wo1", [P, E1, DM])
        xs = part(0, E1, DM)
        xsT = sb("xsT", [P, 2, 2, E1, DM], F16)
        qkv = sb("qkv", [P, 2, 3 * DM])
        qkT = sb("qkT", [P, 2 * P])
        sc = sb("sc", [P, P])
        scmax = sb("scmax", [P, 1])
        scsum = sb("scsum", [P, 1])
        screc = sb("screc", [P, 1])
        pr = sb("pr", [P, P])
        prn = sb("prn", [P, P])
        turned = prn
        prT = sb("prT", [P, P])
        aoT = sb("aoT", [P, P])
        z = part(1, E1, DM)
        zsum = sb("zsum", [P, DM])
        result = sb("result", [P, 2, DM])

        psS = stack.enter_context(nc.psum_tensor("psS", [P, G, 512], F32))
        psT = stack.enter_context(nc.psum_tensor("psT", [P, 512], F32))
        psP = stack.enter_context(nc.psum_tensor("psP", [P, 512], F32))
        psR = stack.enter_context(nc.psum_tensor("psR", [P, 512], F32))
        psO = stack.enter_context(nc.psum_tensor("psO", [P, 512], F32))
        o_ps = psO[:, 0:NH * W1COL].rearrange("p (h w) -> p h w", w=W1COL)
        y_ps = psO[:, 272:400]
        zb = (psR, psO, psP)
        lg_ps = psO[:, 400:400 + E1]

        loads = sem("loads")
        made = sem("made")
        consts = sem("consts")
        prep = sem("prep")
        tanhs = sem("tanhs")
        x_in = sem("x_in")
        ctx_s = [sem(f"ctx_s{j}") for j in range(2)]
        variances = sem("variances")
        roots = sem("roots")
        x_norm = sem("x_norm")
        xc_ps = sem("xc_ps")
        xc_sb = sem("xc_sb")
        proj = sem("proj")
        qx_w = sem("qx_w")
        kT_w = sem("kT_w")
        vx_w = sem("vx_w")
        scores = sem("scores")
        shifted = sem("shifted")
        probs = sem("probs")
        pT_ps = sem("pT_ps")
        pT_sb = sem("pT_sb")
        av = sem("av")
        o_norm = sem("o_norm")
        oT_p = sem("oT_p")
        oT_s = sem("oT_s")
        y_p = sem("y_p")
        y_s = sem("y_s")
        h_norm = sem("h_norm")
        h_kept = sem("h_kept")
        hT_p = sem("hT_p")
        hT_s = sem("hT_s")
        lg_p = sem("lg_p")
        lg_s = sem("lg_s")
        top = sem("top")
        top_kept = sem("top_kept")
        searched = sem("searched")
        counted = sem("counted")
        simprep = sem("simprep")
        gexp_s = sem("gexp_s")
        routes_d = sem("routes_d")
        zeroed = sem("zeroed")
        staged_s = sem("staged_s")
        put = [sem(f"put{j}") for j in range(RING)]
        taken = sem("taken")
        w_in = [sem(f"w_in{j}") for j in range(2)]
        rows_in_s = [sem(f"rows_in_s{j}") for j in range(2)]
        seen = sem("seen")
        rT_ps = sem("rT_ps")
        rT_sb = sem("rT_sb")
        hid_ps = sem("hid_ps")
        hid_sb = sem("hid_sb")
        yrow_ps = sem("yrow_ps")
        yrow_sb = sem("yrow_sb")
        rows_out_s = [sem(f"rows_out_s{j}") for j in range(2)]
        fetch_idx = sem("fetch_idx")
        fetched_s = [sem(f"fetched_s{j}") for j in range(2)]
        merged = sem("merged")
        moe_n = sem("moe_n")
        squares_s = sem("squares_s")
        norm_s = sem("norm_s")
        x2_s = sem("x2_s")
        vdup_s = [sem(f"vdup_s{j}") for j in range(2)]
        g_in = sem("g_in")
        g_ex = sem("g_ex")
        ewts = sem("ewts")
        w32_in = sem("w32_in")
        widths = sem("widths")
        widths_p = sem("widths_p")
        scale_s = sem("scale_s")
        w16_high = sem("w16_high")
        w16_s = sem("w16_s")
        xsT_lo = sem("xsT_lo")
        xs_s = sem("xs_s")
        xsT_p = sem("xsT_p")
        xsT_s = sem("xsT_s")
        qkv_p = sem("qkv_p")
        qkv_s = sem("qkv_s")
        qkT_p = sem("qkT_p")
        qkT_s = sem("qkT_s")
        sc_p = sem("sc_p")
        sc_m = sem("sc_m")
        pr_e = sem("pr_e")
        pr_s = sem("pr_s")
        prT_p = sem("prT_p")
        prT_s = sem("prT_s")
        ao_p = sem("ao_p")
        ao_s = sem("ao_s")
        z_p = sem("z_p")
        z_s = sem("z_s")
        z_half = sem("z_half")
        z_sum = sem("z_sum")
        res_s = sem("res_s")
        res_out = [sem(f"res_out{j}") for j in range(2)]
        LOOPED = [*ctx_s, variances, roots, x_norm, xc_ps, xc_sb, proj, qx_w, kT_w, vx_w, scores, shifted, probs, pT_ps,
                  pT_sb, av, o_norm, oT_p, oT_s, y_p, y_s, h_norm, h_kept, hT_p, hT_s, lg_p, lg_s, top, top_kept,
                  searched, counted, staged_s, taken, *w_in, *rows_in_s, rT_ps, rT_sb, hid_ps, hid_sb, yrow_ps,
                  yrow_sb, *rows_out_s, fetch_idx, merged, moe_n, x2_s, squares_s, norm_s, *vdup_s, g_in, g_ex,
                  xs_s, xsT_p, xsT_s, xsT_lo, qkv_p, qkv_s, qkT_p, qkT_s, sc_p, sc_m, pr_e, pr_s, prT_p, prT_s, ao_p, ao_s, z_p, z_s,
                  z_half, z_sum, res_s, *res_out]

        def number(k, off):
            return off if k is None else k * 2 + off

        def tile(a, k, off):
            if k is None:
                return a[:, off]
            half = a[:, :, :].rearrange("p (k j) d -> p k j d", j=2)
            return half[:, bass.ds(k + off // 2, 1), off % 2, :].rearrange("p o d -> p (o d)")

        def after(engine, semaphore, count):
            if not isinstance(count, int) or count > 0:
                engine.wait_ge(semaphore, count + C)

        def upto(count, total):
            return min(count, total) if isinstance(count, int) else count

        def run_steps(engine, first, last, before, behind, step, between=None, at=0):
            lo = -before
            hi = T - 1 - behind
            hi -= (hi - lo + 1) % 2
            turns = [0, (hi - lo + 1) // 2]
            if between:
                turns.insert(1, (at - lo) // 2)
            for s in range(first, lo):
                step(None, s)
            for start, end in zip(turns[:-1], turns[1:]):
                if start:
                    between()
                with engine.Fori(start, end) as k:
                    for j in range(2):
                        step(k, lo + j)
            for s in range(hi + 1, last + 1):
                step(None, s)

        def bcast(v, n):
            return v.rearrange("(o n) -> o n", o=1).broadcast_to([P, n])

        LOADS = [
            (wq_sb[:, :], Wq), (wk_sb[:, :], Wk), (wv_sb[:, :], Wv), (wo_sb[:, :], Wo), (wr_sb[:, :], Wr),
            (bq_sb[:, :], bq.rearrange("(n o) -> n o", o=1)), (bk_sb[:, :], bk.rearrange("(n o) -> n o", o=1)),
            (bv_sb[:, 0, :], bcast(bv, DM)), (bv_sb[:, 1, :], bcast(bv, DM)), (bo_sb[:, :], bcast(bo, DM)),
            (br_sb[:, :], bcast(br, E0)), (gamma_sb[:, :], bcast(gamma, DM)), (beta_sb[:, :], bcast(beta, DM)),
            (sim_sb[:, :], sim_matrix), (sig[:, :], bcast(gates, E1)),
            (g_sb[:, 0:2], bcast(g_xattn, 2)), (g_sb[:, 2:4], bcast(g_ffn, 2)),
        ]
        block = stack.enter_context(nc.Block())

        @block.sync
        def _(sp):
            for s in LOOPED:
                sp.sem_inc(s, C)
            for dst, src in LOADS:
                sp.dma_start(dst, src).then_inc(loads, 16)
            sp.dma_start(xres[:, 0:4, :], x_d[:, 0:4, :]).then_inc(x_in, 16)

            def load_ctx(k, off):
                i = number(k, off)
                after(sp, xc_ps, i - 1)
                sp.dma_start(ctok[:, off % 2, :], tile(ctx_d, k, off)).then_inc(ctx_s[off % 2], 16)

            for i in range(2):
                load_ctx(None, i)
            sp.wait_ge(x_in, 16)
            sp.dma_start(xres[:, 4:T, :], x_d[:, 4:T, :]).then_inc(x_in, 16)
            for e3, w in enumerate((q_proj, k_proj, v_proj)):
                sp.dma_start(wqkv[:, :, e3, :], w.rearrange("e c h -> c e h")).then_inc(w32_in, 16)
            with sp.Fori(0, T // 2 - 1) as k:
                for j in range(2):
                    load_ctx(k, 2 + j)
            sp.wait_ge(made, 2)
            for c in range(ROWS // P // 16):
                sp.dma_start(routed.rearrange("(p r) d -> p (r d)", p=P)[:, c * 2048:(c + 1) * 2048], zero1[:, :]).then_inc(zeroed, 16)
            sp.dma_start(wo1[:, :, :], o_proj.rearrange("e h c -> h e c")).then_inc(ewts, 16)
            for s in put:
                sp.wait_ge(s, 32 * T // RING)
            w1_d = W1.rearrange("(k j) c f -> k j c f", j=2)
            w2_d = W2.rearrange("(k j) (f p) c -> k j p f c", j=2, p=P)
            b1_d = b1.rearrange("(k j) (f p) -> k j p f", j=2, p=P)
            b2_d = b2.rearrange("(k j) (o c) -> k j o c", j=2, o=1)
            in_d = routed.rearrange("(k j m r p) d -> k j m p r d", j=2, m=XT, r=2, p=P)
            out_rows_d = expert_out.rearrange("(k j m r p) d -> k j m p r d", j=2, m=XT, r=2, p=P)

            def store_rows(k, t):
                after(sp, yrow_sb, k * BLOCKS + t + 1)
                sp.sem_inc(seen, 1)
                sp.dma_start(out_rows_d[bass.ds(k, 1), t // XT, t % XT].rearrange("o p r d -> (o p) r d"),
                             rows_out[:, t % 2, :, :]).then_inc(rows_out_s[t % 2], 16)

            def load_weights(k, j, done, ahead=0):
                one = bass.ds(k, 1)
                after(sp, yrow_sb, done)
                sp.dma_start(w1_sb[:, j, :], w1_d[ahead:][one, j].rearrange("o c f -> (o c) f")).then_inc(w_in[j], 16)
                sp.dma_start(w2_sb[:, j, :, :], w2_d[ahead:][one, j].rearrange("o p f c -> (o p) f c")).then_inc(w_in[j], 16)
                with nc.allow_non_contiguous_dma(reason="one bias per partition"):
                    sp.dma_start(b1_sb[:, j, :], b1_d[ahead:][one, j].rearrange("o p f -> (o p) f")).then_inc(w_in[j], 16)
                sp.dma_start(b2_sb[:, j, :], b2_d[ahead:][one, j].rearrange("o q c -> (o q) c").broadcast_to([P, DM])).then_inc(w_in[j], 16)

            def load_rows(k, t, ahead=0):
                after(sp, rT_ps, (k * BLOCKS) + (ahead * BLOCKS + t - 1))
                sp.dma_start(rows_in[:, t % 2, :, :], in_d[ahead:][bass.ds(k, 1), t // XT, t % XT].rearrange("o p r d -> (o p) r d")).then_inc(rows_in_s[t % 2], 16)

            def two_experts(k, last):
                for t in range(BLOCKS):
                    if t == 1:
                        load_weights(k, 1, k * BLOCKS)
                    if t == XT + 2 and not last:
                        load_weights(k, 0, k * BLOCKS + XT, ahead=1)
                    if t + 2 < BLOCKS:
                        load_rows(k, t + 2)
                    elif not last:
                        load_rows(k, t + 2 - BLOCKS, ahead=1)
                    if t >= 2:
                        store_rows(k, t - 2)
                for t in range(BLOCKS - 2, BLOCKS):
                    store_rows(k, t)

            load_weights(0, 0, 0)
            for t in range(2):
                load_rows(0, t)
            with sp.Fori(0, E0 // 2 - 1) as k:
                two_experts(k, False)
            two_experts(E0 // 2 - 1, True)
            for s in rows_out_s:
                sp.wait_ge(s, 16 * XT * (E0 // 2) + C)

            def load_ctx2(k, off):
                i = number(k, off)
                after(sp, xc_ps, T + i - 1)
                sp.dma_start(ctok[:, off % 2, :], tile(ctx_d, k, off)).then_inc(ctx_s[off % 2], 16)
                after(sp, vx_w, 2 * T + i * 2 - 2)
                half = ctxdup_d.rearrange("s (k j) b d -> s k j b d", j=2)[:, :, off % 2]
                src = half[:, off // 2] if k is None else half[:, bass.ds(k + off // 2, 1)].rearrange("s o b d -> s (o b) d")
                for h in range(2):
                    sp.dma_start(vdup[h * SEQ:(h + 1) * SEQ, off % 2, :, :], src).then_inc(vdup_s[off % 2], 16)

            def step(k, off):
                if k is not None or 0 <= off + 3 < T:
                    load_ctx2(k, off + 3)
                if k is not None or 0 <= off - 6 < T:
                    after(sp, res_s, number(k, off) - 5)
                    sp.dma_start(tile(out_d, k, off - 6), result[:, (off - 6) % 2, :]).then_inc(res_out[(off - 6) % 2], 16)

            run_steps(sp, -3, T + 5, -6, 3, step)
            for s in res_out:
                sp.wait_ge(s, 16 * (T // 2) + C)

        @block.gpsimd
        def _(pool):
            steps = []

            def make(instruction):
                instruction.then_inc(made, 1)
                steps.append(1)
                pool.wait_ge(made, len(steps))
            make(pool.memset(ones[:, :], 1.0))
            make(pool.memset(zero1[:, :], 0.0))
            make(pool.memset(powr[:, :], -0.5))
            make(pool.affine_select(out=ident[:, :], in_=ones[:, :], pattern=[[-1, P]], compare_op=ALU.is_equal,
                                    fill=0.0, base=0, channel_multiplier=1))
            make(pool.affine_select(out=before[:, :], in_=ones[:, :], pattern=[[1, P]], compare_op=ALU.is_gt,
                                    fill=0.0, base=0, channel_multiplier=-1))
            make(pool.affine_select(out=causal[:, :], in_=zero1[:, 0:P], pattern=[[-1, P]], compare_op=ALU.is_ge,
                                    fill=NEG, base=0, channel_multiplier=1))
            make(pool.memset(causal[SEQ:P, 0:SEQ], NEG))
            for h in range(2):
                rows = slice(h * SEQ, (h + 1) * SEQ)
                make(pool.affine_select(out=band[rows, :], in_=zero1[rows, 0:SEQ], pattern=[[-1, SEQ]],
                                        compare_op=ALU.is_ge, fill=NEG, base=BAND, channel_multiplier=1))
                make(pool.affine_select(out=band[rows, :], in_=band[rows, :], pattern=[[1, SEQ]],
                                        compare_op=ALU.is_ge, fill=NEG, base=BAND, channel_multiplier=-1))
            make(pool.iota(iota8[:, :], pattern=[[1, E0]], base=0, channel_multiplier=0,
                           allow_small_or_imprecise_dtypes=True))
            make(pool.iota(iota16[:, :], pattern=[[1, E1]], base=0, channel_multiplier=0,
                           allow_small_or_imprecise_dtypes=True))
            make(pool.iota(caps[:, :], pattern=[[CAP, E0]], base=0, channel_multiplier=0,
                           allow_small_or_imprecise_dtypes=True))

            def step(k, off):
                n = number(k, off)
                after(pool, variances, n + 3)
                pool.tensor_tensor(root[:, 0:2], veps[:, 0:2], powr[:, 0:2], ALU.pow).then_inc(roots, 1)
                if k is not None or 0 <= off - 3 < T:
                    after(pool, top, 2 * n - 4)
                    pool.sem_inc(taken, 1)
                    pool.tensor_copy(tile(topv, k, off - 3), mx8[:, 0:2]).then_inc(top_kept, 1)
                    pool.tensor_copy(tile(topi, k, off - 3), ix8[:, 0:2]).then_inc(top_kept, 1)
                if k is not None or 0 <= off - 2 < T:
                    after(pool, h_norm, n - 1)
                    pool.sem_inc(taken, 1)
                    pool.tensor_copy(tile(hres, k, off - 2), hn[:, :]).then_inc(h_kept, 1)

            run_steps(pool, -2, T + 2, -3, 2, step)
            pool.wait_ge(simprep, 2)
            pool.tensor_tensor(simsq[:, :], simsq[:, :], powr[:, 0:E1], ALU.pow).then_inc(simprep, 1)
            pool.wait_ge(zeroed, 16 * (ROWS // P // 16))
            with pool.Fori(0, T // RING) as k:
                for j in range(RING):
                    pool.wait_ge(staged_s, k * (2 * RING) + 2 * j + 2 + C)
                    pool.sem_inc(taken, 1)
                    for slot in range(2):
                        pool.indirect_dma_start(
                            out=routed, out_offset=bass.IndirectOffsetOnAxis(ap=staged_row[:, j, slot:slot + 1], axis=0),
                            in_=staged[:, j, :], in_offset=None, bounds_check=ROWS - 1, oob_is_err=False).then_inc(put[j], 16)
            for s in rows_out_s:
                pool.wait_ge(s, 16 * XT * (E0 // 2) + C)

            def fetch(k, off):
                i = number(k, off)
                after(pool, merged, i - 1)
                pool.sem_inc(taken, 1)
                pool.tensor_copy(fetch_row[:, off % 2, :], tile(get_row, k, off)).then_inc(fetch_idx, 1)
                after(pool, fetch_idx, i + 1)
                pool.sem_inc(taken, 1)
                for slot in range(2):
                    pool.indirect_dma_start(
                        out=fetched[:, off % 2, slot, :], out_offset=None, in_=expert_out,
                        in_offset=bass.IndirectOffsetOnAxis(ap=fetch_row[:, off % 2, slot:slot + 1], axis=0)).then_inc(fetched_s[off % 2], 16)

            def step(k, off):
                n = number(k, off)
                after(pool, variances, T + 5 + n + 5)
                pool.tensor_tensor(root[:, :], veps[:, :], powr[:, 0:3], ALU.pow).then_inc(roots, 1)
                if k is not None or 0 <= off + 4 < T:
                    xt = tile(xres, k, off + 4)
                    after(pool, moe_n, n + 5)
                    pool.sem_inc(taken, 1)
                    pool.tensor_tensor(moen[:, :], moen[:, :], tggamma[:, :], ALU.mult)
                    pool.tensor_tensor(xt, xt, tgbeta[:, :], ALU.add).then_inc(x2_s, 1)
                    after(pool, x2_s, 2 * n + 9)
                    pool.sem_inc(taken, 1)
                    pool.tensor_tensor(xt, xt, moen[:, :], ALU.add).then_inc(x2_s, 1)
                if k is not None or 0 <= off < T:
                    after(pool, squares_s, n + 1)
                    after(pool, lg_s, T + n)
                    pool.tensor_tensor(norm[:, :], squares[:, :], powr[:, 0:1], ALU.pow).then_inc(norm_s, 1)
                    after(pool, h_norm, T + n + 1)
                    pool.sem_inc(taken, 1)
                    pool.tensor_copy(tile(hres, k, off), hn[:, :]).then_inc(h_kept, 1)
                if k is not None or 0 <= off + 6 < T:
                    fetch(k, off + 6)

            def combine(k, off):
                i = number(k, off)
                after(pool, z_s, i * 4 + 4)
                pool.sem_inc(taken, 1)
                pool.tensor_tensor(z[:, 0:8, :], z[:, 0:8, :], z[:, 8:16, :], ALU.add).then_inc(z_half, 1)
                for level, width in enumerate((4, 2)):
                    after(pool, z_half, i * 3 + level + 1)
                    pool.sem_inc(taken, 1)
                    pool.tensor_tensor(z[:, 0:width, :], z[:, 0:width, :], z[:, width:2 * width, :], ALU.add).then_inc(z_half, 1)
                after(pool, z_half, i * 3 + 3)
                pool.sem_inc(taken, 1)
                pool.tensor_tensor(zsum[:, :], z[:, 0, :], z[:, 1, :], ALU.add).then_inc(z_sum, 1)
                after(pool, z_sum, i + 1)
                pool.sem_inc(taken, 1)
                pool.wait_ge(res_out[off % 2], (i - off % 2) * 8 + C)
                pool.sem_inc(taken, 1)
                pool.tensor_tensor(result[:, off % 2, :], zsum[:, :], tile(xres, k, off), ALU.add).then_inc(res_s, 1)

            def step_both(k, off):
                if k is not None or 0 <= off - SUM_LAG < T:
                    combine(k, off - SUM_LAG)
                if k is not None or off <= T + 1:
                    step(k, off)

            for i in range(2):
                fetch(None, i)
            run_steps(pool, -4, T - 1 + SUM_LAG, -SUM_LAG, 6, step_both)

        MADE = 14

        @block.vector
        def _(dve):
            dve.wait_ge(made, MADE)
            dve.wait_ge(loads, 16 * len(LOADS))
            dve.tensor_reduce(headmask4[:, :], ident[:, :].rearrange("p (g h d) -> p h g d", g=G, h=4),
                              AX.XY, ALU.add).then_inc(prep, 1)
            dve.wait_ge(prep, 1)
            for b in range(2):
                dve.tensor_copy(headmask[:, b, :, :], headmask4[:, :].unsqueeze(2).broadcast_to([P, 4, SEQ])).then_inc(prep, 1)
            dve.tensor_copy(ident_bf[:, :], ident[:, :]).then_inc(prep, 1)
            dve.tensor_copy(ones_bf[:, :], ones[:, :]).then_inc(prep, 1)
            dve.memset(vx[:, :, :, :, :, :, :], 0.0).then_inc(prep, 1)
            dve.wait_ge(prep, 6)
            for h in range(2):
                dve.memset(vx[h * SEQ:(h + 1) * SEQ, :, :, :, :, h, HD].rearrange("p u b g h -> p (u b g h)"), 1.0).then_inc(prep, 1)
            dve.wait_ge(tanhs, 1)
            dve.tensor_scalar(tgbo[:, :], bo_sb[:, :], tg[:, 0:1], None, ALU.mult).then_inc(prep, 1)
            dve.wait_ge(prep, 9)
            dve.tensor_copy(mx[:, 0:1], tg[:, 0:1]).then_inc(consts, 1)

            dve.memset(mv[:, :, :], 1.0)
            dve.memset(veps[:, :], 1.0)
            dve.drain()

            s4 = psS[:, :, 0:2 * P].rearrange("p g (a k) -> p g a k", k=SEQ)

            def maxima(i):
                after(dve, scores, i + 1)
                dve.tensor_reduce(mx[:, :].rearrange("p (g a) -> p g a", g=G), s4, AX.X, ALU.max)

            def shift_scores(i, buffer):
                after(dve, pT_ps, 2 * i - 2)
                dve.tensor_tensor(es[:, buffer].rearrange("p g b (a k) -> p g (b a) k", k=SEQ), s4,
                                  mx[:, :].rearrange("p (g a) -> p g a", g=G).unsqueeze(3).broadcast_to([P, G, 4, SEQ]),
                                  ALU.subtract).then_inc(shifted, 1)

            def split_weights():
                dve.wait_ge(w32_in, 48)
                dve.tensor_reduce(widest[:, :], wqkv, AX.XYZ, ALU.max, apply_absolute_value=True)
                dve.drain()
                dve.tensor_copy(turned[:, :], widest[:, 0:1].broadcast_to([P, P])).then_inc(widths, 1)
                dve.wait_ge(widths_p, 1)
                dve.tensor_reduce(widest[:, :], psR[:, 0:P], AX.X, ALU.max).then_inc(widths, 1)
                dve.drain()
                dve.tensor_scalar(widest[:, :], widest[:, :], 2.0 ** -100, None, ALU.max)
                dve.drain()
                dve.tensor_scalar(exponent[:, :], widest[:, :].bitcast(I32), 0x7F800000, None, ALU.bitwise_and)
                dve.drain()
                dve.tensor_scalar(upscale[:, :], exponent[:, :], -1.0, float((127 + 127 + 13) << 23), ALU.mult, ALU.add)
                dve.tensor_scalar(downscale[:, :], exponent[:, :].bitcast(F32), 2.0 ** -13 / SHARE, None, ALU.mult)
                dve.drain()
                dve.tensor_copy(upscale_f[:, :], upscale[:, :].bitcast(F32)).then_inc(scale_s, 1)
                dve.drain()
                w3 = wqkv.rearrange("p e t d -> p e (t d)")
                dve.wait_ge(w16_high, 1)
                dve.scalar_tensor_tensor(w16[:, 1, :, :], w3, upscale_f[:, 0:1], w16[:, 0, :, :],
                                         ALU.mult, ALU.subtract).then_inc(w16_s, 1)

            def norm_heads():
                dve.reciprocal(rc[:, :], o_ps[:, :, HD])
                dve.drain()
                dve.tensor_tensor(osb[:, :, :], o_ps[:, :, 0:HD], rc[:, :].unsqueeze(2).broadcast_to([P, NH, HD]),
                                  ALU.mult).then_inc(o_norm, 1)

            def step(k, off):
                n = number(k, off)

                def has(lag):
                    return k is not None or 0 <= off + lag < T

                if has(1):
                    after(dve, proj, n + 2)
                    for h in range(2):
                        rows = slice(h * SEQ, (h + 1) * SEQ)
                        v = psP[rows, 2 * P:4 * P].rearrange("p (b g j h d) -> p (b g) j h d", b=2, g=G, j=2, h=2)[:, :, h, :, :]
                        bvv = bv_sb[rows, :, :].rearrange("p b (g j h d) -> p (b g) j h d", g=G, j=2, h=2)[:, :, h, :, :]
                        after(dve, av, n)
                        dst = vx[rows, (off + 1) % 2, :, :, :, h, 0:HD].rearrange("p b g h d -> p (b g) h d")
                        dve.tensor_tensor(dst, v, bvv, ALU.add).then_inc(vx_w, 1)
                if has(-1):
                    after(dve, av, n)
                if has(-2):
                    after(dve, y_p, n - 1)
                if has(-3):
                    after(dve, lg_p, n - 2)
                if has(-1):
                    after(dve, oT_p, n - 1)
                    norm_heads()
                if has(-2):
                    dve.scalar_tensor_tensor(ytmp[:, :], y_ps, tg[:, 0:1], tgbo[:, :], ALU.mult, ALU.add).then_inc(y_s, 1)
                if has(-3):
                    after(dve, top_kept, 2 * n - 6)
                    dve.tensor_tensor(lg[:, :], psO[:, 400:400 + E0], br_sb[:, :], ALU.add).then_inc(lg_s, 1)
                dve.drain()
                if has(-2):
                    x1 = tile(xres, k, off - 2)
                    dve.tensor_tensor(x1, x1, ytmp[:, :], ALU.add)
                if has(2):
                    dve.bn_stats(stats[:, 0, :], tile(xres, k, off + 2))
                if has(-3):
                    dve.max(mx8[:, :], lg[:, :]).then_inc(top, 1)
                dve.drain()
                if has(-2):
                    dve.bn_stats(stats[:, 1, :], x1)
                if has(2):
                    dve.bn_aggr(mv[:, 0, :], stats[:, 0, :])
                if has(-3):
                    dve.max_index(ix8[:, :], mx8[:, :], lg[:, :]).then_inc(top, 1)
                dve.drain()
                if has(-2):
                    dve.bn_aggr(mv[:, 1, :], stats[:, 1, :])
                    dve.drain()
                dve.tensor_scalar(veps[:, 0:2], mv[:, 0:2, 1], EPS, None, ALU.add).then_inc(variances, 1)
                if has(1):
                    maxima(n + 1)
                after(dve, roots, n + 3)
                if has(2):
                    after(dve, xc_ps, n + 2)
                    dve.tensor_scalar(xn[:, :], tile(xres, k, off + 2), mv[:, 0, 0:1], root[:, 0:1],
                                      ALU.subtract, ALU.mult).then_inc(x_norm, 1)
                if has(-2):
                    after(dve, hT_p, n - 2)
                    after(dve, h_kept, n - 2)
                    dve.tensor_scalar(hn[:, :], x1, mv[:, 1, 0:1], root[:, 1:2], ALU.subtract, ALU.mult).then_inc(h_norm, 1)
                dve.drain()
                if has(1):
                    shift_scores(n + 1, (off + 1) % 2)
                if has(2):
                    after(dve, proj, n + 3)
                    after(dve, scores, n + 2)
                    for b in range(2):
                        q = psP[:, b * SEQ:(b + 1) * SEQ].unsqueeze(1).broadcast_to([P, 4, SEQ])
                        dve.scalar_tensor_tensor(qx[:, b, :, :], q, bq_sb[:, 0:1], headmask[:, b, :, :],
                                                 ALU.add, ALU.mult).then_inc(qx_w, 1)
                    dve.tensor_scalar(kT[:, :], psP[:, P:2 * P], bk_sb[:, 0:1], None, ALU.add).then_inc(kT_w, 1)
                if k is None and off == 1:
                    dve.wait_ge(x_in, 32)

            dve.wait_ge(x_in, 16)
            run_steps(dve, -2, T + 2, -4, 2, step, split_weights, SPLIT_AT)
            dve.tensor_tensor(simsq[:, :], sim_sb[:, :], sim_sb[:, :], ALU.mult).then_inc(simprep, 1)
            dve.wait_ge(counted, 1 + C)
            dve.tensor_scalar(simsq[:, :], psT[:, 0:E1], 1e-12, None, ALU.add).then_inc(simprep, 1)
            dve.wait_ge(simprep, 3)
            dve.tensor_tensor(simn[:, :], sim_sb[:, :], simsq[:, :], ALU.mult)
            dve.wait_ge(tanhs, 2)
            dve.tensor_scalar(sig[:, :], sig[:, :], 1.0, None, ALU.add)
            dve.drain()
            dve.reciprocal(sig[:, :], sig[:, :])
            dve.tensor_scalar(tggamma[:, :], gamma_sb[:, :], tg[:, 2:3], None, ALU.mult)
            dve.tensor_scalar(tgbeta[:, :], beta_sb[:, :], tg[:, 2:3], None, ALU.mult)
            dve.tensor_copy(band4[:, :, :], band[:, :].unsqueeze(1).broadcast_to([P, 4, SEQ]))
            dve.wait_ge(top_kept, 2 * T + C)
            dve.tensor_tensor(dist[:, :], topv[:, :, 0], topv[:, :, 1], ALU.subtract).then_inc(routes_d, 1)
            dve.memset(restart[:, :, :], 1.0)
            dve.memset(bit[:, :], 0)
            for slot, hot in enumerate((first, second)):
                dve.tensor_tensor(hot[:, :, :], topi[:, :, slot].unsqueeze(1).broadcast_to([P, E0, T]),
                                  iota8[:, :].unsqueeze(2).broadcast_to([P, E0, T]), ALU.is_equal)
            dve.drain()
            dve.memset(restart[:, :, 0], 0.0)
            dve.tensor_scalar(near[:, :], dist[:, :], SATURATED, None, ALU.min)
            dve.tensor_tensor(scratch[:, :, :], first[:, :, :], second[:, :, :], ALU.add)
            dve.drain()
            dve.tensor_tensor(key[:, :, :], first[:, :, :], near[:, :].unsqueeze(1).broadcast_to([P, E0, T]), ALU.mult)
            dve.tensor_tensor(rank[:, :, :], second[:, :, :], dist[:, :].unsqueeze(1).broadcast_to([P, E0, T]), ALU.mult)
            dve.tensor_scalar(scratch[:, :, :], scratch[:, :, :], -LOWEST, LOWEST, ALU.mult, ALU.add)
            dve.drain()
            dve.tensor_tensor(key[:, :, :], key[:, :, :], rank[:, :, :], ALU.subtract)
            dve.drain()
            dve.tensor_tensor(key[:, :, :], key[:, :, :], scratch[:, :, :], ALU.add)
            dve.memset(cand[:, :], 0)
            dve.drain()

            def count(op, against):
                dve.tensor_tensor(flags[:, :, :], key[:, :, :],
                                  against[:, :].bitcast(F32).unsqueeze(2).broadcast_to([P, E0, T]), op)
                dve.drain()
                with nc.allow_low_precision(reason="counts up to 64 are exact in bfloat16"):
                    dve.tensor_reduce(counts[:, :], flags[:, :, :], AX.X, ALU.add).then_inc(searched, 1)

            count(ALU.is_ge, cand)
            dve.wait_ge(counted, 2 + C)
            dve.tensor_scalar(accept[:, :], psP[:, 0:E0], float(CAP), -1.0, ALU.is_ge, ALU.mult)
            dve.memset(bit[:, :], 0x40000000)
            dve.drain()
            dve.tensor_scalar(thr[:, :], accept[:, :], -1, None, ALU.bitwise_xor)
            dve.drain()
            with dve.Fori(0, 31) as n:
                dve.tensor_tensor(cand[:, :], thr[:, :], bit[:, :], ALU.bitwise_xor)
                dve.drain()
                count(ALU.is_ge, cand)
                dve.wait_ge(counted, n + 3 + C)
                dve.tensor_scalar(accept[:, :], psP[:, 0:E0], float(CAP), -1.0, ALU.is_ge, ALU.mult)
                dve.drain()
                dve.tensor_tensor(accept[:, :], accept[:, :], bit[:, :], ALU.bitwise_and)
                dve.drain()
                dve.tensor_tensor(thr[:, :], thr[:, :], accept[:, :], ALU.bitwise_xor)
                dve.tensor_scalar(bit[:, :], bit[:, :], 1, None, ALU.logical_shift_right)
                dve.drain()
            count(ALU.is_gt, thr)
            dve.wait_ge(counted, 34 + C)
            dve.tensor_scalar(left[:, :], psP[:, 0:E0], -1.0, float(CAP), ALU.mult, ALU.add)
            dve.tensor_copy(keep[:, :, :], flags[:, :, :])
            dve.drain()
            dve.tensor_tensor(scratch[:, :, :], key[:, :, :], thr[:, :].bitcast(F32).unsqueeze(2).broadcast_to([P, E0, T]), ALU.is_equal)
            dve.tensor_scalar(rank[:, :, :], key[:, :, :], LOWEST, None, ALU.is_gt)
            dve.drain()
            dve.tensor_tensor(scratch[:, :, :], scratch[:, :, :], rank[:, :, :], ALU.mult)
            dve.drain()
            dve.tensor_copy(flags[:, :, :], scratch[:, :, :]).then_inc(searched, 1)

            def ranks(n):
                dve.wait_ge(counted, 35 + n + C)
                flat = rank[:, :, :].rearrange("p e t -> p (e t)")
                dve.tensor_tensor_scan(flat, restart[:, :, :].rearrange("p e t -> p (e t)"), psR[:, :], 0.0, ALU.mult, ALU.add)
                dve.drain()
                dve.tensor_tensor(flat, flat, psR[:, :], ALU.subtract)
                dve.drain()
                dve.tensor_tensor(flat, flat, psT[:, :], ALU.add)
                dve.drain()

            ranks(0)
            dve.tensor_tensor(rank[:, :, :], rank[:, :, :], left[:, :].unsqueeze(2).broadcast_to([P, E0, T]), ALU.is_lt)
            dve.drain()
            dve.tensor_tensor(rank[:, :, :], rank[:, :, :], scratch[:, :, :], ALU.mult)
            dve.drain()
            dve.tensor_tensor(keep[:, :, :], keep[:, :, :], rank[:, :, :], ALU.add)
            dve.drain()
            dve.tensor_copy(flags[:, :, :], keep[:, :, :]).then_inc(searched, 1)
            ranks(1)
            dve.tensor_tensor(rank[:, :, :], rank[:, :, :], caps[:, :].unsqueeze(2).broadcast_to([P, E0, T]), ALU.add)
            dve.wait_ge(gexp_s, 1)
            dve.tensor_scalar(gexp[:, 0, :], gexp[:, 1, :], 1.0, None, ALU.add)
            dve.drain()
            dve.reciprocal(gexp[:, 0, :], gexp[:, 0, :])
            dve.drain()
            dve.tensor_tensor(gexp[:, 1, :], gexp[:, 1, :], gexp[:, 0, :], ALU.mult)
            for slot, hot in enumerate((first, second)):
                dve.tensor_tensor(scratch[:, :, :], hot[:, :, :], keep[:, :, :], ALU.mult)
                dve.drain()
                dve.tensor_reduce(kept[:, slot, :], scratch[:, :, :].rearrange("p e t -> p t e"), AX.X, ALU.add)
                dve.drain()
                dve.tensor_tensor(scratch[:, :, :], scratch[:, :, :], rank[:, :, :], ALU.mult)
                dve.drain()
                dve.tensor_reduce(rowf[:, slot, :], scratch[:, :, :].rearrange("p e t -> p t e"), AX.X, ALU.add)
                dve.drain()
                dve.tensor_tensor(gate[:, :, slot], gexp[:, slot, :], kept[:, slot, :], ALU.mult)
                dve.tensor_copy(get_row[:, :, slot], rowf[:, slot, :])
                dve.tensor_scalar(near[:, :], kept[:, slot, :], -float(SKIP), float(SKIP), ALU.mult, ALU.add)
                dve.drain()
                dve.tensor_tensor(put_row[:, :, slot], rowf[:, slot, :], near[:, :], ALU.add)
                dve.drain()
            def stage(k, j):
                if k is None:
                    h, r = hres[:, j, :], put_row[:, j, :]
                else:
                    dve.wait_ge(put[j], k * 32)
                    h = hres[:, :, :].rearrange("p (k j) d -> p k j d", j=RING)[:, bass.ds(k, 1), j, :].rearrange("p o d -> p (o d)")
                    r = put_row[:, :, :].rearrange("p (k j) d -> p k j d", j=RING)[:, bass.ds(k, 1), j, :].rearrange("p o d -> p (o d)")
                dve.tensor_copy(staged[:, j, :], h).then_inc(staged_s, 1)
                dve.tensor_copy(staged_row[:, j, :], r).then_inc(staged_s, 1)

            for j in range(RING):
                stage(None, j)
            with dve.Fori(1, T // RING) as k:
                for j in range(RING):
                    stage(k, j)
            yb = (psR, psO)
            tb = (psT, psP)

            def add_bias(k, t):
                n = k * BLOCKS + t
                dve.wait_ge(yrow_ps, n + 1 + C)
                dve.wait_ge(rows_out_s[t % 2], k * (16 * XT) + 16 * (t // 2) + C)
                dve.tensor_tensor(rows_out[:, t % 2, :, :], yb[t % 2][:, 0:2 * P].rearrange("p (r d) -> p r d", r=2),
                                  b2_sb[:, t // XT, :].unsqueeze(1).broadcast_to([P, 2, DM]), ALU.add).then_inc(yrow_sb, 1)

            def keep_turned_rows(k, t):
                n = k * BLOCKS + t
                after(dve, rT_ps, n + 1)
                after(dve, hid_ps, n - 1)
                dve.tensor_copy(rowsT[:, t % 2, :], tb[t % 2][:, 0:2 * P]).then_inc(rT_sb, 1)

            with dve.Fori(0, E0 // 2) as k:
                keep_turned_rows(k, 0)
                for t in range(BLOCKS):
                    if t + 1 < BLOCKS:
                        keep_turned_rows(k, t + 1)
                    if t % XT == 0:
                        dve.wait_ge(w_in[t // XT], k * 64 + 64 + C)
                    if t >= 1:
                        add_bias(k, t - 1)
                add_bias(k, BLOCKS - 1)
            def weigh(k, off):
                i = number(k, off)
                after(dve, xsT_p, i * 4)
                after(dve, h_kept, T + i + 1)
                dve.tensor_tensor(xs[:, :, :], tile(hres, k, off).unsqueeze(1).broadcast_to([P, E1, DM]),
                                  tile(rw, k, off).unsqueeze(2).broadcast_to([P, E1, DM]), ALU.mult).then_inc(xs_s, 1)

            def keep_low_shares(i, buffer, c):
                after(dve, xsT_s, i * 4 + c + 1)
                dve.scalar_tensor_tensor(xsT[:, buffer, 1, 4 * c:4 * c + 4, :].rearrange("p e t -> p (e t)"), psS[:, c, :], SHARE,
                                         xsT[:, buffer, 0, 4 * c:4 * c + 4, :].rearrange("p e t -> p (e t)"),
                                         ALU.mult, ALU.subtract).then_inc(xsT_lo, 1)

            def weight_outputs(k, off, c):
                i = number(k, off)
                after(dve, z_p, i * 4 + c + 1)
                if c == 0:
                    after(dve, z_sum, i)
                dve.scalar_tensor_tensor(z[:, 4 * c:4 * c + 4, :], zb[c % 3][:, :].rearrange("p (e d) -> p e d", e=4), tg[:, 3:4],
                                         tile(rw, k, off)[:, 4 * c:4 * c + 4].unsqueeze(2).broadcast_to([P, 4, DM]),
                                         ALU.mult, ALU.mult).then_inc(z_s, 1)

            def step(k, off):
                n = number(k, off)

                def has(lag):
                    return k is not None or 0 <= off + lag < T

                m = n - E_LAG
                if has(1 - E_LAG):
                    weigh(k, off - E_LAG + 1)
                if has(4):
                    gt = tile(gate, k, off + 4)
                    dve.wait_ge(fetched_s[off % 2], (n + 4 - off % 2) * 16 + 32)
                    dve.scalar_tensor_tensor(moe[:, :], fetched[:, off % 2, 0, :], gt[:, 0:1], tile(hres, k, off + 4), ALU.mult, ALU.add)
                if has(1):
                    maxima(T + n + 1)
                dve.drain()
                if has(1):
                    shift_scores(T + n + 1, (off + 1) % 2)
                if has(3):
                    after(dve, x2_s, 2 * n + 8)
                if has(4):
                    dve.scalar_tensor_tensor(moe2[:, :], fetched[:, off % 2, 1, :], gt[:, 1:2], moe[:, :], ALU.mult, ALU.add).then_inc(merged, 1)
                dve.drain()
                if has(3):
                    dve.bn_stats(stats[:, 1, :], tile(xres, k, off + 3))
                if has(4):
                    dve.bn_stats(stats[:, 0, :], moe2[:, :])
                if has(-1 - E_LAG):
                    after(dve, sc_p, m)
                    after(dve, pr_e, m - 1)
                    dve.scalar_tensor_tensor(sc[:, :], psT[:, 2 * P:3 * P], float(DM) ** -0.5, causal[:, :], ALU.mult, ALU.add)
                    dve.drain()
                    dve.tensor_reduce(scmax[:, :], sc[:, :], AX.X, ALU.max, negate=True).then_inc(sc_m, 1)
                if has(0):
                    after(dve, av, T + n + 1)
                if has(-1):
                    after(dve, lg_p, T + n)
                    after(dve, norm_s, n)
                if has(0):
                    norm_heads()
                    x3 = tile(xres, k, off)
                if has(-1):
                    dve.scalar_tensor_tensor(lgr[:, :], lg_ps, norm[:, 0:1], sig[:, :], ALU.mult, ALU.subtract).then_inc(lg_s, 1)
                dve.drain()
                if has(-1 - E_LAG):
                    after(dve, pr_e, m)
                    dve.reciprocal(screc[:, :], scsum[:, :])
                if has(0):
                    dve.scalar_tensor_tensor(x3, osb[:, :, :].rearrange("p h d -> p (h d)"), tg[:, 1:2], x3, ALU.mult, ALU.add)
                if has(-1):
                    dve.max(mx8[:, :], lgr[:, :])
                    dve.tensor_scalar(relu[:, :], lgr[:, :], 0.0, None, ALU.max)
                    dve.tensor_scalar(active[:, :], lgr[:, :], 0.0, None, ALU.is_gt)
                dve.drain()
                if has(-1 - E_LAG):
                    after(dve, prT_p, m - 1)
                    dve.tensor_scalar(prn[:, :], pr[:, :], screc[:, 0:1], None, ALU.mult).then_inc(pr_s, 1)
                if has(0):
                    dve.bn_stats(stats[:, 2, :], x3)
                if has(-1):
                    dve.max_index(ix8[:, :], mx8[:, :], lgr[:, :])
                    dve.tensor_scalar(nomax[:, :], mx8[:, 0:1], 0.0, -1.0, ALU.max, ALU.mult).then_inc(g_in, 1)
                    dve.tensor_scalar(idle[:, :], mx8[:, 0:1], 0.0, None, ALU.is_le)
                dve.drain()
                if has(0):
                    dve.bn_aggr(mv[:, 2, :], stats[:, 2, :])
                if has(3):
                    dve.bn_aggr(mv[:, 1, :], stats[:, 1, :])
                if has(4):
                    dve.bn_aggr(mv[:, 0, :], stats[:, 0, :])
                if has(-1):
                    dve.tensor_copy(ixf[:, :], ix8[:, 0:2])
                dve.drain()
                if k is not None or off <= T + 1:
                    dve.tensor_scalar(veps[:, 0:3], mv[:, :, 1], EPS, None, ALU.add).then_inc(variances, 1)
                if has(-1):
                    dve.tensor_scalar(oneh[:, :], iota16[:, :], ixf[:, 0:1], None, ALU.is_equal)
                    dve.drain()
                    dve.scalar_tensor_tensor(oneh2[:, :], iota16[:, :], ixf[:, 1:2], oneh[:, :], ALU.is_equal, ALU.add)
                    dve.drain()
                    dve.scalar_tensor_tensor(oneh[:, :], oneh2[:, :], idle[:, 0:1], active[:, :], ALU.mult, ALU.add)
                    dve.drain()
                    after(dve, g_ex, n)
                    dve.tensor_tensor_reduce(gpr[:, :], gex[:, :], oneh[:, :], 1.0, 0.0, ALU.mult, ALU.add, gsum[:, :])
                if k is not None or off <= T + 1:
                    after(dve, roots, T + 5 + n + 5)
                if has(4):
                    after(dve, x2_s, 2 * n + 8)
                    dve.tensor_scalar(moen[:, :], moe2[:, :], mv[:, 0, 0:1], root[:, 0:1], ALU.subtract, ALU.mult).then_inc(moe_n, 1)
                if has(0):
                    after(dve, hT_p, T + n)
                    after(dve, h_kept, T + n)
                    dve.tensor_scalar(hn[:, :], x3, mv[:, 2, 0:1], root[:, 2:3], ALU.subtract, ALU.mult).then_inc(h_norm, 1)
                if has(3):
                    after(dve, xc_ps, T + n + 3)
                    dve.tensor_scalar(xn[:, :], tile(xres, k, off + 3), mv[:, 1, 0:1], root[:, 1:2],
                                      ALU.subtract, ALU.mult).then_inc(x_norm, 1)
                dve.drain()
                if has(-1):
                    dve.reciprocal(grec[:, :], gsum[:, :])
                if has(0):
                    dve.tensor_tensor_reduce(hsq[:, :], hn[:, :], hn[:, :], 1.0, 1e-12, ALU.mult, ALU.add, squares[:, 0:1]).then_inc(squares_s, 1)
                dve.drain()
                if has(-1):
                    dve.tensor_scalar(tile(rw, k, off - 1), gpr[:, :], grec[:, 0:1], None, ALU.mult)
                if has(1 - E_LAG):
                    for c in range(2):
                        keep_low_shares(m + 1, (off + 1 - E_LAG) % 2, c)
                if has(-E_LAG):
                    after(dve, qkv_p, m + 1)
                    after(dve, ao_p, m - 1)
                    after(dve, qkT_p, m)
                    dve.tensor_scalar(qkv[:, (off - E_LAG) % 2, :], psP[:, 0:3 * DM], downscale[:, 0:1], None,
                                      ALU.mult).then_inc(qkv_s, 1)
                if has(1 - E_LAG):
                    for c in range(2, 4):
                        keep_low_shares(m + 1, (off + 1 - E_LAG) % 2, c)
                if has(-1 - E_LAG):
                    for c in range(4):
                        weight_outputs(k, off - E_LAG - 1, c)
                if not has(-1 - E_LAG):
                    dve.drain()

            run_steps(dve, -4, T + 4, -4, 4, step)

        @block.scalar
        def _(act):
            act.wait_ge(loads, 16 * len(LOADS))
            act.activation(tg[:, :], g_sb[:, :], ACT.Tanh).then_inc(tanhs, 1)
            act.activation(sig[:, :], sig[:, :], ACT.Exp, scale=-1.0).then_inc(tanhs, 1)
            act.wait_ge(consts, 1)

            def evacuate_probs(i, b):
                after(act, pT_ps, 2 * i + b + 1)
                after(act, av, i)
                act.copy(pT[:, b].rearrange("p g k -> p (g k)"), psR[:, :]).then_inc(pT_sb, 1)

            def split_weights():
                act.wait_ge(scale_s, 1)
                for e in range(0, E1, 4):
                    w = act.activation(w16[:, 0, e:e + 4, :], wqkv[:, e:e + 4, :, :].rearrange("p e t d -> p e (t d)"),
                                       ACT.Copy, scale=upscale_f[:, 0:1])
                w.then_inc(w16_high, 1)

            def exponentials(i, buffer):
                after(act, shifted, i + 1)
                e = es[:, buffer].rearrange("p g b k -> p (g b k)")
                act.activation(e, e, ACT.Exp, scale=SCALE).then_inc(probs, 1)

            def step(k, off):
                n = number(k, off)

                def has(lag):
                    return k is not None or 0 <= off + lag < T

                if has(0):
                    evacuate_probs(n, 0)
                if has(2):
                    after(act, xc_ps, n + 3)
                if has(-1):
                    after(act, oT_p, n)
                if has(-2):
                    after(act, hT_p, n - 1)
                if has(2):
                    after(act, proj, n + 2)
                    act.copy(xT[:, :], psT[:, 0:P]).then_inc(xc_sb, 1)
                    act.copy(cT[:, :, :, :], psT[:, P:2 * P].rearrange("p (b k) -> p b k", b=2).unsqueeze(2)
                             .broadcast_to([P, 2, 2, SEQ])).then_inc(xc_sb, 1)
                if has(-1):
                    after(act, y_p, n - 1)
                    act.copy(oT[:, :], psT[:, 2 * P:3 * P]).then_inc(oT_s, 1)
                if has(-2):
                    after(act, lg_p, n - 2)
                    act.copy(hT[:, :], psT[:, 3 * P:4 * P]).then_inc(hT_s, 1)
                if has(0):
                    evacuate_probs(n, 1)
                if has(1):
                    exponentials(n + 1, (off + 1) % 2)

            run_steps(act, -2, T + 1, -2, 3, step, split_weights, SPLIT_AT)
            act.wait_ge(routes_d, 1)
            act.activation(gexp[:, 1, :], dist[:, :], ACT.Exp, scale=-1.0).then_inc(gexp_s, 1)
            with act.Fori(0, E0 // 2) as k:
                for t in range(BLOCKS):
                    j = t // XT
                    n = k * BLOCKS + t
                    if t % XT == 0:
                        act.wait_ge(w_in[j], k * 64 + 64 + C)
                    act.wait_ge(hid_ps, n + 1 + C)
                    after(act, yrow_ps, n - 1)
                    for f in range(FB):
                        m = act.activation(hidT[:, t % 2, f, :], psS[:, 2 * (t % 2) + f // 2, (f % 2) * 256:(f % 2) * 256 + 256],
                                           ACT.Gelu, bias=b1_sb[:, j, f:f + 1])
                    m.then_inc(hid_sb, 1)
            def evacuate_shares(i, buffer, c):
                after(act, xsT_p, i * 4 + c + 1)
                after(act, qkv_p, i - 1)
                act.activation(xsT[:, buffer, 0, 4 * c:4 * c + 4, :].rearrange("p e t -> p (e t)"), psS[:, c, :], ACT.Copy,
                               scale=SHARE).then_inc(xsT_s, 1)

            def step(k, off):
                n = number(k, off)
                m = n - E_LAG

                def has(lag):
                    return k is not None or 0 <= off + lag < T

                if has(0):
                    evacuate_probs(T + n, 0)
                if has(2):
                    after(act, xc_ps, T + n + 3)
                if has(-1):
                    after(act, hT_p, T + n)
                if has(2):
                    after(act, scores, T + n + 2)
                    act.copy(kT[:, :], psT[:, 0:P]).then_inc(kT_w, 1)
                    for h in range(4):
                        w = act.activation(qx[:, :, h, :], psT[:, P:2 * P].rearrange("p (b q) -> p b q", b=2), ACT.Copy,
                                           scale=headmask4[:, h:h + 1])
                    w.then_inc(qx_w, 2)
                if has(-1):
                    after(act, lg_p, T + n - 1)
                    act.copy(hT[:, :], psT[:, 3 * P:4 * P]).then_inc(hT_s, 1)
                if has(0):
                    evacuate_probs(T + n, 1)
                if has(1):
                    exponentials(T + n + 1, (off + 1) % 2)
                if has(-1 - E_LAG):
                    after(act, qkT_p, m)
                    act.copy(qkT[:, :], psT[:, 0:2 * P]).then_inc(qkT_s, 1)
                    after(act, sc_m, m)
                    after(act, pr_s, m - 1)
                    act.activation(pr[:, :], sc[:, :], ACT.Exp, bias=scmax[:, 0:1], accum_out=scsum[:, :]).then_inc(pr_e, 1)
                if has(-1):
                    after(act, g_in, n)
                    act.activation(gex[:, :], relu[:, :], ACT.Exp, bias=nomax[:, 0:1]).then_inc(g_ex, 1)
                if has(1 - E_LAG):
                    for c in range(2):
                        evacuate_shares(m + 1, (off + 1 - E_LAG) % 2, c)
                if has(-1 - E_LAG):
                    after(act, prT_p, m)
                    after(act, ao_p, m - 1)
                    act.copy(prT[:, :], psT[:, 3 * P:4 * P]).then_inc(prT_s, 1)
                if has(1 - E_LAG):
                    for c in range(2, 4):
                        evacuate_shares(m + 1, (off + 1 - E_LAG) % 2, c)
                if has(-1 - E_LAG):
                    after(act, ao_p, m)
                    after(act, z_p, 4 * m - 4)
                    act.copy(aoT[:, :], psT[:, 0:P]).then_inc(ao_s, 1)
                if has(2):
                    act.wait_ge(vdup_s[off % 2], (n + 2 - off % 2) * 16 + 32 + C)
                    after(act, av, T + n + 1)
                    for h in range(2):
                        rows = slice(h * SEQ, (h + 1) * SEQ)
                        v = vdup[rows, off % 2, :, :].rearrange("p b (g j h d) -> p (b g) j h d", g=G, j=2, h=2)[:, :, h, :, :]
                        dst = vx[rows, off % 2, :, :, :, h, 0:HD].rearrange("p b g h d -> p (b g) h d")
                        act.copy(dst, v).then_inc(vx_w, 1)

            run_steps(act, -4, T + 4, -4, 2, step)

        @block.tensor
        def _(pe):
            pe.wait_ge(consts, 1)

            def score_products(start):
                for b in range(2):
                    for hj in range(2):
                        for g in range(G):
                            rows = slice(32 * g, 32 * g + 32)
                            m = pe.matmul(psS[:, g, (2 * b + hj) * SEQ:(2 * b + hj + 1) * SEQ],
                                          qx[rows, b, 2 * hj:2 * hj + 2, :], kT[rows, b * SEQ:(b + 1) * SEQ],
                                          start=start, stop=True, skip_group_check=not start)
                m.then_inc(scores, 1)

            def turn_probs(i, buffer, b):
                after(pe, probs, i + 1)
                after(pe, pT_sb, 2 * i + b)
                for g in range(G):
                    m = pe.transpose(psR[:, g * P:(g + 1) * P], es[:, buffer, g, b, :], ident[:, :])
                m.then_inc(pT_ps, 1)

            def value_products(buffer):
                for b in range(2):
                    for g in range(G):
                        for h in range(2):
                            head = 4 * g + h
                            m = pe.matmul(o_ps[b * SEQ:(b + 1) * SEQ, head:head + 3:2, :],
                                          pT[:, b, g, h * SEQ:(h + 1) * SEQ], vx[:, buffer, b, g, h, :, :],
                                          start=True, stop=True)
                m.then_inc(av, 1)

            def split_weights():
                pe.wait_ge(widths, 1)
                pe.transpose(psR[:, 0:P], turned[:, :], ident[:, :]).then_inc(widths_p, 1)
                pe.wait_ge(widths, 2)

            def step(k, off):
                n = number(k, off)

                def has(lag):
                    return k is not None or 0 <= off + lag < T

                if has(1):
                    after(pe, qx_w, 2 * n + 4)
                    after(pe, kT_w, n + 2)
                    after(pe, shifted, n + 1)
                    score_products(True)
                if has(0):
                    turn_probs(n, off % 2, 0)
                after(pe, xc_sb, min(2 * T, 2 * n + 4) if k is None else 2 * n + 4)
                after(pe, oT_s, n - 1)
                after(pe, hT_s, n - 2)
                if has(2):
                    after(pe, x_norm, n + 3)
                    pe.transpose(psT[:, 0:P], xn[:, :], ident[:, :])
                    pe.wait_ge(ctx_s[off % 2], (n + 2 - off % 2) * 8 + 16 + C)
                    pe.transpose(psT[:, P:2 * P], ctok[:, off % 2, :], ident[:, :]).then_inc(xc_ps, 1)
                if has(-1):
                    after(pe, o_norm, n)
                    pe.transpose(psT[:, 2 * P:3 * P], osb[:, :, :].rearrange("p h d -> p (h d)"), ident[:, :]).then_inc(oT_p, 1)
                if has(-2):
                    after(pe, h_norm, n - 1)
                    pe.transpose(psT[:, 3 * P:4 * P], hn[:, :], ident[:, :]).then_inc(hT_p, 1)
                if has(0):
                    turn_probs(n, off % 2, 1)
                if has(2):
                    after(pe, xc_sb, 2 * n + 6)
                    after(pe, qx_w, 2 * n + 4)
                    after(pe, kT_w, n + 2)
                    after(pe, vx_w, 2 * n + 4)
                    pe.matmul(psP[:, 0:P], wq_sb[:, :], xT[:, :], start=True, stop=True)
                    pe.matmul(psP[:, P:2 * P], wk_sb[:, :], cT[:, :, 0, :], start=True, stop=True)
                    for b in range(2):
                        m = pe.matmul(psP[:, (2 + b) * P:(3 + b) * P], cT[:, b, :, :], wv_sb[:, :], start=True, stop=True)
                    m.then_inc(proj, 1)
                after(pe, o_norm, min(T, n) if k is None else n)
                after(pe, y_s, n - 1)
                after(pe, lg_s, n - 2)
                if has(-1):
                    after(pe, oT_s, n)
                    pe.matmul(y_ps, oT[:, :], wo_sb[:, :], start=True, stop=True).then_inc(y_p, 1)
                if has(-2):
                    after(pe, hT_s, n - 1)
                    pe.matmul(psO[:, 400:400 + E0], hT[:, :], wr_sb[:, :], start=True, stop=True).then_inc(lg_p, 1)
                if has(0):
                    after(pe, pT_sb, 2 * n + 2)
                    after(pe, vx_w, 2 * n + 2)
                    value_products(off % 2)

            run_steps(pe, -2, T + 1, -2, 3, step, split_weights, SPLIT_AT)
            pe.wait_ge(simprep, 1)
            pe.matmul(psT[:, 0:E1], ones[:, :], simsq[:, :], start=True, stop=True).then_inc(counted, 1)
            with pe.Fori(0, 32) as n:
                pe.wait_ge(searched, n + 1 + C)
                pe.matmul(psP[:, 0:E0], ones_bf[:, :], counts[:, :], start=True, stop=True).then_inc(counted, 1)
            pe.wait_ge(searched, 33 + C)
            pe.matmul(psP[:, 0:E0], ones_bf[:, :], counts[:, :], start=True, stop=True).then_inc(counted, 1)
            for r in range(2):
                pe.wait_ge(searched, 34 + r + C)
                f = flags[:, :, :].rearrange("p e t -> p (e t)")
                pe.matmul(psT[:, :], before[:, :], f, start=True, stop=True)
                pe.matmul(psR[:, :], ones_bf[:, :], f, start=True, stop=True).then_inc(counted, 1)
            yb = (psR, psO)
            tb = (psT, psP)

            def turn_rows(k, t):
                after(pe, rT_sb, k * BLOCKS + t - 1)
                pe.wait_ge(rows_in_s[t % 2], k * (16 * XT) + 16 * (t // 2) + 16 + C)
                for r in range(2):
                    w = pe.transpose(tb[t % 2][:, r * P:(r + 1) * P], rows_in[:, t % 2, r, :], ident[:, :])
                w.then_inc(rT_ps, 1)

            def hidden_products(k, t):
                n = k * BLOCKS + t
                if t % XT == 0:
                    pe.wait_ge(w_in[t // XT], k * 64 + 64 + C)
                after(pe, rT_sb, n + 1)
                after(pe, hid_sb, n - 1)
                for f in range(FB):
                    w = pe.matmul(psS[:, 2 * (t % 2) + f // 2, (f % 2) * 256:(f % 2) * 256 + 256],
                                  w1_sb[:, t // XT, f * P:(f + 1) * P], rowsT[:, t % 2, :], start=True, stop=True)
                w.then_inc(hid_ps, 1)

            def expert_out_rows(k, t):
                n = k * BLOCKS + t
                after(pe, hid_sb, n + 1)
                after(pe, yrow_sb, n - 1)
                for r in range(2):
                    for f in range(FB):
                        w = pe.matmul(yb[t % 2][:, r * P:(r + 1) * P], hidT[:, t % 2, f, r * P:(r + 1) * P],
                                      w2_sb[:, t // XT, f, :], start=(f == 0), stop=(f == FB - 1))
                w.then_inc(yrow_ps, 1)

            with pe.Fori(0, E0 // 2) as k:
                turn_rows(k, 0)
                for t in range(BLOCKS):
                    if t + 1 < BLOCKS:
                        turn_rows(k, t + 1)
                    hidden_products(k, t)
                    if t >= 1:
                        expert_out_rows(k, t - 1)
                expert_out_rows(k, BLOCKS - 1)
            def turn_shares(i, c):
                for e in range(4 * c, 4 * c + 4):
                    w = pe.transpose(psS[:, c, (e % 4) * P:(e % 4 + 1) * P], xs[:, e, :], ident[:, :])
                w.then_inc(xsT_p, 1)

            def project(i, buffer, c):
                if c == 0:
                    after(pe, qkv_s, i)
                after(pe, xsT_lo, i * 4 + c + 1)
                for e in range(4 * c, 4 * c + 4):
                    for part, (x_part, w_part) in enumerate(((0, 0), (0, 1), (1, 0))):
                        w = pe.matmul(psP[:, 0:3 * DM], xsT[:, buffer, x_part, e, :], w16[:, w_part, e, :],
                                      start=(e == 0 and part == 0), stop=(e == E1 - 1 and part == 2))
                if c == 3:
                    w.then_inc(qkv_p, 1)

            def step(k, off):
                n = number(k, off)
                m = n - E_LAG
                b = (off - E_LAG) % 2
                o = 1 - b

                def has(lag):
                    return k is not None or 0 <= off + lag < T

                after(pe, xsT_lo, upto(4 * m + 4, 4 * T))
                if has(1):
                    after(pe, qx_w, 2 * T + 2 * n + 4)
                    after(pe, kT_w, T + n + 2)
                    after(pe, shifted, T + n + 1)
                    for g in range(G):
                        pe.matmul(psS[:, g, 0:2 * P], ident_bf[:, :], band4[:, :, :], start=True, stop=True, skip_group_check=True)
                    score_products(False)
                after(pe, z_s, upto(4 * m - 4, 4 * T))
                after(pe, ao_s, upto(m - 1, T))
                if has(0):
                    turn_probs(T + n, off % 2, 0)
                after(pe, kT_w, upto(T + n + 2, 2 * T))
                after(pe, qx_w, upto(2 * T + 2 * n + 4, 4 * T))
                after(pe, hT_s, upto(T + n - 1, 2 * T))
                if has(2):
                    pe.wait_ge(ctx_s[off % 2], 8 * T + (n + 2 - off % 2) * 8 + 16 + C)
                    pe.transpose(psT[:, 0:P], ctok[:, off % 2, :], ident[:, :])
                    after(pe, x_norm, T + n + 3)
                    pe.transpose(psT[:, P:2 * P], xn[:, :], ident[:, :]).then_inc(xc_ps, 1)
                if has(-1):
                    after(pe, h_norm, T + n)
                    pe.transpose(psT[:, 3 * P:4 * P], hn[:, :], ident[:, :]).then_inc(hT_p, 1)
                if has(-E_LAG):
                    project(m, b, 0)
                if has(0):
                    turn_probs(T + n, off % 2, 1)
                after(pe, kT_w, upto(T + n + 3, 2 * T))
                after(pe, qx_w, upto(2 * T + 2 * n + 6, 4 * T))
                after(pe, hT_s, upto(T + n, 2 * T))
                if has(-1 - E_LAG):
                    after(pe, qkv_s, m)
                    after(pe, prT_s, m - 1)
                    pe.transpose(psT[:, 0:P], qkv[:, o, 0:P], ident[:, :])
                    pe.transpose(psT[:, P:2 * P], qkv[:, o, P:2 * P], ident[:, :]).then_inc(qkT_p, 1)
                if has(-E_LAG):
                    project(m, b, 1)
                if has(-1 - E_LAG):
                    after(pe, qkT_s, m)
                    pe.matmul(psT[:, 2 * P:3 * P], qkT[:, 0:P], qkT[:, P:2 * P], start=True, stop=True).then_inc(sc_p, 1)
                after(pe, o_norm, upto(T + n, 2 * T))
                after(pe, lg_s, upto(T + n - 1, 2 * T))
                if has(-1):
                    pe.matmul(lg_ps, hT[:, :], simn[:, :], start=True, stop=True).then_inc(lg_p, 1)
                if has(0):
                    after(pe, pT_sb, 2 * T + 2 * n + 2)
                    after(pe, vx_w, 2 * T + 2 * n + 2)
                    value_products(off % 2)
                if has(-E_LAG):
                    project(m, b, 2)
                if has(1 - E_LAG):
                    after(pe, shifted, upto(T + n + 2, 2 * T))
                    after(pe, xs_s, m + 2)
                    turn_shares(m + 1, 0)
                    turn_shares(m + 1, 1)
                if has(-1 - E_LAG):
                    after(pe, pr_s, m)
                    pe.transpose(psT[:, 3 * P:4 * P], prn[:, :], ident[:, :]).then_inc(prT_p, 1)
                if has(1 - E_LAG):
                    turn_shares(m + 1, 2)
                    turn_shares(m + 1, 3)
                if has(-E_LAG):
                    project(m, b, 3)
                if has(-1 - E_LAG):
                    after(pe, prT_s, m)
                    pe.matmul(psT[:, 0:P], qkv[:, o, 2 * P:3 * P], prT[:, :], start=True, stop=True).then_inc(ao_p, 1)
                if has(-1 - E_LAG):
                    after(pe, pT_sb, upto(2 * T + 2 * n + 2, 4 * T))
                    after(pe, o_norm, upto(T + n + 1, 2 * T))
                    after(pe, lg_s, upto(T + n, 2 * T))
                    after(pe, ao_s, m)
                    for c in range(4):
                        if c == 2:
                            after(pe, qkv_s, upto(m + 1, T))
                        if c == 3:
                            after(pe, z_s, 4 * m - 3)
                        pe.matmul(zb[c % 3][:, :], aoT[:, :], wo1[:, 4 * c:4 * c + 4, :], start=True, stop=True).then_inc(z_p, 1)

            pe.wait_ge(ewts, 16)
            pe.wait_ge(w16_s, 1)
            run_steps(pe, -4, T + 4, -4, 2, step)


_INS = ['x', 'ctx_1024', 'g_xattn', 'g_ffn', 'L0_xattn_Wq', 'L0_xattn_bq', 'L0_xattn_Wk', 'L0_xattn_bk', 'L0_xattn_Wv',
        'L0_xattn_bv', 'L0_xattn_Wo', 'L0_xattn_bo', 'L0_ffn_Wr', 'L0_ffn_br', 'L0_ffn_W1', 'L0_ffn_b1', 'L0_ffn_W2',
        'L0_ffn_b2', 'L0_ffn_gamma', 'L0_ffn_beta', 'L0_ffn_token_mask', 'L1_ffn_sim_matrix', 'L1_ffn_gates',
        'L1_ffn_q_proj', 'L1_ffn_k_proj', 'L1_ffn_v_proj', 'L1_ffn_o_proj']
_OUTS = [((128, 64, 128), 'float32')]


def kernel(**inputs):
    import numpy as _np
    import concourse.bacc as _bacc
    from concourse import mybir as _mybir
    from concourse.bass_utils import run_bass_kernel_spmd as _run

    nc = _bacc.Bacc("TRN2", target_bir_lowering=False, num_devices=1)
    arrays, args = {}, []
    for name in _INS:
        a = _np.ascontiguousarray(inputs[name])
        arrays[f"in_{name}_dram"] = a
        args.append(nc.dram_tensor(f"in_{name}_dram", a.shape, _mybir.dt.from_np(a.dtype), kind="ExternalInput").ap())
    for i, (shape, dtype) in enumerate(_OUTS):
        dt = _mybir.dt.from_np(_np.dtype(dtype))
        args.append(nc.dram_tensor(f"out_{i}_dram", shape, dt, kind="ExternalOutput").ap())
    build(nc, *args)
    r = _run(nc, [arrays], core_ids=[0])
    got = tuple(r.results[0][f"out_{i}_dram"] for i in range(len(_OUTS)))
    return got[0]
```
